# Optimizing a Trainium2 kernel written in Bass

```python
import numpy as np
import jax
import jax.numpy as jnp

def _softmax(x, axis=-1):
    return jax.nn.softmax(x, axis=axis)

def _gelu(x):
    return jax.nn.gelu(x, approximate=True)

def _silu(x):
    return jax.nn.silu(x)

def _sigmoid(x):
    return jax.nn.sigmoid(x)

def _layernorm(x, axis=-1, eps=1e-05):
    m = jnp.mean(x, axis=axis, keepdims=True)
    v = jnp.var(x, axis=axis, keepdims=True)
    return (x - m) / jnp.sqrt(v + eps)

def _scatter_add(tgt, idx, src, axis=0):
    return tgt.at[idx].add(src)

def _segment_sum(src, seg, n):
    return jax.ops.segment_sum(src, seg, n)
kernel_name = 'mk_xattn_seq_d4_seqx_r4_256301'

def setup_inputs(seed: int=0):
    np.random.seed(seed)
    _w = jnp.asarray

    def _rec_inputs():
        import jax
        import jax.numpy as jnp
        _rk = jax.random.key(seed)
        x = -0.0003929 + 0.9999 * jax.random.normal(jax.random.fold_in(_rk, 1), (16, 256, 512), jnp.float32)
        _lenS = 256 - jax.random.randint(jax.random.fold_in(_rk, 7), (16,), 0, max(1, 256 // 4) + 1, jnp.int32)
        _lenS2 = 256 - jax.random.randint(jax.random.fold_in(_rk, 8), (16,), 0, max(1, 256 // 4) + 1, jnp.int32)
        _ctx_2048P = jax.random.normal(jax.random.fold_in(_rk, 11), (16, 16, 512), jnp.float32)
        _ctx_2048c = jax.random.dirichlet(jax.random.fold_in(_rk, 511), 0.3 * jnp.ones((16,), jnp.float32), (16, 256))
        _ctx_2048t = jnp.einsum('bsk,bkd->bsd', _ctx_2048c, _ctx_2048P)
        _ctx_2048t = _ctx_2048t * jax.lax.rsqrt(jnp.mean(jnp.square(_ctx_2048t)) + 1e-12) * 0.953939
        ctx_2048 = -8.57375e-05 + 0.999917 * (_ctx_2048t + 0.3 * jax.random.normal(jax.random.fold_in(_rk, 611), (16, 256, 512), jnp.float32))
        _validS = jnp.arange(256)[None, :] < _lenS[:, None]
        _validS2 = jnp.arange(256)[None, :] < _lenS2[:, None]
        _causal = jnp.tril(jnp.ones((256, 256), dtype=bool))
        mask_BxS2_bf1 = jnp.ones((16, 256), dtype=bool)
        return (x, ctx_2048, mask_BxS2_bf1)
    x, ctx_2048, mask_BxS2_bf1 = _rec_inputs()

    def _L0_xattn_setup():
        import jax, jax.numpy as jnp
        import numpy as np
        HIDDEN = 512
        HEADS = 16
        HEAD_DIM = HIDDEN // HEADS
        LN_EPS = 1e-05
        GATE_INIT = 0.5

        def _layer_norm(x, gamma, beta):
            mu = jnp.mean(x, axis=-1, keepdims=True)
            var = jnp.mean(jnp.square(x - mu), axis=-1, keepdims=True)
            return (x - mu) * jax.lax.rsqrt(var + LN_EPS) * gamma + beta
        key = jax.random.key(seed)
        ks = jax.random.split(key, 8)
        B, T_TEXT, T_AUDIO = (4, 512, 375)
        s = 0.02
        return {'hidden_states': jax.random.normal(ks[0], (B, T_TEXT, HIDDEN), jnp.float32), 'audio_kv': jax.random.normal(ks[1], (B, T_AUDIO, HIDDEN), jnp.float32), 'audio_attention_mask': jnp.ones((B, T_AUDIO), dtype=bool), 'Wq': jax.random.normal(ks[2], (HIDDEN, HIDDEN), jnp.float32) * s, 'Wk': jax.random.normal(ks[3], (HIDDEN, HIDDEN), jnp.float32) * s, 'Wv': jax.random.normal(ks[4], (HIDDEN, HIDDEN), jnp.float32) * s, 'Wo': jax.random.normal(ks[5], (HIDDEN, HIDDEN), jnp.float32) * s, 'ln_gamma': jnp.ones((HIDDEN,), jnp.float32), 'ln_beta': jnp.zeros((HIDDEN,), jnp.float32), 'gate': jnp.array([GATE_INIT], jnp.float32)}
    _L0_xattn_all = _L0_xattn_setup()
    _L0_xattn_in = {k: v for k, v in _L0_xattn_all.items() if k in ('Wq', 'Wk', 'Wv', 'Wo', 'ln_gamma', 'ln_beta', 'gate')}
    del _L0_xattn_all

    def _L1_xattn_setup():
        import jax, jax.numpy as jnp
        import numpy as np
        H = 512
        B, L, S = (4, 1024, 10)
        key = jax.random.key(seed)
        k1, k2, k3, k4, k5, k6 = jax.random.split(key, 6)
        scale = 1.0 / np.sqrt(H)
        return {'h_english': jax.random.normal(k1, (B, L, H), dtype=jnp.float32), 'h_lojban': jax.random.normal(k2, (B, S, H), dtype=jnp.float32), 'w_q': jax.random.normal(k3, (H, H), dtype=jnp.float32) * scale, 'w_k': jax.random.normal(k4, (H, H), dtype=jnp.float32) * scale, 'w_v': jax.random.normal(k5, (H, H), dtype=jnp.float32) * scale, 'w_o': jax.random.normal(k6, (H, H), dtype=jnp.float32) * scale, 'alpha': jnp.float32(0.1)}
    _L1_xattn_all = _L1_xattn_setup()
    _L1_xattn_in = {k: v for k, v in _L1_xattn_all.items() if k in ('w_q', 'w_k', 'w_v', 'w_o', 'alpha')}
    del _L1_xattn_all

    def _L2_xattn_setup():
        import jax, jax.numpy as jnp
        import numpy as np
        E, H, L, B = (512, 32, 256, 4)
        S = E // H
        DM, DD = (32, 64)

        def _ln(x, w, b, eps=1e-05):
            m = x.mean(-1, keepdims=True)
            v = ((x - m) ** 2).mean(-1, keepdims=True)
            return (x - m) / jnp.sqrt(v + eps) * w + b

        def _block(x, state, ln1_w, ln1_b, ln2_w, ln2_b, maa_x, maa_w1, maa_w2, maa_stack, time_decay, td_w1, td_w2, u, Wr, Wk, Wv, Wg, Wo, gn_w, gn_b, ffn_maa_k, ffn_maa_r, Wfk, Wfr, Wfv):
            b, l, e = x.shape
            h = u.shape[0]
            s_ = e // h
            xa = _ln(x, ln1_w, ln1_b)
            sx = jnp.concatenate([state[:, 1:2] - xa[:, :1], xa[:, :-1] - xa[:, 1:]], axis=1)
            xxx = jnp.tanh((xa + sx * maa_x) @ maa_w1).reshape(b, l, 5, DM)
            xxx = jnp.einsum('blfd,fde->blfe', xxx, maa_w2)
            xm = xa[:, :, None] + sx[:, :, None] * (maa_stack + xxx)
            xk, xw, xv, xr, xg = (xm[:, :, j] for j in range(5))
            w = jnp.exp(-jnp.exp(time_decay + jnp.tanh(xw @ td_w1) @ td_w2)).reshape(b, l, h, s_)
            r = (xr @ Wr.T).reshape(b, l, h, s_)
            k = (xk @ Wk.T).reshape(b, l, h, s_)
            v = (xv @ Wv.T).reshape(b, l, h, s_)
            g = jax.nn.silu(xg @ Wg.T)
            s0 = state[:, 2:2 + s_].reshape(b, h, s_, s_)

            def step(s, rkvw):
                r_t, k_t, v_t, w_t = rkvw
                a = k_t[..., :, None] * v_t[..., None, :]
                out = jnp.einsum('bhi,bhij->bhj', r_t, u * a + s)
                s = a + w_t[..., :, None] * s
                return (s, out)
            rkvw = tuple((jnp.moveaxis(t, 1, 0) for t in (r, k, v, w)))
            _, out = jax.lax.scan(step, s0, rkvw)
            out = jnp.moveaxis(out, 0, 1).reshape(b, l, e)
            og = out.reshape(b, l, h, s_)
            m = og.mean(-1, keepdims=True)
            va = ((og - m) ** 2).mean(-1, keepdims=True)
            og = ((og - m) / jnp.sqrt(va + 1e-05)).reshape(b, l, e) * gn_w + gn_b
            x1 = x + og * g @ Wo.T
            xc = _ln(x1, ln2_w, ln2_b)
            sx2 = jnp.concatenate([state[:, 0:1] - xc[:, :1], xc[:, :-1] - xc[:, 1:]], axis=1)
            xk2 = xc + sx2 * ffn_maa_k
            xr2 = xc + sx2 * ffn_maa_r
            rr = jax.nn.sigmoid(xr2 @ Wfr.T)
            kk = jnp.square(jax.nn.relu(xk2 @ Wfk.T))
            return x1 + rr * (kk @ Wfv.T)
        key = jax.random.key(seed)
        ks = jax.random.split(key, 24)
        sc = 0.02
        d = {'x': jax.random.normal(ks[0], (B, L, E), jnp.float32), 'state': jax.random.normal(ks[1], (B, 2 + S, E), jnp.float32) * 0.1, 'ln1_w': jnp.ones((E,), jnp.float32), 'ln1_b': jnp.zeros((E,), jnp.float32), 'ln2_w': jnp.ones((E,), jnp.float32), 'ln2_b': jnp.zeros((E,), jnp.float32), 'maa_x': jax.random.normal(ks[2], (E,), jnp.float32) * 0.1, 'maa_w1': jax.random.normal(ks[3], (E, 5 * DM), jnp.float32) * sc, 'maa_w2': jax.random.normal(ks[4], (5, DM, E), jnp.float32) * sc, 'maa_stack': jax.random.normal(ks[5], (1, 5, E), jnp.float32) * 0.1, 'time_decay': jax.random.normal(ks[6], (E,), jnp.float32) * 0.5, 'td_w1': jax.random.normal(ks[7], (E, DD), jnp.float32) * sc, 'td_w2': jax.random.normal(ks[8], (DD, E), jnp.float32) * sc, 'u': jax.random.normal(ks[9], (H, S, 1), jnp.float32) * 0.1, 'Wr': jax.random.normal(ks[10], (E, E), jnp.float32) * sc, 'Wk': jax.random.normal(ks[11], (E, E), jnp.float32) * sc, 'Wv': jax.random.normal(ks[12], (E, E), jnp.float32) * sc, 'Wg': jax.random.normal(ks[13], (E, E), jnp.float32) * sc, 'Wo': jax.random.normal(ks[14], (E, E), jnp.float32) * sc, 'gn_w': jnp.ones((E,), jnp.float32), 'gn_b': jnp.zeros((E,), jnp.float32), 'ffn_maa_k': jax.random.normal(ks[15], (E,), jnp.float32) * 0.1, 'ffn_maa_r': jax.random.normal(ks[16], (E,), jnp.float32) * 0.1, 'Wfk': jax.random.normal(ks[17], (E, E), jnp.float32) * sc, 'Wfr': jax.random.normal(ks[18], (E, E), jnp.float32) * sc, 'Wfv': jax.random.normal(ks[19], (E, E), jnp.float32) * sc}
        return d
    _L2_xattn_all = _L2_xattn_setup()
    _L2_xattn_in = {k: v for k, v in _L2_xattn_all.items() if k in ('ln1_w', 'ln1_b', 'ln2_w', 'ln2_b', 'maa_x', 'maa_w1', 'maa_w2', 'maa_stack', 'time_decay', 'td_w1', 'td_w2', 'u', 'Wr', 'Wk', 'Wv', 'Wg', 'Wo', 'gn_w', 'gn_b', 'ffn_maa_k', 'ffn_maa_r', 'Wfk', 'Wfr', 'Wfv')}
    del _L2_xattn_all

    def _L3_xattn_setup():
        import jax, jax.numpy as jnp
        import numpy as np
        D = 512
        H = 16
        HD = D // H
        INNER = 4 * D
        EPS = 1e-05

        def layer_norm(x, w, b):
            mu = jnp.mean(x, axis=-1, keepdims=True)
            var = jnp.mean(jnp.square(x - mu), axis=-1, keepdims=True)
            return (x - mu) * jax.lax.rsqrt(var + EPS) * w + b
        key = jax.random.key(seed)
        ks = jax.random.split(key, 12)
        B, LQ, LK = (4, 256, 512)
        std = 0.02
        inp = {'hidden_states': jax.random.normal(ks[0], (B, LQ, D), jnp.float32), 'encoder_hidden_states': jax.random.normal(ks[1], (B, LK, D), jnp.float32), 'encoder_attention_mask': jnp.ones((B, LK), dtype=bool), 'ln1_w': jnp.ones((D,), jnp.float32), 'ln1_b': jnp.zeros((D,), jnp.float32), 'q_w': jax.random.normal(ks[2], (D, D), jnp.float32) * std, 'q_b': jnp.zeros((D,), jnp.float32), 'k_w': jax.random.normal(ks[3], (D, D), jnp.float32) * std, 'k_b': jnp.zeros((D,), jnp.float32), 'v_w': jax.random.normal(ks[4], (D, D), jnp.float32) * std, 'v_b': jnp.zeros((D,), jnp.float32), 'cproj_w': jax.random.normal(ks[5], (D, D), jnp.float32) * std, 'cproj_b': jnp.zeros((D,), jnp.float32), 'ln2_w': jnp.ones((D,), jnp.float32), 'ln2_b': jnp.zeros((D,), jnp.float32), 'fc_w': jax.random.normal(ks[6], (D, INNER), jnp.float32) * std, 'fc_b': jnp.zeros((INNER,), jnp.float32), 'proj_w': jax.random.normal(ks[7], (INNER, D), jnp.float32) * std, 'proj_b': jnp.zeros((D,), jnp.float32)}
        return inp
    _L3_xattn_all = _L3_xattn_setup()
    _L3_xattn_in = {k: v for k, v in _L3_xattn_all.items() if k in ('ln1_w', 'ln1_b', 'q_w', 'q_b', 'k_w', 'k_b', 'v_w', 'v_b', 'cproj_w', 'cproj_b', 'ln2_w', 'ln2_b', 'fc_w', 'fc_b', 'proj_w', 'proj_b')}
    del _L3_xattn_all
    return {'x': x, 'ctx_2048': ctx_2048, 'mask_BxS2_bf1': mask_BxS2_bf1, 'L0_xattn_Wq': _L0_xattn_in['Wq'], 'L0_xattn_Wk': _L0_xattn_in['Wk'], 'L0_xattn_Wv': _L0_xattn_in['Wv'], 'L0_xattn_Wo': _L0_xattn_in['Wo'], 'L0_xattn_ln_gamma': _L0_xattn_in['ln_gamma'], 'L0_xattn_ln_beta': _L0_xattn_in['ln_beta'], 'L0_xattn_gate': _L0_xattn_in['gate'], 'L1_xattn_w_q': _L1_xattn_in['w_q'], 'L1_xattn_w_k': _L1_xattn_in['w_k'], 'L1_xattn_w_v': _L1_xattn_in['w_v'], 'L1_xattn_w_o': _L1_xattn_in['w_o'], 'L1_xattn_alpha': _L1_xattn_in['alpha'], 'L2_xattn_ln1_w': _L2_xattn_in['ln1_w'], 'L2_xattn_ln1_b': _L2_xattn_in['ln1_b'], 'L2_xattn_ln2_w': _L2_xattn_in['ln2_w'], 'L2_xattn_ln2_b': _L2_xattn_in['ln2_b'], 'L2_xattn_maa_x': _L2_xattn_in['maa_x'], 'L2_xattn_maa_w1': _L2_xattn_in['maa_w1'], 'L2_xattn_maa_w2': _L2_xattn_in['maa_w2'], 'L2_xattn_maa_stack': _L2_xattn_in['maa_stack'], 'L2_xattn_time_decay': _L2_xattn_in['time_decay'], 'L2_xattn_td_w1': _L2_xattn_in['td_w1'], 'L2_xattn_td_w2': _L2_xattn_in['td_w2'], 'L2_xattn_u': _L2_xattn_in['u'], 'L2_xattn_Wr': _L2_xattn_in['Wr'], 'L2_xattn_Wk': _L2_xattn_in['Wk'], 'L2_xattn_Wv': _L2_xattn_in['Wv'], 'L2_xattn_Wg': _L2_xattn_in['Wg'], 'L2_xattn_Wo': _L2_xattn_in['Wo'], 'L2_xattn_gn_w': _L2_xattn_in['gn_w'], 'L2_xattn_gn_b': _L2_xattn_in['gn_b'], 'L2_xattn_ffn_maa_k': _L2_xattn_in['ffn_maa_k'], 'L2_xattn_ffn_maa_r': _L2_xattn_in['ffn_maa_r'], 'L2_xattn_Wfk': _L2_xattn_in['Wfk'], 'L2_xattn_Wfr': _L2_xattn_in['Wfr'], 'L2_xattn_Wfv': _L2_xattn_in['Wfv'], 'L3_xattn_ln1_w': _L3_xattn_in['ln1_w'], 'L3_xattn_ln1_b': _L3_xattn_in['ln1_b'], 'L3_xattn_q_w': _L3_xattn_in['q_w'], 'L3_xattn_q_b': _L3_xattn_in['q_b'], 'L3_xattn_k_w': _L3_xattn_in['k_w'], 'L3_xattn_k_b': _L3_xattn_in['k_b'], 'L3_xattn_v_w': _L3_xattn_in['v_w'], 'L3_xattn_v_b': _L3_xattn_in['v_b'], 'L3_xattn_cproj_w': _L3_xattn_in['cproj_w'], 'L3_xattn_cproj_b': _L3_xattn_in['cproj_b'], 'L3_xattn_ln2_w': _L3_xattn_in['ln2_w'], 'L3_xattn_ln2_b': _L3_xattn_in['ln2_b'], 'L3_xattn_fc_w': _L3_xattn_in['fc_w'], 'L3_xattn_fc_b': _L3_xattn_in['fc_b'], 'L3_xattn_proj_w': _L3_xattn_in['proj_w'], 'L3_xattn_proj_b': _L3_xattn_in['proj_b']}

def reference(x, ctx_2048, mask_BxS2_bf1, L0_xattn_Wq, L0_xattn_Wk, L0_xattn_Wv, L0_xattn_Wo, L0_xattn_ln_gamma, L0_xattn_ln_beta, L0_xattn_gate, L1_xattn_w_q, L1_xattn_w_k, L1_xattn_w_v, L1_xattn_w_o, L1_xattn_alpha, L2_xattn_ln1_w, L2_xattn_ln1_b, L2_xattn_ln2_w, L2_xattn_ln2_b, L2_xattn_maa_x, L2_xattn_maa_w1, L2_xattn_maa_w2, L2_xattn_maa_stack, L2_xattn_time_decay, L2_xattn_td_w1, L2_xattn_td_w2, L2_xattn_u, L2_xattn_Wr, L2_xattn_Wk, L2_xattn_Wv, L2_xattn_Wg, L2_xattn_Wo, L2_xattn_gn_w, L2_xattn_gn_b, L2_xattn_ffn_maa_k, L2_xattn_ffn_maa_r, L2_xattn_Wfk, L2_xattn_Wfr, L2_xattn_Wfv, L3_xattn_ln1_w, L3_xattn_ln1_b, L3_xattn_q_w, L3_xattn_q_b, L3_xattn_k_w, L3_xattn_k_b, L3_xattn_v_w, L3_xattn_v_b, L3_xattn_cproj_w, L3_xattn_cproj_b, L3_xattn_ln2_w, L3_xattn_ln2_b, L3_xattn_fc_w, L3_xattn_fc_b, L3_xattn_proj_w, L3_xattn_proj_b):
    import jax
    import jax.numpy as jnp

    def _L0_xattn_ref(hidden_states, audio_kv, audio_attention_mask, Wq, Wk, Wv, Wo, ln_gamma, ln_beta, gate):
        import jax, jax.numpy as jnp
        import numpy as np
        HIDDEN = 512
        HEADS = 16
        HEAD_DIM = HIDDEN // HEADS
        LN_EPS = 1e-05
        GATE_INIT = 0.5

        def _layer_norm(x, gamma, beta):
            mu = jnp.mean(x, axis=-1, keepdims=True)
            var = jnp.mean(jnp.square(x - mu), axis=-1, keepdims=True)
            return (x - mu) * jax.lax.rsqrt(var + LN_EPS) * gamma + beta
        B, Tt, D = hidden_states.shape
        Ta = audio_kv.shape[1]
        scale = HEAD_DIM ** (-0.5)
        a = _layer_norm(audio_kv, ln_gamma, ln_beta)
        Q = (hidden_states @ Wq.T).reshape(B, Tt, HEADS, HEAD_DIM).transpose(0, 2, 1, 3)
        K = (a @ Wk.T).reshape(B, Ta, HEADS, HEAD_DIM).transpose(0, 2, 1, 3)
        V = (a @ Wv.T).reshape(B, Ta, HEADS, HEAD_DIM).transpose(0, 2, 1, 3)
        scores = jnp.einsum('bhtd,bhsd->bhts', Q, K) * scale
        mask = audio_attention_mask[:, None, None, :]
        scores = jnp.where(mask, scores, jnp.float32(-jnp.inf))
        attn = jax.nn.softmax(scores, axis=-1)
        out = jnp.einsum('bhts,bhsd->bhtd', attn, V)
        out = out.transpose(0, 2, 1, 3).reshape(B, Tt, D)
        out = out @ Wo.T
        return hidden_states + jnp.tanh(gate) * out

    def _L1_xattn_ref(h_english, h_lojban, w_q, w_k, w_v, w_o, alpha):
        import jax, jax.numpy as jnp
        import numpy as np
        H = 512
        B, L, S = (4, 1024, 10)
        h = h_english.shape[-1]
        q = jnp.einsum('blh,oh->blo', h_english, w_q)
        k = jnp.einsum('bsh,oh->bso', h_lojban, w_k)
        v = jnp.einsum('bsh,oh->bso', h_lojban, w_v)
        scores = jnp.einsum('blh,bsh->bls', q, k) / jnp.sqrt(jnp.float32(h))
        probs = jax.nn.softmax(scores, axis=-1)
        context = jnp.einsum('bls,bsh->blh', probs, v)
        delta = jnp.einsum('blh,oh->blo', context, w_o)
        return h_english + alpha * delta

    def _L2_xattn_ref(x, state, ln1_w, ln1_b, ln2_w, ln2_b, maa_x, maa_w1, maa_w2, maa_stack, time_decay, td_w1, td_w2, u, Wr, Wk, Wv, Wg, Wo, gn_w, gn_b, ffn_maa_k, ffn_maa_r, Wfk, Wfr, Wfv):
        import jax, jax.numpy as jnp
        import numpy as np
        E, H, L, B = (512, 32, 256, 4)
        S = E // H
        DM, DD = (32, 64)

        def _ln(x, w, b, eps=1e-05):
            m = x.mean(-1, keepdims=True)
            v = ((x - m) ** 2).mean(-1, keepdims=True)
            return (x - m) / jnp.sqrt(v + eps) * w + b

        def _block(x, state, ln1_w, ln1_b, ln2_w, ln2_b, maa_x, maa_w1, maa_w2, maa_stack, time_decay, td_w1, td_w2, u, Wr, Wk, Wv, Wg, Wo, gn_w, gn_b, ffn_maa_k, ffn_maa_r, Wfk, Wfr, Wfv):
            b, l, e = x.shape
            h = u.shape[0]
            s_ = e // h
            xa = _ln(x, ln1_w, ln1_b)
            sx = jnp.concatenate([state[:, 1:2] - xa[:, :1], xa[:, :-1] - xa[:, 1:]], axis=1)
            xxx = jnp.tanh((xa + sx * maa_x) @ maa_w1).reshape(b, l, 5, DM)
            xxx = jnp.einsum('blfd,fde->blfe', xxx, maa_w2)
            xm = xa[:, :, None] + sx[:, :, None] * (maa_stack + xxx)
            xk, xw, xv, xr, xg = (xm[:, :, j] for j in range(5))
            w = jnp.exp(-jnp.exp(time_decay + jnp.tanh(xw @ td_w1) @ td_w2)).reshape(b, l, h, s_)
            r = (xr @ Wr.T).reshape(b, l, h, s_)
            k = (xk @ Wk.T).reshape(b, l, h, s_)
            v = (xv @ Wv.T).reshape(b, l, h, s_)
            g = jax.nn.silu(xg @ Wg.T)
            s0 = state[:, 2:2 + s_].reshape(b, h, s_, s_)

            def step(s, rkvw):
                r_t, k_t, v_t, w_t = rkvw
                a = k_t[..., :, None] * v_t[..., None, :]
                out = jnp.einsum('bhi,bhij->bhj', r_t, u * a + s)
                s = a + w_t[..., :, None] * s
                return (s, out)
            rkvw = tuple((jnp.moveaxis(t, 1, 0) for t in (r, k, v, w)))
            _, out = jax.lax.scan(step, s0, rkvw)
            out = jnp.moveaxis(out, 0, 1).reshape(b, l, e)
            og = out.reshape(b, l, h, s_)
            m = og.mean(-1, keepdims=True)
            va = ((og - m) ** 2).mean(-1, keepdims=True)
            og = ((og - m) / jnp.sqrt(va + 1e-05)).reshape(b, l, e) * gn_w + gn_b
            x1 = x + og * g @ Wo.T
            xc = _ln(x1, ln2_w, ln2_b)
            sx2 = jnp.concatenate([state[:, 0:1] - xc[:, :1], xc[:, :-1] - xc[:, 1:]], axis=1)
            xk2 = xc + sx2 * ffn_maa_k
            xr2 = xc + sx2 * ffn_maa_r
            rr = jax.nn.sigmoid(xr2 @ Wfr.T)
            kk = jnp.square(jax.nn.relu(xk2 @ Wfk.T))
            return x1 + rr * (kk @ Wfv.T)
        return _block(x, state, ln1_w, ln1_b, ln2_w, ln2_b, maa_x, maa_w1, maa_w2, maa_stack, time_decay, td_w1, td_w2, u, Wr, Wk, Wv, Wg, Wo, gn_w, gn_b, ffn_maa_k, ffn_maa_r, Wfk, Wfr, Wfv)

    def _L3_xattn_ref(hidden_states, encoder_hidden_states, encoder_attention_mask, ln1_w, ln1_b, q_w, q_b, k_w, k_b, v_w, v_b, cproj_w, cproj_b, ln2_w, ln2_b, fc_w, fc_b, proj_w, proj_b):
        import jax, jax.numpy as jnp
        import numpy as np
        D = 512
        H = 16
        HD = D // H
        INNER = 4 * D
        EPS = 1e-05

        def layer_norm(x, w, b):
            mu = jnp.mean(x, axis=-1, keepdims=True)
            var = jnp.mean(jnp.square(x - mu), axis=-1, keepdims=True)
            return (x - mu) * jax.lax.rsqrt(var + EPS) * w + b
        B, LQ, _ = hidden_states.shape
        LK = encoder_hidden_states.shape[1]
        residual = hidden_states
        x = layer_norm(hidden_states, ln1_w, ln1_b)
        q = (x @ q_w + q_b).reshape(B, LQ, H, HD).transpose(0, 2, 1, 3)
        k = (encoder_hidden_states @ k_w + k_b).reshape(B, LK, H, HD).transpose(0, 2, 1, 3)
        v = (encoder_hidden_states @ v_w + v_b).reshape(B, LK, H, HD).transpose(0, 2, 1, 3)
        scale = 1.0 / np.sqrt(HD).astype(np.float32)
        scores = jnp.einsum('bhqd,bhkd->bhqk', q, k) * scale
        mask = encoder_attention_mask[:, None, None, :]
        mask_value = jnp.finfo(scores.dtype).min
        scores = jnp.where(mask, scores, mask_value)
        attn = jax.nn.softmax(scores, axis=-1)
        out = jnp.einsum('bhqk,bhkd->bhqd', attn, v)
        out = out.transpose(0, 2, 1, 3).reshape(B, LQ, D)
        out = out @ cproj_w + cproj_b
        hidden = out + residual
        residual = hidden
        y = layer_norm(hidden, ln2_w, ln2_b)
        y = jax.nn.gelu(y @ fc_w + fc_b, approximate=True)
        y = y @ proj_w + proj_b
        return residual + y
    x = _L0_xattn_ref(x, ctx_2048, mask_BxS2_bf1, L0_xattn_Wq, L0_xattn_Wk, L0_xattn_Wv, L0_xattn_Wo, L0_xattn_ln_gamma, L0_xattn_ln_beta, L0_xattn_gate)
    x = _L1_xattn_ref(x, ctx_2048, L1_xattn_w_q, L1_xattn_w_k, L1_xattn_w_v, L1_xattn_w_o, L1_xattn_alpha)
    x = _L2_xattn_ref(x, ctx_2048, L2_xattn_ln1_w, L2_xattn_ln1_b, L2_xattn_ln2_w, L2_xattn_ln2_b, L2_xattn_maa_x, L2_xattn_maa_w1, L2_xattn_maa_w2, L2_xattn_maa_stack, L2_xattn_time_decay, L2_xattn_td_w1, L2_xattn_td_w2, L2_xattn_u, L2_xattn_Wr, L2_xattn_Wk, L2_xattn_Wv, L2_xattn_Wg, L2_xattn_Wo, L2_xattn_gn_w, L2_xattn_gn_b, L2_xattn_ffn_maa_k, L2_xattn_ffn_maa_r, L2_xattn_Wfk, L2_xattn_Wfr, L2_xattn_Wfv)
    x = _L3_xattn_ref(x, ctx_2048, mask_BxS2_bf1, L3_xattn_ln1_w, L3_xattn_ln1_b, L3_xattn_q_w, L3_xattn_q_b, L3_xattn_k_w, L3_xattn_k_b, L3_xattn_v_w, L3_xattn_v_b, L3_xattn_cproj_w, L3_xattn_cproj_b, L3_xattn_ln2_w, L3_xattn_ln2_b, L3_xattn_fc_w, L3_xattn_fc_b, L3_xattn_proj_w, L3_xattn_proj_b)
    return x

_drawn_inputs = setup_inputs


def setup_inputs(seed=0):
    import zlib

    import numpy as np

    out = dict(_drawn_inputs(seed))
    spreads = {'L0_xattn_ln_gamma': (1.0, 0.6),
     'L0_xattn_ln_beta': (0.0, 0.8),
     'L2_xattn_ln1_w': (1.0, 0.2),
     'L2_xattn_ln1_b': (0.0, 0.287),
     'L2_xattn_ln2_w': (1.0, 0.6),
     'L2_xattn_ln2_b': (0.0, 0.8),
     'L2_xattn_gn_w': (1.0, 0.6),
     'L2_xattn_gn_b': (0.0, 0.687),
     'L3_xattn_ln1_w': (1.0, 0.6),
     'L3_xattn_ln1_b': (0.0, 0.8),
     'L3_xattn_q_b': (0.0, 0.8),
     'L3_xattn_k_b': (0.0, 0.8),
     'L3_xattn_v_b': (0.0, 0.1),
     'L3_xattn_cproj_b': (0.0, 0.1),
     'L3_xattn_ln2_w': (1.0, 0.2),
     'L3_xattn_ln2_b': (0.0, 0.341),
     'L3_xattn_fc_b': (0.0, 0.1),
     'L3_xattn_proj_b': (0.0, 0.1)}
    factors = {'L0_xattn_Wq': 8.0,
     'L0_xattn_Wk': 8.0,
     'L1_xattn_w_q': 2.796,
     'L1_xattn_w_k': 2.805,
     'L2_xattn_maa_x': 8.0,
     'L2_xattn_maa_w1': 2.932,
     'L2_xattn_maa_w2': 2.953,
     'L2_xattn_td_w1': 8.0,
     'L2_xattn_td_w2': 8.0,
     'L2_xattn_u': 3.034,
     'L2_xattn_ffn_maa_k': 5.485,
     'L2_xattn_ffn_maa_r': 8.0,
     'L2_xattn_Wfr': 3.949,
     'L3_xattn_q_w': 7.42,
     'L3_xattn_k_w': 7.279}
    for name, (base, spread) in spreads.items():
        noise = np.random.default_rng([zlib.crc32(name.encode()), seed]).standard_normal(out[name].shape)
        drawn = base * np.exp(spread * noise) if base else spread * noise
        out[name] = jnp.asarray(drawn.astype(out[name].dtype))
    for name, factor in factors.items():
        out[name] = (out[name] * factor).astype(out[name].dtype)
    return out
```

```python
from contextlib import ExitStack

import numpy as np
import concourse.bass as bass
from concourse import mybir

F32 = mybir.dt.float32
F32R = mybir.dt.float32r
U8 = mybir.dt.uint8
ALU = mybir.AluOpType
ACT = mybir.ActivationFunctionType
AX = mybir.AxisListType

P = 128
B = 16
T = 256
NT = T // P
D = 512
KC = D // P
H = 16
HD = D // H
RH = 32
RS = D // RH
GH = P // RS
DM = 32
NMIX = 5
DD = 64
INNER = 4 * D
NI = INNER // P
EPS = 1e-5
FMAX = 3.4028235e38
JH = 4


class Batch:

    def __init__(self, u, c):
        self.u, self.c = u, c
        self.par = c % 2

    def times(self, n, plus=0):
        return self.u * (2 * n) + (self.c * n + plus)

    def half(self, n, plus=0):
        return self.u * n + ((self.c // 2) * n + plus)

    def back(self, lag):
        return Batch(self.u, self.c - lag)

    def exists(self):
        return not isinstance(self.u, int) or 0 <= 2 * self.u + self.c


class Steps:

    def __init__(self, nc, ctx, seen):
        self.nc, self.ctx, self.seen, self.found, self.sems, self.waited = nc, ctx, seen, {}, {}, {}
        self.names = {id(nc.tensor): "pe", id(nc.vector): "dve", id(nc.scalar): "act",
                      id(nc.gpsimd): "pool", id(nc.sync): "sp"}

    def sem(self, *key):
        if key not in self.sems:
            self.sems[key] = self.ctx.enter_context(self.nc.semaphore("_".join(map(str, key))))
        return self.sems[key]


class Lane:
    def __init__(self, steps, name, b):
        self.s, self.name, self.b, self.par, self.n = steps, name, b, b.par, {}

    def did(self, eng, ins, step=None):
        key = (self.name, self.s.names[id(eng)])
        self.n[key] = self.n.get(key, 0) + 1
        ins.then_inc(self.s.sem(*key), 1)
        if step is not None:
            self.s.found[(self.name, step)] = (key, self.n[key])

    def moved(self, ins, step):
        key = (self.name, "dma", step)
        self.n[key] = self.n.get(key, 0) + 16
        ins.then_inc(self.s.sem(*key, self.par), 16)
        self.s.found[(self.name, step)] = (key, None)

    def slot(self, ins, step, slot):
        key = (self.name, slot)
        self.n[key] = self.n.get(key, 0) + 16
        ins.then_inc(self.s.sem(*key), 16)
        self.s.found[(self.name, step)] = (key, self.n[key])

    def end(self):
        for key, n in self.n.items():
            self.s.found[key] = n

    def need(self, eng, *steps, lag=0, of=None):
        lane = of or self.name
        for step in steps:
            b = Batch(0, 0) if lane.endswith("setup") else self.b.back(lag)
            if not b.exists():
                continue
            assert b.c >= 0
            key, count = self.s.seen.get((lane, step), ((lane, "pe"), 1))
            per = self.s.seen.get(key, 1)
            if count is None:
                sem, value, const = self.s.sem(*key, b.par), b.half(per, per), (b.c // 2) * per + per
            else:
                sem, value, const = self.s.sem(*key), b.times(per, count), b.c * per + count
            known = (id(eng), sem.name if hasattr(sem, "name") else id(sem))
            if self.s.waited.get(known, -10 ** 9) >= const:
                continue
            self.s.waited[known] = const
            eng.wait_ge(sem, value)
            if eng in (self.s.nc.sync, self.s.nc.gpsimd):
                self.hold(eng)

    def hold(self, eng):
        eng.sem_inc(self.s.sem("held", self.s.names[id(eng)]), 1)

    def ring(self, eng, step, n, depth, total):
        if n >= depth:
            self.need(eng, f"{step}{n - depth}")
        else:
            self.need(eng, f"{step}{n - depth + total}", lag=1)


def pipeline(nc, steps, lanes, stages):
    K = len(stages)
    peel = K + (B - K) % 2

    def turn(u, c):
        steps.waited = {}
        work = []
        for k, stage in enumerate(stages):
            b = Batch(u, c - k)
            if isinstance(u, int) and not 0 <= c - k < B:
                continue
            lane = Lane(steps, lanes[k], b)
            work.append([stage(lane), lane, 0, max(steps.seen.get((lanes[k], "yields"), 1), 1)])
        while work:
            w = min(work, key=lambda w: w[2] / w[3])
            try:
                next(w[0])
                w[2] += 1
            except StopIteration:
                steps.found[(w[1].name, "yields")] = w[2]
                w[1].end()
                work.remove(w)

    for t in range(peel):
        turn(0, t)
    with nc.Fori(0, (B - peel) // 2) as u:
        turn(u, peel)
        turn(u, peel + 1)
    for t in range(B, B + K - 1):
        turn(0, t)


def program(nc, d, seen):
    PE, DVE, ACTE, POOL, SP = nc.tensor, nc.vector, nc.scalar, nc.gpsimd, nc.sync
    top = ExitStack()
    steps = Steps(nc, top, seen)
    with top:
        def tile(ctx, name, shape, dt=F32):
            return ctx.enter_context(nc.sbuf_tensor(name, shape, dt))

        def pair(ctx, name, shape):
            return [tile(ctx, f"{name}_{part}", shape, F32R) for part in ("hi", "lo")]

        def both(ctx, make, name, *a):
            return [make(ctx, f"{name}{i}", *a) for i in range(2)]

        banks = [top.enter_context(nc.psum_tensor(f"bank{i}", [P, 512], F32)) for i in range(8)]
        ident = tile(top, "ident", [P, P])
        headsum = tile(top, "headsum", [P, GH])
        mhalf = tile(top, "mhalf", [P, RH * NT])

        def setup_done(S, *engines):
            S.end()
            for e in engines:
                for step in [k[1] for k in steps.found if k[0] == S.name and isinstance(steps.found[k], tuple)]:
                    S.need(e, step, of=S.name)

        S = Lane(steps, "const_setup", Batch(0, 0))
        S.did(POOL, POOL.memset(ident[:, :], 0.0), "zero")
        S.need(POOL, "zero", of="const_setup")
        S.did(POOL, POOL.affine_select(out=ident[:, :], in_=ident[:, :], compare_op=ALU.not_equal, fill=1.0,
                                       base=0, pattern=[[-1, P]], channel_multiplier=1), "ident")
        S.did(POOL, POOL.memset(mhalf[:, :], -0.5), "mhalf")
        S.did(POOL, POOL.memset(headsum[:, :], 1.0), "ones")
        S.need(POOL, "ones", of="const_setup")
        S.did(POOL, POOL.affine_select(out=headsum[:, :], in_=headsum[:, :], compare_op=ALU.is_ge, fill=0.0,
                                       base=0, pattern=[[-RS, GH]], channel_multiplier=1), "low")
        S.need(POOL, "low", of="const_setup")
        S.did(POOL, POOL.affine_select(out=headsum[:, :], in_=headsum[:, :], compare_op=ALU.is_ge, fill=0.0,
                                       base=RS - 1, pattern=[[RS, GH]], channel_multiplier=-1), "headsum")
        setup_done(S, PE, DVE, POOL)

        def product(out, pairs, first=True, last=True):
            n = len(pairs)
            for i, (lhs, rhs) in enumerate(pairs):
                for j, (x, y) in enumerate(((0, 0), (0, 1), (1, 0))):
                    ins = PE.matmul(out, lhs[x], rhs[y], start=first and i == 0 and j == 0,
                                    stop=last and i == n - 1 and j == 2)
            return ins

        def parts(pr, *idx):
            return [t[idx] for t in pr]

        def load_weights(ctx, S, names):
            out = []
            tmp = ExitStack()
            stage = [tmp.enter_context(nc.sbuf_tensor(f"{S.name}_stage{i}", [P, KC * D], F32, side="right"))
                     for i in range(2)]
            for i, (name, src) in enumerate(names):
                rows, cols = src.shape
                c = rows // min(rows, P)
                w = pair(ctx, f"w_{name}", [min(rows, P), c, cols])
                st = stage[i % 2][0:min(rows, P), 0:c * cols].rearrange("p (c n) -> p c n", c=c)
                if i >= 2:
                    S.need(SP, f"lo{i - 2}", of=S.name)
                S.slot(SP.dma_start(st, src.rearrange("(c p) n -> p c n", p=min(rows, P))), f"load{i}", f"stage{i % 2}")
                S.need(ACTE, f"load{i}", of=S.name)
                S.did(ACTE, ACTE.activation(w[0][:, :, :], st, ACT.Copy), f"hi{i}")
                S.need(DVE, f"hi{i}", f"load{i}", of=S.name)
                S.did(DVE, DVE.tensor_tensor(w[1][:, :, :], st, w[0][:, :, :].bitcast(F32), ALU.subtract), f"lo{i}")
                out.append(w)
            tmp.close()
            return out

        def columns(ctx, S, name, key=None):
            src = d[name]
            n = src.shape[0] // P
            t = tile(ctx, f"c_{name}", [P, n])
            with nc.allow_non_contiguous_dma(reason="a vector of features, once"):
                S.moved(SP.dma_start(t[:, :], src.rearrange("(c p) -> p c", p=P)), "vectors")
            return t

        def rows(ctx, S, name):
            n = d[name].shape[0]
            t = tile(ctx, f"r_{name}", [P, n])
            S.moved(SP.dma_start(t[:, :], d[name].rearrange("(a n) -> a n", a=1).broadcast_to([P, n])), "vectors")
            return t

        def norm(L, x, xn, st, src):
            stats, agg, rstd = st
            L.need(DVE, src)
            L.need(DVE, "pow", "norm1", lag=1)
            for t in range(NT):
                L.did(DVE, DVE.bn_stats(stats[:, t, :], x[:, t, :]), f"bn{t}")
                L.need(DVE, f"bn{t}")
                L.hold(DVE)
                L.did(DVE, DVE.bn_aggr(agg[:, t, :], stats[:, t, :]), f"agg{t}")
            L.need(POOL, "agg1")
            L.need(POOL, "norm1", lag=1)
            L.did(POOL, POOL.tensor_scalar(rstd[:, :], agg[:, :, 1], EPS, None, ALU.add), "vareps")
            L.need(POOL, "vareps")
            L.did(POOL, POOL.tensor_tensor(rstd[:, :], rstd[:, :], mhalf[:, 0:NT], ALU.pow), "pow")
            L.need(DVE, "pow")
            L.need(DVE, "xposed1", lag=1)
            for t in range(NT):
                L.did(DVE, DVE.tensor_scalar(xn[:, t, :], x[:, t, :], agg[:, t, 0:1], rstd[:, t:t + 1],
                                             ALU.subtract, ALU.mult), f"norm{t}")

        def norm_tiles(ctx, name):
            return (tile(ctx, f"{name}_stats", [P, NT, 6]), tile(ctx, f"{name}_agg", [P, NT, 2]),
                    tile(ctx, f"{name}_rstd", [P, NT]))

        def xpose(L, x, bank, c2, name):
            for c in range(2):
                for t in range(NT):
                    ins = PE.transpose(bank[:, c * T + t * P:c * T + (t + 1) * P],
                                       x[:, t, (2 * c2 + c) * P:(2 * c2 + c + 1) * P], ident[:, :])
            L.did(PE, ins, name)

        def split(L, full, pr, name, free=None):
            if free:
                L.need(ACTE, free, lag=1)
            L.did(ACTE, ACTE.activation(pr[0][:], full, ACT.Copy), f"{name}_hi")
            L.need(POOL, f"{name}_hi")
            L.did(POOL, POOL.tensor_tensor(pr[1][:], full, pr[0][:].bitcast(F32), ALU.subtract), f"{name}_lo")

        def chunk2(t, c2):
            return t[:, 2 * c2:2 * c2 + 2, :]

        def as2(bank, n=T):
            return bank[:, 0:2 * n].rearrange("p (c t) -> p c t", c=2)

        def proj_T(bank, w, xT, c2):
            for c in range(2):
                m = 2 * c2 + c
                ins = product(bank[:, c * T:(c + 1) * T],
                              [(parts(w, slice(None), k, slice(m * P, (m + 1) * P)), parts(xT, slice(None), k, slice(None)))
                               for k in range(KC)])
            return ins

        def proj_N(bank, w, xT, t, k0=0, kn=KC, **kw):
            return product(bank[:, :],
                           [(parts(xT, slice(None), k, slice(t * P, (t + 1) * P)), parts(w, slice(None), k, slice(None)))
                            for k in range(k0, k0 + kn)], **kw)

        def attention(ph, x_in, x_out, first):
            ctx = ExitStack()
            with ctx:
                S = Lane(steps, f"{ph}setup", Batch(0, 0))
                F, Bk = f"{ph}f", f"{ph}b"
                if first:
                    gamma, beta = columns(ctx, S, "L0_xattn_ln_gamma"), columns(ctx, S, "L0_xattn_ln_beta")
                    gate = tile(ctx, "gate", [P, 1])
                    S.moved(SP.dma_start(gate[:, :], d["L0_xattn_gate"].rearrange("(a n) -> a n", a=1).broadcast_to([P, 1])), "vectors")
                    ws = ["L0_WqT", "L0_WkT", "L0_WvT", "L0_WoT"]
                else:
                    gamma, beta = columns(ctx, S, "L3_xattn_ln1_w"), columns(ctx, S, "L3_xattn_ln1_b")
                    qb, kb = columns(ctx, S, "L3_xattn_q_b"), columns(ctx, S, "L3_xattn_k_b")
                    vb, cb = rows(ctx, S, "L3_xattn_v_b"), rows(ctx, S, "L3_xattn_cproj_b")
                    ws = ["L3_xattn_q_w", "L3_xattn_k_w", "L3_xattn_v_w", "L3_xattn_cproj_w"]
                wq, wk, wv, wo = load_weights(ctx, S, [(w, d[w]) for w in ws])
                scale = float(HD) ** -0.5
                if first:
                    tg = tile(ctx, "tanh_gate", [P, 1])
                    S.need(ACTE, "vectors", of=S.name)
                    S.did(ACTE, ACTE.activation(tg[:, :], gate[:, :], ACT.Tanh), "tanh_gate")
                else:
                    nqb = tile(ctx, "neg_scaled_qb", [P, KC])
                    S.need(DVE, "vectors", of=S.name)
                    S.did(DVE, DVE.tensor_scalar(nqb[:, :], qb[:, :], -scale, None, ALU.mult), "nqb")
                setup_done(S, PE, DVE, ACTE, POOL, SP)

                x = both(ctx, tile, f"{ph}_x", [P, NT, D])
                raw = tile(ctx, f"{ph}_ctx", [P, NT, D]) if first else None
                other = tile(ctx, f"{ph}_oT", [P, KC, T])
                otherp = pair(ctx, f"{ph}_oTp", [P, KC, T])
                nst = norm_tiles(ctx, ph)
                xn = tile(ctx, f"{ph}_xn", [P, NT, D])
                aT = tile(ctx, f"{ph}_aT", [P, KC, T])
                aTp = pair(ctx, f"{ph}_aTp", [P, KC, T])
                QT = both(ctx, tile, f"{ph}_QT", [P, KC, T])
                KT = both(ctx, tile, f"{ph}_KT", [P, KC, T])
                V = both(ctx, tile, f"{ph}_V", [P, NT, D])
                m8 = both(ctx, tile, f"{ph}_m8", [P, T], U8)
                mb = both(ctx, tile, f"{ph}_mb", [P, T])
                NS = 4
                sm = [tile(ctx, f"{ph}_s{i}", [P, NT, T]) for i in range(NS)]
                smin = tile(ctx, f"{ph}_smin", [P, NT, H])
                ssum = tile(ctx, f"{ph}_ssum", [P, NT, H])
                rsum = tile(ctx, f"{ph}_rsum", [P, NT, H])
                pT = both(ctx, tile, f"{ph}_pT", [P, NT, T])
                on = tile(ctx, f"{ph}_on", [P, NT, D])
                oTp = pair(ctx, f"{ph}_attT", [P, KC, T])
                y = tile(ctx, f"{ph}_y", [P, NT, D])

                fb = banks[0:2]
                NF = 8

                def front(L):
                    b = L.b
                    L.need(SP, "out1", lag=2, of=Bk)
                    tok = lambda n: n.rearrange("(t p) f -> p t f", p=P)
                    L.moved(SP.dma_start(x[L.par][:, :, :], tok(x_in[bass.ds(b.times(T), T), :])), "ld_x")
                    if first:
                        L.need(SP, "norm1", lag=1)
                        L.moved(SP.dma_start(raw[:, :, :], tok(d["ctx"][bass.ds(b.times(T), T), :])), "ld_raw")
                    L.need(SP, "o_lo", lag=1)
                    L.moved(SP.dma_start(other[:, :, :], d["xT" if first else "ctxT"][:, bass.ds(b.times(T), T)]
                                         .rearrange("(c p) t -> p c t", p=P)), "ld_other")
                    L.need(SP, "mask1", lag=2)
                    L.moved(SP.dma_start(m8[L.par][:, :], d["mask"][bass.ds(b.times(1), 1), :].broadcast_to([P, T])), "ld_mask")
                    yield
                    L.need(DVE, "ld_mask")
                    L.need(DVE, f"min{H - 1}_1", lag=2, of=Bk)
                    big = 3e38 if first else FMAX
                    L.did(DVE, DVE.tensor_scalar(mb[L.par][:, :], m8[L.par][:, :], 1.0, -big, ALU.subtract, ALU.mult), "mask0")
                    L.need(DVE, "mask0")
                    L.did(DVE, DVE.tensor_scalar(mb[L.par][:, :], mb[L.par][:, :], 10.0 if first else 1.0, None, ALU.mult), "mask1")
                    L.need(ACTE, "ld_other")
                    L.need(ACTE, "mm5" if not first else "mm3", "mm7", lag=1)
                    split(L, other[:, :, :], otherp, "o")
                    norm(L, raw if first else x[L.par], xn, nst, "ld_raw" if first else "ld_x")
                    yield
                    for c2 in range(2):
                        L.need(PE, "norm1")
                        L.ring(PE, "ev", c2, 2, NF)
                        xpose(L, xn, fb[c2], c2, f"xposed{c2}")
                        L.need(ACTE, f"xposed{c2}")
                        L.need(ACTE, "a_lo", lag=1)
                        for c in range(2):
                            k = 2 * c2 + c
                            L.did(ACTE, ACTE.activation(aT[:, k, :], fb[c2][:, c * T:(c + 1) * T], ACT.Identity,
                                                        scale=gamma[:, k:k + 1], bias=beta[:, k:k + 1]), f"ev{c2}")
                        yield
                    L.need(ACTE, "ev1")
                    L.need(ACTE, "mm7", "mm3", lag=1)
                    split(L, aT[:, :, :], aTp, "a")
                    xTq, kvT = (otherp, aTp) if first else (aTp, otherp)
                    qs, kvs = ("o", "a") if first else ("a", "o")
                    for i in range(2):
                        L.need(PE, f"{qs}_lo")
                        L.ring(PE, "ev", 2 + i, 2, NF)
                        L.did(PE, proj_T(fb[i], wq, xTq, i), f"mm{2 + i}")
                        L.need(ACTE, f"mm{2 + i}")
                        L.need(ACTE, f"qk{H - 1}", lag=2, of=Bk)
                        if first:
                            L.did(ACTE, ACTE.activation(chunk2(QT[L.par], i), as2(fb[i]), ACT.Copy, scale=-scale), f"ev{2 + i}")
                        else:
                            for c in range(2):
                                k = 2 * i + c
                                L.did(ACTE, ACTE.activation(QT[L.par][:, k, :], fb[i][:, c * T:(c + 1) * T], ACT.Identity,
                                                            scale=-scale, bias=nqb[:, k:k + 1]), f"ev{2 + i}")
                        yield
                    for i in range(2):
                        L.need(PE, f"{kvs}_lo")
                        L.ring(PE, "ev", 4 + i, 2, NF)
                        L.did(PE, proj_T(fb[i], wk, kvT, i), f"mm{4 + i}")
                        L.need(ACTE, f"mm{4 + i}")
                        L.need(ACTE, f"qk{H - 1}", lag=2, of=Bk)
                        if first:
                            L.did(ACTE, ACTE.activation(chunk2(KT[L.par], i), as2(fb[i]), ACT.Copy), f"ev{4 + i}")
                        else:
                            for c in range(2):
                                k = 2 * i + c
                                L.did(ACTE, ACTE.activation(KT[L.par][:, k, :], fb[i][:, c * T:(c + 1) * T], ACT.Identity,
                                                            bias=kb[:, k:k + 1]), f"ev{4 + i}")
                        yield
                    for t in range(NT):
                        L.ring(PE, "ev", 6 + t, 2, NF)
                        L.did(PE, proj_N(fb[t], wv, kvT, t), f"mm{6 + t}")
                        L.need(DVE, f"mm{6 + t}")
                        L.need(DVE, f"av{H - 1}", lag=2, of=Bk)
                        if first:
                            L.did(DVE, DVE.tensor_copy(V[L.par][:, t, :], fb[t][:, :]), f"ev{6 + t}")
                        else:
                            L.did(DVE, DVE.tensor_tensor(V[L.par][:, t, :], fb[t][:, :], vb[:, :], ALU.add), f"ev{6 + t}")
                        yield
                    if not first:
                        L.need(POOL, "norm1")
                        L.did(POOL, POOL.tensor_tensor(x[L.par][:, :, :], x[L.par][:, :, :],
                                                       cb[:, None, :].broadcast_to([P, NT, D]), ALU.add), "x_cb")

                sb, tb, ob = banks[2:4], banks[4:6], banks[6:8]

                def back(L):
                    q, k, v = QT[L.par], KT[L.par], V[L.par]
                    L.need(DVE, "ld_x", of=F)

                    def scores(h):
                        r, c = slice(HD * (h % 4), HD * (h % 4) + HD), h // 4
                        L.need(PE, "ev3", "ev5", of=F)
                        if h >= 2:
                            L.need(PE, f"min{h - 2}_1")
                        else:
                            L.need(PE, f"oT_lo{h}", lag=1)
                        for t in range(NT):
                            ins = PE.matmul(sb[h % 2][:, t * T:(t + 1) * T], q[r, c, t * P:(t + 1) * P], k[r, c, :],
                                            start=True, stop=True)
                        L.did(PE, ins, f"qk{h}")
                        L.need(DVE, f"qk{h}")
                        L.need(DVE, "mask1", of=F)
                        L.ring(DVE, "tr", h, NS, H)
                        if h == 0:
                            L.need(DVE, f"exp{H - 1}_1", lag=1)
                        L.hold(DVE)
                        for t in range(NT):
                            L.did(DVE, DVE.tensor_tensor_reduce(
                                out=sm[h % NS][:, t, :], in0=sb[h % 2][:, t * T:(t + 1) * T], in1=mb[L.par][:, :], scale=1.0,
                                scalar=FMAX, op0=ALU.add, op1=ALU.min, accum_out=smin[:, t, h:h + 1]), f"min{h}_{t}")
                        if h == 0:
                            L.need(ACTE, "rsum", lag=1)
                        for t in range(NT):
                            L.need(ACTE, f"min{h}_{t}")
                            L.did(ACTE, ACTE.activation(sm[h % NS][:, t, :], sm[h % NS][:, t, :], ACT.Exp, scale=-1.0,
                                                        bias=smin[:, t, h:h + 1], accum_out=ssum[:, t, h:h + 1]), f"exp{h}_{t}")

                    def transpose_p(h):
                        L.need(PE, f"exp{h}_1")
                        if h >= 2:
                            L.need(PE, f"pT{h - 2}")
                        else:
                            L.need(PE, f"out{h}", lag=1)
                        for kt in range(NT):
                            for t in range(NT):
                                ins = PE.transpose(tb[h % 2][:, kt * T + t * P:kt * T + (t + 1) * P],
                                                   sm[h % NS][:, t, kt * P:(kt + 1) * P], ident[:, :])
                        L.did(PE, ins, f"tr{h}")
                        e = ACTE if h % 2 else DVE
                        L.need(e, f"tr{h}")
                        L.ring(e, "av", h, 2, H)
                        if h % 2:
                            L.did(e, ACTE.activation(pT[h % 2][:, :, :], as2(tb[h % 2]), ACT.Copy), f"pT{h}")
                        else:
                            L.did(e, DVE.tensor_copy(pT[h % 2][:, :, :], as2(tb[h % 2])), f"pT{h}")

                    def values(h):
                        L.need(PE, "ev7", of=F)
                        L.need(PE, f"pT{h}")
                        if h == 0:
                            L.need(PE, "on1", lag=1)
                        for t in range(NT):
                            for kt in range(NT):
                                ins = PE.matmul(ob[t][:, h * HD:(h + 1) * HD], pT[h % 2][:, kt, t * P:(t + 1) * P],
                                                v[:, kt, h * HD:(h + 1) * HD], start=kt == 0, stop=kt == NT - 1)
                        L.did(PE, ins, f"av{h}")

                    for h in range(H + 2):
                        if h < H:
                            scores(h)
                        if 1 <= h < H + 1:
                            transpose_p(h - 1)
                        if h >= 2:
                            values(h - 2)
                        yield
                    L.need(DVE, f"exp{H - 1}_1")
                    L.need(DVE, "on1", lag=1)
                    L.did(DVE, DVE.reciprocal(rsum[:, :, :], ssum[:, :, :]), "rsum")
                    L.need(DVE, "rsum", f"av{H - 1}")
                    L.need(DVE, "ox1", lag=1)
                    for t in range(NT):
                        L.did(DVE, DVE.tensor_tensor(on[:, t, :].rearrange("p (h e) -> p h e", h=H),
                                                     ob[t][:, :].rearrange("p (h e) -> p h e", h=H),
                                                     rsum[:, t, :, None].broadcast_to([P, H, HD]), ALU.mult), f"on{t}")
                    for c2 in range(2):
                        L.need(PE, "on1")
                        L.need(PE, f"min{H - 2 + c2}_1")
                        xpose(L, on, sb[c2], c2, f"ox{c2}")
                        L.need(ACTE, f"ox{c2}")
                        L.need(ACTE, "o1", lag=1)
                        L.did(ACTE, ACTE.activation(chunk2(oTp[0], c2), as2(sb[c2]), ACT.Copy), f"oT_hi{c2}")
                        L.need(DVE, f"oT_hi{c2}")
                        L.did(DVE, DVE.tensor_tensor(chunk2(oTp[1], c2), as2(sb[c2]), chunk2(oTp[0], c2).bitcast(F32),
                                                     ALU.subtract), f"oT_lo{c2}")
                        yield
                    for t in range(NT):
                        L.need(PE, "oT_lo1")
                        L.need(PE, f"pT{H - 2 + t}")
                        L.did(PE, proj_N(tb[t], wo, oTp, t), f"o{t}")
                        L.need(DVE, f"o{t}")
                        L.need(DVE, "st", lag=1)
                        if first:
                            L.did(DVE, DVE.scalar_tensor_tensor(y[:, t, :], tb[t][:, :], tg[:, 0:1], x[L.par][:, t, :],
                                                                ALU.mult, ALU.add), f"out{t}")
                        else:
                            L.need(DVE, "x_cb", of=F)
                            L.did(DVE, DVE.tensor_tensor(y[:, t, :], tb[t][:, :], x[L.par][:, t, :], ALU.add), f"out{t}")
                        yield
                    L.need(POOL, "out1")
                    L.moved(POOL.dma_start(x_out[bass.ds(L.b.times(T), T), :].rearrange("(t p) f -> p t f", p=P), y[:, :, :]), "st")

                pipeline(nc, steps, [F, Bk], [front, back])
                finish(ph, [Bk])

        def finish(ph, lanes):
            for name in lanes:
                for b in (B - 2, B - 1):
                    L = Lane(steps, name, Batch(0, b))
                    steps.waited = {}
                    L.need(SP, "st")
            nc.all_engine_barrier()

        def wide_attention(x_in, x_out):
            ctx = ExitStack()
            with ctx:
                S = Lane(steps, "Bsetup", Batch(0, 0))
                G = pair(ctx, "G", [P, KC, D])
                U = pair(ctx, "U", [P, KC, D])
                alpha = tile(ctx, "alpha", [P, 1])
                S.moved(SP.dma_start(alpha[:, :], d["L1_xattn_alpha"].rearrange("(a n) -> a n", a=1).broadcast_to([P, 1])), "vectors")
                tmp = ExitStack()
                with tmp:
                    wq, wk, wv, woT = load_weights(tmp, S, [(w, d[w]) for w in ("L1_xattn_w_q", "L1_xattn_w_k", "L1_xattn_w_v", "L1_WoT")])
                    for i, (dst, lhs, rhs, last) in enumerate(((G, wq, wk, "lo1"), (U, wv, woT, "lo3"))):
                        for m in range(KC):
                            n = i * KC + m
                            S.need(PE, last, of=S.name)
                            ins = product(banks[n][:, :], [(parts(lhs, slice(None), k, slice(m * P, (m + 1) * P)),
                                                            parts(rhs, slice(None), k, slice(None))) for k in range(KC)])
                            S.did(PE, ins, f"fold{n}")
                            S.need(ACTE, f"fold{n}", of=S.name)
                            S.did(ACTE, ACTE.activation(dst[0][:, m, :], banks[n][:, :], ACT.Copy), f"fold_hi{n}")
                            S.need(DVE, f"fold_hi{n}", of=S.name)
                            S.did(DVE, DVE.tensor_tensor(dst[1][:, m, :], banks[n][:, :], dst[0][:, m, :].bitcast(F32),
                                                         ALU.subtract), f"fold_lo{n}")
                setup_done(S, PE, DVE, ACTE, POOL, SP)
                scale = float(D) ** -0.5

                x = both(ctx, tile, "B_x", [P, NT, D])
                cT = tile(ctx, "B_cT", [P, KC, T])
                cTp = both(ctx, pair, "B_cTp", [P, KC, T])
                xTp = pair(ctx, "B_xTp", [P, KC, T])
                qTp = both(ctx, pair, "B_qTp", [P, KC, T])
                Vp = both(ctx, pair, "B_Vp", [P, NT, D])
                smax = tile(ctx, "B_smax", [P, NT])
                nmax = tile(ctx, "B_nmax", [P, NT])
                pr = tile(ctx, "B_p", [P, NT, T])
                ssum = tile(ctx, "B_ssum", [P, NT])
                rsum = tile(ctx, "B_rsum", [P, NT])
                pTp = pair(ctx, "B_pTp", [P, NT, T])
                y = tile(ctx, "B_y", [P, NT, D])
                fb = banks[0:4]

                def evac(L, bank, pr_c, n, free):
                    L.need(ACTE, f"mm{n}")
                    for f, lag, of in free:
                        L.need(ACTE, f, lag=lag, of=of)
                    L.did(ACTE, ACTE.activation(pr_c[0], bank, ACT.Copy), f"hi{n}")
                    L.need(DVE, f"hi{n}")
                    L.did(DVE, DVE.tensor_tensor(pr_c[1], bank, pr_c[0].bitcast(F32), ALU.subtract), f"ev{n}")

                def front(L):
                    b = L.b
                    L.need(SP, "out1", lag=2, of="Bb")
                    L.moved(SP.dma_start(x[L.par][:, :, :], x_in[bass.ds(b.times(T), T), :].rearrange("(t p) f -> p t f", p=P)), "ld_x")
                    L.need(SP, "c_lo", lag=1)
                    L.moved(SP.dma_start(cT[:, :, :], d["ctxT"][:, bass.ds(b.times(T), T)].rearrange("(c p) t -> p c t", p=P)), "ld_c")
                    yield
                    L.need(ACTE, "ld_c")
                    L.need(ACTE, "mm5", lag=2)
                    L.need(ACTE, "qk", lag=2, of="Bb")
                    split(L, cT[:, :, :], cTp[L.par], "c")
                    for i in range(2):
                        L.need(PE, "ld_x")
                        L.ring(PE, "ev", i, 4, 8)
                        xpose(L, x[L.par], fb[i], i, f"mm{i}")
                        evac(L, as2(fb[i]), [chunk2(xTp[j], i) for j in range(2)], i, [("mm3", 1, None)])
                        yield
                    for i in range(2):
                        n = 2 + i
                        L.need(PE, "ev1")
                        L.ring(PE, "ev", n, 4, 8)
                        L.did(PE, proj_T(fb[n], G, xTp, i), f"mm{n}")
                        evac(L, as2(fb[n]), [chunk2(qTp[L.par][j], i) for j in range(2)], n, [("qk", 2, "Bb")])
                        yield
                    for t in range(NT):
                        n = 4 + t
                        L.need(PE, "c_lo")
                        L.ring(PE, "ev", n, 4, 8)
                        L.did(PE, proj_N(fb[t], U, cTp[L.par], t), f"mm{n}")
                        evac(L, fb[t][:, :], [Vp[L.par][j][:, t, :] for j in range(2)], n, [("pv1", 2, "Bb")])
                        yield
                    S.s.found[(L.name, "ev6")] = S.s.found[(L.name, "ev2")]
                    S.s.found[(L.name, "ev7")] = S.s.found[(L.name, "ev3")]

                sb, tb, ob = banks[4], banks[5], banks[6:8]

                def back(L):
                    L.need(PE, "ev3", of="Bf")
                    L.need(PE, "exp1", lag=1)
                    for t in range(NT):
                        ins = product(sb[:, t * T:(t + 1) * T],
                                      [(parts(qTp[L.par], slice(None), k, slice(t * P, (t + 1) * P)),
                                        parts(cTp[L.par], slice(None), k, slice(None))) for k in range(KC)])
                    L.did(PE, ins, "qk")
                    L.need(DVE, "qk")
                    L.did(DVE, DVE.reduce_max(smax[:, :], as2(sb), AX.X), "max")
                    L.need(DVE, "max")
                    L.need(DVE, "exp1", lag=1)
                    L.did(DVE, DVE.tensor_scalar(nmax[:, :], smax[:, :], -scale, None, ALU.mult), "nmax")
                    L.need(ACTE, "nmax")
                    L.need(ACTE, "pt", "rsum", lag=1)
                    for t in range(NT):
                        L.did(ACTE, ACTE.activation(pr[:, t, :], sb[:, t * T:(t + 1) * T], ACT.Exp, scale=scale,
                                                    bias=nmax[:, t:t + 1], accum_out=ssum[:, t:t + 1]), f"exp{t}")
                    L.need(DVE, "exp1")
                    L.need(DVE, "out1", lag=1)
                    L.did(DVE, DVE.reciprocal(rsum[:, :], ssum[:, :]), "recip")
                    L.need(DVE, "recip")
                    L.did(DVE, DVE.tensor_scalar(rsum[:, :], rsum[:, :], alpha[:, 0:1], None, ALU.mult), "rsum")
                    yield
                    yield
                    L.need(PE, "exp1")
                    L.need(PE, "pT_lo", lag=1)
                    for kt in range(NT):
                        for t in range(NT):
                            ins = PE.transpose(tb[:, kt * T + t * P:kt * T + (t + 1) * P], pr[:, t, kt * P:(kt + 1) * P], ident[:, :])
                    L.did(PE, ins, "pt")
                    L.need(ACTE, "pt")
                    L.need(ACTE, "pv1", lag=1)
                    L.did(ACTE, ACTE.activation(pTp[0][:, :, :], as2(tb), ACT.Copy), "pT_hi")
                    L.need(DVE, "pT_hi")
                    L.did(DVE, DVE.tensor_tensor(pTp[1][:, :, :], as2(tb), pTp[0][:, :, :].bitcast(F32), ALU.subtract), "pT_lo")
                    yield
                    yield
                    for t in range(NT):
                        L.need(PE, "pT_lo")
                        L.need(PE, "ev5", of="Bf")
                        L.need(PE, f"out{t}", lag=1)
                        ins = product(ob[t][:, :], [(parts(pTp, slice(None), kt, slice(t * P, (t + 1) * P)),
                                                     parts(Vp[L.par], slice(None), kt, slice(None))) for kt in range(NT)])
                        L.did(PE, ins, f"pv{t}")
                        L.need(DVE, f"pv{t}", "rsum")
                        L.need(DVE, "st", lag=1)
                        L.did(DVE, DVE.scalar_tensor_tensor(y[:, t, :], ob[t][:, :], rsum[:, t:t + 1], x[L.par][:, t, :],
                                                            ALU.mult, ALU.add), f"out{t}")
                    L.need(POOL, "out1")
                    L.moved(POOL.dma_start(x_out[bass.ds(L.b.times(T), T), :].rearrange("(t p) f -> p t f", p=P), y[:, :, :]), "st")
                    yield

                pipeline(nc, steps, ["Bf", "Bb"], [front, back])
                finish("B", ["Bb"])

        def mix_T(L, out, xT, sx, coef, name):
            for k in range(KC):
                L.did(DVE, DVE.scalar_tensor_tensor(out[:, k, :], sx[:, k, :], coef[:, k:k + 1], xT[:, k, 1:T + 1],
                                                    ALU.mult, ALU.add), name)

        def tokens(ap, b):
            return ap[bass.ds(b.times(T), T), :].rearrange("(t p) f -> p t f", p=P)

        def load_column0(L, xT, row, step):
            with nc.allow_non_contiguous_dma(reason="one token's features, one per partition"):
                L.moved(SP.dma_start(xT[:, :, 0:1], d["ctxT"][:, bass.ds(L.b.times(T, row), 1)]
                                     .rearrange("(c p) t -> p c t", p=P)), step)

        def time_mix(x_in, z_out):
            ctx = ExitStack()
            with ctx:
                S = Lane(steps, "Csetup", Batch(0, 0))
                L2 = lambda n: d["L2_xattn_" + n]
                ln_w, ln_b, maa_x, stack, decay, u, gn_w, gn_b = [
                    columns(ctx, S, "L2_xattn_" + n) for n in
                    ("ln1_w", "ln1_b", "maa_x", "maa_stack", "time_decay", "u", "gn_w", "gn_b")]
                wr, wk, wv, wg, w1, w2a, w2b, td1, td2 = load_weights(ctx, S, [
                    ("Wr", d["L2_WrT"]), ("Wk", d["L2_WkT"]), ("Wv", d["L2_WvT"]), ("Wg", d["L2_WgT"]),
                    ("maa_w1", L2("maa_w1")), ("maa_w2a", L2("maa_w2")[0:P, :]), ("maa_w2b", L2("maa_w2")[P:NMIX * DM, :]),
                    ("td_w1", L2("td_w1")), ("td_w2", L2("td_w2"))])
                S.need(DVE, "vectors", of=S.name)
                for t_, n in ((gn_w, "half_w"), (gn_b, "half_b")):
                    S.did(DVE, DVE.tensor_scalar(t_[:, :], t_[:, :], 0.5, None, ALU.mult), n)
                setup_done(S, PE, DVE, ACTE, POOL, SP)

                x = tile(ctx, "C_x", [P, NT, D])
                nst = norm_tiles(ctx, "C")
                xn = tile(ctx, "C_xn", [P, NT, D])
                ruk = xn[:, :, :].rearrange("p t d -> p (t d)").rearrange("p (c t) -> p c t", c=KC)
                xaT = tile(ctx, "C_xaT", [P, KC, T + 1])
                sx = tile(ctx, "C_sx", [P, KC, T])
                mf = tile(ctx, "C_mix", [P, KC, T])
                mp = pair(ctx, "C_mixp", [P, KC, T])
                tx = tile(ctx, "C_tx", [P, 2, T])
                txp = pair(ctx, "C_txp", [P, 2, T])
                th = tile(ctx, "C_th", [P, 2, T])
                vT = tile(ctx, "C_vT", [P, KC, T])
                vtok = both(ctx, tile, "C_vtok", [P, NT, D])
                wT = both(ctx, tile, "C_wT", [P, KC, T])
                kT = both(ctx, tile, "C_kT", [P, KC, T])
                rT = both(ctx, tile, "C_rT", [P, KC, T])
                gT = both(ctx, tile, "C_gT", [P, KC, T])
                ctok = both(ctx, tile, "C_ctok", [P, NT, RH])
                s0 = both(ctx, tile, "C_s0", [P, KC, RS])
                NV, NX = 4, 2
                Vb = [tile(ctx, f"C_V{i}", [P, JH, T]) for i in range(NV)]
                Sx = [tile(ctx, f"C_S{i}", [P, JH, T]) for i in range(NX)]
                og = tile(ctx, "C_og", [P, NT * RH, RS])
                sq = tile(ctx, "C_sq", [P, NT * RH, RS])
                s1 = tile(ctx, "C_s1", [P, NT * RH])
                s2 = tile(ctx, "C_s2", [P, NT * RH])
                zT = tile(ctx, "C_zT", [P, KC, T])
                fb, NF = banks[0:4], 28
                YB, ZB = banks[4:6], banks[6:8]
                UN = KC * (RS // JH)

                def front(L):
                    b, par = L.b, L.par
                    n = [0]

                    def bank(eng=PE):
                        k = n[0]
                        n[0] += 1
                        L.ring(PE, "ev", k, 4, NF)
                        return k, fb[k % 4]

                    L.need(SP, "norm1", lag=1)
                    L.moved(SP.dma_start(x[:, :, :], tokens(x_in, b)), "ld_x")
                    L.need(SP, "mixadd4", lag=1)
                    load_column0(L, xaT, 1, "ld_prev")
                    L.need(SP, f"scan{UN - 1}", f"s0_{UN - 1}", lag=2, of="Cb")
                    for g in range(KC):
                        L.moved(SP.dma_start(s0[par][:, g, :], d["ctx"][bass.ds(b.times(T, 2 + 4 * g), 4), :]
                                             .rearrange("r (q j) -> (r q) j", j=RS)), "ld_s0")
                    L.need(DVE, "cmm", lag=1)
                    norm(L, x, xn, nst, "ld_x")
                    yield
                    for c2 in range(2):
                        k, bk = bank()
                        L.need(PE, "norm1")
                        xpose(L, xn, bk, c2, f"xposed{c2}")
                        L.need(ACTE, f"xposed{c2}")
                        L.need(ACTE, "mixadd4", lag=1)
                        for c in range(2):
                            m = 2 * c2 + c
                            L.did(ACTE, ACTE.activation(xaT[:, m, 1:T + 1], bk[:, c * T:(c + 1) * T], ACT.Identity,
                                                        scale=ln_w[:, m:m + 1], bias=ln_b[:, m:m + 1]), f"ev{k}")
                        yield
                    L.need(DVE, "ev1", "ld_prev")
                    L.did(DVE, DVE.tensor_tensor(sx[:, :, :], xaT[:, :, 0:T], xaT[:, :, 1:T + 1], ALU.subtract), "sx")
                    L.need(DVE, "sx")
                    L.need(DVE, "mix4_lo", lag=1)
                    mix_T(L, mf, xaT, sx, maa_x, "xi")
                    L.need(ACTE, "xi")
                    L.need(ACTE, "proj4_1", lag=1)
                    split(L, mf[:, :, :], mp, "xi")
                    k, bk = bank()
                    L.need(PE, "xi_lo")
                    for c, rows_ in ((0, P), (1, DM)):
                        ins = product(bk[0:rows_, c * T:(c + 1) * T],
                                      [(parts(w1, slice(None), q, slice(c * P, c * P + rows_)), parts(mp, slice(None), q, slice(None)))
                                       for q in range(KC)])
                    L.did(PE, ins, "w1mm")
                    L.need(ACTE, "w1mm")
                    L.need(ACTE, "tx_lo", lag=1)
                    L.did(ACTE, ACTE.activation(tx[:, 0, :], bk[:, 0:T], ACT.Tanh), "tx0")
                    L.did(ACTE, ACTE.activation(tx[0:DM, 1, :], bk[0:DM, T:2 * T], ACT.Tanh), f"ev{k}")
                    L.need(ACTE, f"ev{k}")
                    L.need(ACTE, "w2mm4_1", lag=1)
                    for rows_, c in ((P, 0), (DM, 1)):
                        L.did(ACTE, ACTE.activation(txp[0][0:rows_, c, :], tx[0:rows_, c, :], ACT.Copy), "tx_hi")
                    L.need(POOL, "tx_hi")
                    for rows_, c in ((P, 0), (DM, 1)):
                        L.did(POOL, POOL.tensor_tensor(txp[1][0:rows_, c, :], tx[0:rows_, c, :],
                                                       txp[0][0:rows_, c, :].bitcast(F32), ALU.subtract), "tx_lo")
                    yield

                    def mix(f, last_reader):
                        w2 = w2a if f < 4 else w2b
                        r = slice(DM * (f % 4), DM * (f % 4) + DM)
                        for c2 in range(2):
                            k, bk = bank()
                            L.need(PE, "tx_lo")
                            for c in range(2):
                                m = 2 * c2 + c
                                ins = product(bk[:, c * T:(c + 1) * T], [(parts(w2, r, 0, slice(m * P, (m + 1) * P)),
                                                                          parts(txp, r, f // 4, slice(None)))])
                            L.did(PE, ins, f"w2mm{f}_{c2}")
                            L.need(DVE, f"w2mm{f}_{c2}", last_reader[0])
                            for c in range(2):
                                m = 2 * c2 + c
                                L.did(DVE, DVE.scalar_tensor_tensor(mf[:, m, :], bk[:, c * T:(c + 1) * T],
                                                                    stack[:, KC * f + m:KC * f + m + 1], sx[:, m, :],
                                                                    ALU.add, ALU.mult), f"ev{k}")
                        L.need(POOL, f"ev{k}")
                        L.did(POOL, POOL.tensor_tensor(mf[:, :, :], mf[:, :, :], xaT[:, :, 1:T + 1], ALU.add), f"mixadd{f}")
                        L.need(ACTE, f"mixadd{f}", last_reader[1])
                        split(L, mf[:, :, :], mp, f"mix{f}")

                    def proj(f, w, evac, free=()):
                        for c2 in range(2):
                            k, bk = bank()
                            L.need(PE, f"mix{f}_lo")
                            L.did(PE, proj_T(bk, w, mp, c2), f"proj{f}_{c2}")
                            evac(k, bk, c2)

                    def copy_to(dst, f, last, lag, of):
                        def evac(k, bk, c2):
                            L.need(ACTE, f"proj{f}_{c2}")
                            L.need(ACTE, *last, lag=lag, of=of)
                            L.did(ACTE, ACTE.activation(chunk2(dst, c2), as2(bk), ACT.Copy), f"ev{k}")
                        return evac

                    mix(2, ("xi_lo", "w1mm"))
                    yield
                    L.need(ACTE, "st_v", "vx1", lag=1)
                    proj(2, wv, copy_to(vT, 2, ("st_v",), 1, None))
                    yield
                    L.need(SP, f"ev{n[0] - 1}")
                    L.moved(SP.dma_start(d["vT"][bass.ds(b.times(D), D), :].rearrange("(c p) t -> p c t", p=P), vT[:, :, :]), "st_v")
                    for t in range(NT):
                        last = f"ev{n[0] - 1}" if t == 0 else None
                        k, bk = bank()
                        if last:
                            L.need(PE, last)
                        for c in range(KC):
                            ins = PE.transpose(bk[:, c * P:(c + 1) * P], vT[:, c, t * P:(t + 1) * P], ident[:, :])
                        L.did(PE, ins, f"vx{t}")
                        L.need(ACTE, f"vx{t}")
                        L.need(ACTE, "cv", lag=2, of="Cb")
                        L.did(ACTE, ACTE.activation(vtok[par][:, t, :], bk[:, :], ACT.Copy), f"ev{k}")
                    yield
                    mix(1, ("mix2_lo", "proj2_1"))
                    yield
                    k, bk = bank()
                    L.need(PE, "mix1_lo")
                    L.did(PE, product(bk[0:DD, 0:T], [(parts(td1, slice(None), q, slice(None)), parts(mp, slice(None), q, slice(None)))
                                                      for q in range(KC)]), "proj1_1")
                    L.need(ACTE, "proj1_1", "tx_lo", "w2mm1_1", "w2mm2_1")
                    L.need(ACTE, "td2mm", "td_lo", lag=1)
                    L.did(ACTE, ACTE.activation(th[0:DD, 0, :], bk[0:DD, 0:T], ACT.Tanh), f"ev{k}")
                    L.need(ACTE, f"ev{k}")
                    L.did(ACTE, ACTE.activation(tdp[0][:, :], th[0:DD, 0, :], ACT.Copy), "td_hi")
                    L.need(POOL, "td_hi")
                    L.did(POOL, POOL.tensor_tensor(tdp[1][:, :], th[0:DD, 0, :], tdp[0][:, :].bitcast(F32), ALU.subtract), "td_lo")
                    for c2 in range(2):
                        k, bk = bank()
                        L.need(PE, "td_lo")
                        for c in range(2):
                            m = 2 * c2 + c
                            ins = product(bk[:, c * T:(c + 1) * T], [(parts(td2, slice(None), 0, slice(m * P, (m + 1) * P)), parts(tdp))])
                        L.did(PE, ins, "td2mm")
                        L.need(ACTE, "td2mm")
                        L.need(ACTE, f"scan{UN - 1}", lag=2, of="Cb")
                        for c in range(2):
                            m = 2 * c2 + c
                            L.did(ACTE, ACTE.activation(wT[par][:, m, :], bk[:, c * T:(c + 1) * T], ACT.Exp,
                                                        bias=decay[:, m:m + 1]), f"ev{k}")
                    L.need(ACTE, f"ev{k}")
                    L.did(ACTE, ACTE.activation(wT[par][:, :, :], wT[par][:, :, :], ACT.Exp, scale=-1.0), "w")
                    yield
                    mix(0, ("mix1_lo", "proj1_1"))
                    yield
                    proj(0, wk, copy_to(kT[par], 0, (f"a{UN - 1}",), 2, "Cb"))
                    kdone = f"ev{n[0] - 1}"
                    yield
                    mix(3, ("mix0_lo", "proj0_1"))
                    yield
                    proj(3, wr, copy_to(rT[par], 3, (f"m{UN - 1}", f"m{UN - 2}"), 2, "Cb"))
                    rdone = f"ev{n[0] - 1}"
                    yield
                    L.need(DVE, kdone, rdone, "xposed1")
                    for m in range(KC):
                        L.did(DVE, DVE.scalar_tensor_tensor(ruk[:, m, :], rT[par][:, m, :], u[:, m:m + 1], kT[par][:, m, :],
                                                            ALU.mult, ALU.mult), "ruk")
                    mix(4, ("mix3_lo", "proj3_1"))
                    yield

                    def gate(k, bk, c2):
                        L.need(ACTE, f"proj4_{c2}", "td_lo")
                        if c2:
                            L.need(ACTE, f"ev{k - 1}")
                        else:
                            L.need(ACTE, "gate_done", lag=1)
                        L.did(ACTE, ACTE.activation(th[:, :, :], as2(bk), ACT.Tanh, scale=0.5), f"th{c2}")
                        L.need(DVE, f"th{c2}")
                        L.need(DVE, "z", lag=2, of="Cb")
                        L.did(DVE, DVE.scalar_tensor_tensor(chunk2(gT[par], c2), th[:, :, :], 1.0, as2(bk), ALU.add, ALU.mult), f"ev{k}")
                        if c2:
                            S_ = L.s.found
                            S_[(L.name, "gate_done")] = S_[(L.name, f"ev{k}")]

                    L.need(ACTE, "gate_done", lag=1)
                    proj(4, wg, gate)
                    yield
                    k, bk = bank()
                    L.need(PE, "ruk")
                    for t in range(NT):
                        for g in range(KC):
                            ins = PE.matmul(bk[:, t * RH + g * GH:t * RH + (g + 1) * GH], ruk[:, g, t * P:(t + 1) * P],
                                            headsum[:, :], start=True, stop=True)
                    L.did(PE, ins, "cmm")
                    L.need(DVE, "cmm")
                    L.need(DVE, "cv", lag=2, of="Cb")
                    L.did(DVE, DVE.tensor_copy(ctok[par][:, :, :].rearrange("p t h -> p (t h)"), bk[:, 0:NT * RH]), f"ev{k}")
                    assert n[0] == NF - 1
                    L.s.found[(L.name, f"ev{NF - 1}")] = L.s.found[(L.name, f"ev{NF - 5}")]
                    yield

                def back(L):
                    b, par = L.b, L.par
                    w, k, r, s = wT[par], kT[par], rT[par], s0[par]
                    vsrc = d["vT"]

                    def load(n):
                        g, q = n // (RS // JH), n % (RS // JH)
                        L.need(SP, "st_v", of="Cf")
                        L.ring(SP, "red", n, NV, UN)
                        src = vsrc[bass.ds(b.times(D, g * P), P), :].rearrange("(h j) t -> h j t", j=RS)[:, q * JH:(q + 1) * JH, :]
                        L.slot(SP.dma_start(Vb[n % NV][:, :, :].rearrange("p j t -> p (j t)"),
                                             src.rearrange("h j t -> h (j t)")[:, None, :].broadcast_to([GH, RS, JH * T])), f"ld_v{n}", f"v_slot{n % NV}")

                    for n in range(2):
                        load(n)
                    for n in range(UN):
                        if n + 2 < UN:
                            load(n + 2)
                        g, q = n // (RS // JH), n % (RS // JH)
                        v, sc = Vb[n % NV], Sx[n % NX]
                        L.need(DVE, f"ld_v{n}")
                        L.need(DVE, "w", kdone_name, of="Cf")
                        L.did(DVE, DVE.tensor_tensor(v[:, :, :], v[:, :, :], k[:, g:g + 1, :].broadcast_to([P, JH, T]), ALU.mult), f"a{n}")
                        L.need(ACTE, "ld_s0", of="Cf")
                        L.ring(ACTE, "m", n, NX, UN)
                        L.did(ACTE, ACTE.activation(sc[:, :, 0:1], s[:, g, q * JH:(q + 1) * JH, None], ACT.Copy), f"s0_{n}")
                        L.need(DVE, "ld_s0", of="Cf")
                        L.need(DVE, f"a{n}")
                        L.ring(DVE, "m", n, NX, UN)
                        for j in range(JH):
                            L.did(DVE, DVE.tensor_tensor_scan(sc[:, j, 1:T], w[:, g, 0:T - 1], v[:, j, 0:T - 1],
                                                              s[:, g, q * JH + j:q * JH + j + 1], ALU.mult, ALU.add), f"scan{n}")
                        e = POOL if q == 3 else DVE
                        L.need(e, f"scan{n}", f"s0_{n}")
                        L.need(e, rdone_name, of="Cf")
                        L.did(e, e.tensor_tensor(v[:, :, :], sc[:, :, :], r[:, g:g + 1, :].broadcast_to([P, JH, T]), ALU.mult), f"m{n}")
                        L.need(PE, f"m{n}")
                        if n == 0:
                            L.need(PE, "og1", lag=1)
                        for t in range(NT):
                            for j in range(JH):
                                out = YB[t][:, g * P:(g + 1) * P].rearrange("p (h j) -> p h j", j=RS)[:, :, q * JH + j]
                                ins = PE.matmul(out, v[:, j, t * P:(t + 1) * P], headsum[:, :], start=True, stop=True)
                        L.did(PE, ins, f"red{n}")
                        yield
                    heads = lambda ap: ap.rearrange("p (h j) -> p h j", j=RS)
                    L.need(POOL, cdone_name, vdone_name, of="Cf")
                    L.need(POOL, "zx1", lag=1)
                    L.did(POOL, POOL.tensor_tensor(og[:, :, :], heads(vtok[par][:, :, :].rearrange("p t d -> p (t d)")),
                                                   ctok[par][:, :, :].rearrange("p t h -> p (t h)")[:, :, None]
                                                   .broadcast_to([P, NT * RH, RS]), ALU.mult), "cv")
                    L.need(DVE, "cv", f"red{UN - 1}")
                    for t in range(NT):
                        o = og[:, t * RH:(t + 1) * RH, :]
                        L.did(DVE, DVE.tensor_tensor(o, heads(YB[t][:, :]), o, ALU.add), f"og{t}")
                    L.need(DVE, "og1")
                    L.need(DVE, "centred", lag=1)
                    L.did(DVE, DVE.reduce_sum(s1[:, :], og[:, :, :], AX.X), "sum")
                    L.need(DVE, "sum")
                    L.did(DVE, DVE.tensor_scalar(s1[:, :], s1[:, :], 1.0 / RS, None, ALU.mult), "mean")
                    L.need(POOL, "mean")
                    L.did(POOL, POOL.tensor_tensor(og[:, :, :], og[:, :, :], s1[:, :, None].broadcast_to([P, NT * RH, RS]),
                                                   ALU.subtract), "centred")
                    yield
                    L.need(ACTE, "centred")
                    L.need(ACTE, "sumsq", lag=1)
                    L.did(ACTE, ACTE.activation(sq[:, :, :], og[:, :, :], ACT.Square), "sq")
                    L.need(DVE, "sq")
                    L.need(DVE, "normed", lag=1)
                    L.did(DVE, DVE.reduce_sum(s2[:, :], sq[:, :, :], AX.X), "sumsq")
                    L.need(DVE, "sumsq")
                    L.did(DVE, DVE.tensor_scalar(s2[:, :], s2[:, :], 1.0 / RS, EPS, ALU.mult, ALU.add), "var")
                    L.need(POOL, "var")
                    L.did(POOL, POOL.tensor_tensor(s2[:, :], s2[:, :], mhalf[:, :], ALU.pow), "rstd")
                    L.need(POOL, "rstd")
                    L.did(POOL, POOL.tensor_tensor(og[:, :, :], og[:, :, :], s2[:, :, None].broadcast_to([P, NT * RH, RS]),
                                                   ALU.mult), "normed")
                    yield
                    flat = og[:, :, :].rearrange("p (t h) j -> p t (h j)", t=NT)
                    for c2 in range(2):
                        L.need(PE, "normed")
                        L.need(PE, f"zev{c2}", lag=1)
                        xpose(L, flat, ZB[c2], c2, f"zx{c2}")
                        L.need(ACTE, f"zx{c2}")
                        L.need(ACTE, "st", lag=1)
                        for c in range(2):
                            m = 2 * c2 + c
                            L.did(ACTE, ACTE.activation(zT[:, m, :], ZB[c2][:, c * T:(c + 1) * T], ACT.Identity,
                                                        scale=gn_w[:, m:m + 1], bias=gn_b[:, m:m + 1]), f"zev{c2}")
                    L.need(POOL, "zev1")
                    L.need(POOL, gdone_name, of="Cf")
                    L.did(POOL, POOL.tensor_tensor(zT[:, :, :], zT[:, :, :], gT[par][:, :, :], ALU.mult), "z")
                    L.need(POOL, "z")
                    L.moved(POOL.dma_start(z_out[bass.ds(b.times(D), D), :].rearrange("(c p) t -> p c t", p=P), zT[:, :, :]), "st")
                    yield

                tdp = pair(ctx, "C_tdp", [DD, T])
                vdone_name, kdone_name, rdone_name, gdone_name, cdone_name = "ev8", "ev15", "ev19", "ev25", "ev26"
                vdone_name, kdone_name, rdone_name, gdone_name, cdone_name = EVN
                pipeline(nc, steps, ["Cf", "Cb"], [front, back])
                finish("C", ["Cb"])

        def channel_mix(x_in, z_in, x_out):
            ctx = ExitStack()
            with ctx:
                S = Lane(steps, "Dsetup", Batch(0, 0))
                ln_w, ln_b, fk, fr = [columns(ctx, S, "L2_xattn_" + n) for n in ("ln2_w", "ln2_b", "ffn_maa_k", "ffn_maa_r")]
                wo, wfk, wfr, wfv = load_weights(ctx, S, [(n, d[f"L2_{n}T"]) for n in ("Wo", "Wfk", "Wfr", "Wfv")])
                setup_done(S, PE, DVE, ACTE, POOL, SP)
                zT = tile(ctx, "D_zT", [P, KC, T])
                zTp = pair(ctx, "D_zTp", [P, KC, T])
                x = tile(ctx, "D_x", [P, NT, D])
                x1 = both(ctx, tile, "D_x1", [P, NT, D])
                xr = both(ctx, tile, "D_xr", [P, NT, D])
                nst = norm_tiles(ctx, "D")
                xn = tile(ctx, "D_xn", [P, NT, D])
                xcT = both(ctx, tile, "D_xcT", [P, KC, T + 1])
                sx = tile(ctx, "D_sx", [P, KC, T])
                mk, mr = both(ctx, tile, "D_mix", [P, KC, T])
                mkp, mrp = both(ctx, pair, "D_mixp", [P, KC, T])
                kr = tile(ctx, "D_kr", [P, KC, T])
                kkp = both(ctx, pair, "D_kkp", [P, KC, T])
                rt = both(ctx, tile, "D_rt", [P, NT, D])
                y = tile(ctx, "D_y", [P, NT, D])

                def first(L):
                    b, par = L.b, L.par
                    L.need(SP, "z_lo", lag=1)
                    L.moved(SP.dma_start(zT[:, :, :], z_in[bass.ds(b.times(D), D), :].rearrange("(c p) t -> p c t", p=P)), "ld_z")
                    L.need(SP, "x1_1", lag=1)
                    L.moved(SP.dma_start(x[:, :, :], tokens(x_in, b)), "ld_x")
                    L.need(SP, "mr", lag=2, of="D1")
                    load_column0(L, xcT[par], 0, "ld_prev")
                    L.need(ACTE, "ld_z")
                    L.need(ACTE, "o1", lag=1)
                    split(L, zT[:, :, :], zTp, "z")
                    yield
                    for t in range(NT):
                        L.need(PE, "z_lo")
                        L.need(PE, f"x1_{t}", lag=1)
                        L.did(PE, proj_N(banks[t], wo, zTp, t), f"o{t}")
                        L.need(DVE, f"o{t}", "ld_x")
                        L.need(DVE, "xr", lag=2, of="D1")
                        L.did(DVE, DVE.tensor_tensor(x1[par][:, t, :], banks[t][:, :], x[:, t, :], ALU.add), f"x1_{t}")
                        yield
                    norm(L, x1[par], xn, nst, "x1_1")
                    yield
                    for c2 in range(2):
                        L.need(PE, "norm1")
                        L.need(PE, f"xc{c2}", lag=1)
                        xpose(L, xn, banks[2 + c2], c2, f"xposed{c2}")
                        L.need(ACTE, f"xposed{c2}")
                        L.need(ACTE, "mr", lag=2, of="D1")
                        for c in range(2):
                            m = 2 * c2 + c
                            L.did(ACTE, ACTE.activation(xcT[par][:, m, 1:T + 1], banks[2 + c2][:, c * T:(c + 1) * T],
                                                        ACT.Identity, scale=ln_w[:, m:m + 1], bias=ln_b[:, m:m + 1]), f"xc{c2}")
                        yield

                def second(L):
                    par = L.par
                    xc = xcT[par]
                    L.need(POOL, "x1_1", of="D0")
                    L.need(POOL, "out1", lag=2, of="D2")
                    L.did(POOL, POOL.tensor_copy(xr[par][:, :, :], x1[par][:, :, :]), "xr")
                    L.need(DVE, "xc1", "ld_prev", of="D0")
                    L.did(DVE, DVE.tensor_tensor(sx[:, :, :], xc[:, :, 0:T], xc[:, :, 1:T + 1], ALU.subtract), "sx")
                    L.need(DVE, "sx")
                    L.need(DVE, "mk_lo", lag=1)
                    mix_T(L, mk, xc, sx, fk, "mk")
                    L.need(DVE, "mr_lo", lag=1)
                    mix_T(L, mr, xc, sx, fr, "mr")
                    L.need(ACTE, "mk")
                    L.need(ACTE, "k1", lag=1)
                    split(L, mk[:, :, :], mkp, "mk")
                    L.need(ACTE, "mr")
                    L.need(ACTE, "r1", lag=1)
                    split(L, mr[:, :, :], mrp, "mr")
                    yield
                    for c2 in range(2):
                        L.need(PE, "mk_lo")
                        L.need(PE, f"rt{c2}", lag=1)
                        L.did(PE, proj_T(banks[4 + c2], wfk, mkp, c2), f"k{c2}")
                        L.need(ACTE, f"k{c2}")
                        L.need(ACTE, "kk_lo", lag=1)
                        L.did(ACTE, ACTE.activation(chunk2(kr, c2), as2(banks[4 + c2]), ACT.Relu), f"kr{c2}")
                        yield
                    L.need(POOL, "kr1")
                    L.did(POOL, POOL.tensor_tensor(kr[:, :, :], kr[:, :, :], kr[:, :, :], ALU.mult), "kk")
                    L.need(ACTE, "kk")
                    L.need(ACTE, "v1", lag=2, of="D2")
                    split(L, kr[:, :, :], kkp[par], "kk")
                    for t in range(NT):
                        L.need(PE, "mr_lo", f"kr{t}")
                        L.did(PE, proj_N(banks[4 + t], wfr, mrp, t), f"r{t}")
                        L.need(ACTE, f"r{t}")
                        L.need(ACTE, "gated1", lag=2, of="D2")
                        L.did(ACTE, ACTE.activation(rt[par][:, t, :], banks[4 + t][:, :], ACT.Tanh, scale=0.5), f"rt{t}")
                        yield

                def third(L):
                    par = L.par
                    for t in range(NT):
                        L.need(PE, "kk_lo", of="D1")
                        L.need(PE, f"gated{t}", lag=1)
                        L.did(PE, proj_N(banks[6 + t], wfv, kkp[par], t), f"v{t}")
                        L.need(DVE, f"v{t}")
                        L.need(DVE, f"rt{t}", "xr", of="D1")
                        L.need(DVE, "st", lag=1)
                        L.did(DVE, DVE.scalar_tensor_tensor(y[:, t, :], rt[par][:, t, :], 1.0, banks[6 + t][:, :],
                                                            ALU.add, ALU.mult), f"gated{t}")
                        L.need(DVE, f"gated{t}")
                        L.did(DVE, DVE.scalar_tensor_tensor(y[:, t, :], y[:, t, :], 0.5, xr[par][:, t, :],
                                                            ALU.mult, ALU.add), f"out{t}")
                        yield
                    L.need(POOL, "out1")
                    L.moved(POOL.dma_start(tokens(x_out, L.b), y[:, :, :]), "st")

                pipeline(nc, steps, ["D0", "D1", "D2"], [first, second, third])
                finish("D", ["D2"])

        def mlp(x_in, x_out):
            ctx = ExitStack()
            with ctx:
                S = Lane(steps, "Fsetup", Batch(0, 0))
                ln_w, ln_b, fcb = [columns(ctx, S, "L3_xattn_" + n) for n in ("ln2_w", "ln2_b", "fc_b")]
                pb = rows(ctx, S, "L3_xattn_proj_b")
                fc, pj = d["L3_xattn_fc_w"], d["L3_xattn_proj_w"]
                ws = load_weights(ctx, S, [(f"fc{i}", fc[:, i * D:(i + 1) * D]) for i in range(4)]
                                  + [(f"pj{i}", pj[i * D:(i + 1) * D, :]) for i in range(4)])
                setup_done(S, PE, DVE, ACTE, POOL, SP)
                x = both(ctx, tile, "F_x", [P, NT, D])
                nst = norm_tiles(ctx, "F")
                xn = tile(ctx, "F_xn", [P, NT, D])
                aT = tile(ctx, "F_aT", [P, KC, T])
                aTp = both(ctx, pair, "F_aTp", [P, KC, T])
                NH = 4
                hf = both(ctx, tile, "F_h", [P, 2, T])
                hp = [pair(ctx, f"F_hp{i}", [P, 2, T]) for i in range(NH)]
                y = tile(ctx, "F_y", [P, NT, D])
                NU = NI // 2

                def front(L):
                    b, par = L.b, L.par
                    L.need(SP, "out1", lag=2, of="F1")
                    L.moved(SP.dma_start(x[par][:, :, :], tokens(x_in, b)), "ld_x")
                    norm(L, x[par], xn, nst, "ld_x")
                    L.need(POOL, "norm1")
                    L.did(POOL, POOL.tensor_tensor(x[par][:, :, :], x[par][:, :, :], pb[:, None, :].broadcast_to([P, NT, D]), ALU.add), "x_pb")
                    yield
                    for c2 in range(2):
                        L.need(PE, "norm1")
                        L.need(PE, f"ev{c2}", lag=1)
                        xpose(L, xn, banks[c2], c2, f"xposed{c2}")
                        L.need(ACTE, f"xposed{c2}")
                        L.need(ACTE, "a_lo", lag=1)
                        for c in range(2):
                            m = 2 * c2 + c
                            L.did(ACTE, ACTE.activation(aT[:, m, :], banks[c2][:, c * T:(c + 1) * T], ACT.Identity,
                                                        scale=ln_w[:, m:m + 1], bias=ln_b[:, m:m + 1]), f"ev{c2}")
                        yield
                    L.need(ACTE, "ev1")
                    L.need(ACTE, f"fc{NU - 1}", lag=2, of="F1")
                    split(L, aT[:, :, :], aTp[par], "a")
                    yield

                def back(L):
                    par = L.par

                    def up(n):
                        bk = banks[2 + n % 4]
                        L.need(PE, "a_lo", of="F0")
                        L.ring(PE, "g", n, 4, NU)
                        for c in range(2):
                            m = 2 * n + c
                            w, q = ws[m // 4], m % 4
                            ins = product(bk[:, c * T:(c + 1) * T], [(parts(w, slice(None), k, slice(q * P, (q + 1) * P)),
                                                                      parts(aTp[par], slice(None), k, slice(None))) for k in range(KC)])
                        L.did(PE, ins, f"fc{n}")
                        L.need(ACTE, f"fc{n}")
                        L.ring(ACTE, "lo", n, 2, NU)
                        for c in range(2):
                            m = 2 * n + c
                            L.did(ACTE, ACTE.activation(hf[n % 2][:, c, :], bk[:, c * T:(c + 1) * T], ACT.Gelu_apprx_tanh,
                                                        bias=fcb[:, m:m + 1]), f"g{n}")
                        L.need(ACTE, f"g{n}")
                        L.ring(ACTE, "pj", n, NH, NU)
                        L.did(ACTE, ACTE.activation(hp[n % NH][0][:, :, :], hf[n % 2][:, :, :], ACT.Copy), f"hi{n}")
                        L.need(DVE, f"hi{n}")
                        L.did(DVE, DVE.tensor_tensor(hp[n % NH][1][:, :, :], hf[n % 2][:, :, :],
                                                     hp[n % NH][0][:, :, :].bitcast(F32), ALU.subtract), f"lo{n}")

                    def down(n):
                        L.need(PE, f"lo{n}")
                        if n == 0:
                            L.need(PE, "out1", lag=1)
                        for t in range(NT):
                            w = ws[4 + n // 2]
                            ins = product(banks[6 + t][:, :],
                                          [(parts(hp[n % NH], slice(None), c, slice(t * P, (t + 1) * P)),
                                            parts(w, slice(None), (2 * n + c) % 4, slice(None))) for c in range(2)],
                                          first=n == 0, last=n == NU - 1)
                        L.did(PE, ins, f"pj{n}")

                    for n in range(NU + 2):
                        if n < NU:
                            up(n)
                        if n >= 2:
                            down(n - 2)
                        yield
                    for t in range(NT):
                        L.need(DVE, f"pj{NU - 1}")
                        L.need(DVE, "x_pb", of="F0")
                        L.need(DVE, "st", lag=1)
                        L.did(DVE, DVE.tensor_tensor(y[:, t, :], banks[6 + t][:, :], x[par][:, t, :], ALU.add), f"out{t}")
                    L.need(POOL, "out1")
                    L.moved(POOL.dma_start(tokens(x_out, L.b), y[:, :, :]), "st")
                    yield

                pipeline(nc, steps, ["F0", "F1"], [front, back])
                finish("F", ["F1"])

        at = [d["x"], d["x1"], d["x2"], d["x3"], d["x4"]]
        flow = {"A": lambda i, o: attention("A", i, o, True), "B": wide_attention,
                "CD": lambda i, o: (time_mix(i, d["zT"]), channel_mix(i, d["zT"], o)),
                "E": lambda i, o: attention("E", i, o, False), "F": mlp}
        todo = [k for k in flow if k in PHASES]
        for n, k in enumerate(todo):
            flow[k](at[n], d["out"] if n == len(todo) - 1 else at[n + 1])
    return steps.found


PHASES = ["A", "B", "CD", "E", "F"]
EVN = ("ev8", "ev15", "ev19", "ev25", "ev26")


_NAMES = ["L0_xattn_ln_gamma", "L0_xattn_ln_beta", "L0_xattn_gate", "L1_xattn_w_q", "L1_xattn_w_k", "L1_xattn_w_v",
          "L1_xattn_alpha", "L3_xattn_ln1_w", "L3_xattn_ln1_b", "L3_xattn_q_w", "L3_xattn_q_b", "L3_xattn_k_w",
          "L3_xattn_k_b", "L3_xattn_v_w", "L3_xattn_v_b", "L3_xattn_cproj_w", "L3_xattn_cproj_b",
          "L3_xattn_ln2_w", "L3_xattn_ln2_b", "L3_xattn_fc_w", "L3_xattn_fc_b", "L3_xattn_proj_w", "L3_xattn_proj_b"] \
    + ["L2_xattn_" + n for n in ("ln1_w", "ln1_b", "ln2_w", "ln2_b", "maa_x", "maa_w1", "maa_w2", "maa_stack",
                                 "time_decay", "td_w1", "td_w2", "u", "gn_w", "gn_b", "ffn_maa_k", "ffn_maa_r")]


def layout(i):
    a = {n: np.asarray(i[n]) for n in _NAMES}
    x, c = np.asarray(i["x"]).reshape(B * T, D), np.asarray(i["ctx_2048"]).reshape(B * T, D)
    a.update(x=x, xT=x.T, ctx=c, ctxT=c.T, mask=np.asarray(i["mask_BxS2_bf1"]).view(np.uint8),
             L1_WoT=np.asarray(i["L1_xattn_w_o"]).T)
    for w in ("Wq", "Wk", "Wv", "Wo"):
        a[f"L0_{w}T"] = np.asarray(i[f"L0_xattn_{w}"]).T
    for w in ("Wr", "Wk", "Wv", "Wg", "Wo", "Wfk", "Wfr", "Wfv"):
        a[f"L2_{w}T"] = np.asarray(i[f"L2_xattn_{w}"]).T
    a["L1_xattn_alpha"] = a["L1_xattn_alpha"].reshape(1)
    a["L2_xattn_maa_w2"] = a["L2_xattn_maa_w2"].reshape(NMIX * DM, D)
    a["L2_xattn_maa_stack"] = a["L2_xattn_maa_stack"].reshape(NMIX * D)
    a["L2_xattn_u"] = a["L2_xattn_u"].reshape(D)
    return {n: np.ascontiguousarray(v) for n, v in a.items()}


def build(nc, arrays, seen):
    d = {n: nc.dram_tensor(f"in_{n}", v.shape, mybir.dt.from_np(v.dtype), kind="ExternalInput").ap()
         for n, v in arrays.items()}
    d["out"] = nc.dram_tensor("out_0", (B * T, D), F32, kind="ExternalOutput").ap()
    for n in ("x1", "x2", "x3", "x4"):
        d[n] = nc.dram_tensor(f"act_{n}", (B * T, D), F32, kind="Internal").ap()
    d["zT"] = nc.dram_tensor("act_zT", (B * D, T), F32, kind="Internal").ap()
    d["vT"] = nc.dram_tensor("act_vT", (B * D, T), F32, kind="Internal").ap()
    return program(nc, d, seen)


def kernel(**inputs):
    import concourse.bacc as _bacc
    from concourse.bass_utils import run_bass_kernel_spmd as _run

    arrays = layout(inputs)
    seen = build(_bacc.Bacc("TRN2", target_bir_lowering=False, num_devices=1), arrays, {})
    nc = _bacc.Bacc("TRN2", target_bir_lowering=False, num_devices=1)
    build(nc, arrays, seen)
    r = _run(nc, [{f"in_{n}": v for n, v in arrays.items()}], core_ids=[0])
    return r.results[0]["out_0"].reshape(B, T, D)
```

```python
from contextlib import ExitStack

import numpy as np
import concourse.bass as bass
from concourse import mybir

F32 = mybir.dt.float32
F32R = mybir.dt.float32r
U8 = mybir.dt.uint8
ALU = mybir.AluOpType
ACT = mybir.ActivationFunctionType
AX = mybir.AxisListType

P = 128
B = 16
T = 256
NT = T // P
D = 512
KC = D // P
H = 16
HD = D // H
RH = 32
RS = D // RH
GH = P // RS
DM = 32
NMIX = 5
DD = 64
INNER = 4 * D
NI = INNER // P
EPS = 1e-5
FMAX = 3.4028235e38
JH = 4


class Batch:

    def __init__(self, u, c):
        self.u, self.c = u, c
        self.par = c % 2

    def times(self, n, plus=0):
        return self.u * (2 * n) + (self.c * n + plus)

    def half(self, n, plus=0):
        return self.u * n + ((self.c // 2) * n + plus)

    def back(self, lag):
        return Batch(self.u, self.c - lag)

    def exists(self):
        return not isinstance(self.u, int) or 0 <= 2 * self.u + self.c


class Steps:

    def __init__(self, nc, ctx, seen):
        self.nc, self.ctx, self.seen, self.found, self.sems, self.waited = nc, ctx, seen, {}, {}, {}
        self.names = {id(nc.tensor): "pe", id(nc.vector): "dve", id(nc.scalar): "act",
                      id(nc.gpsimd): "pool", id(nc.sync): "sp"}

    def sem(self, *key):
        if key not in self.sems:
            self.sems[key] = self.ctx.enter_context(self.nc.semaphore("_".join(map(str, key))))
        return self.sems[key]


class Lane:
    def __init__(self, steps, name, b):
        self.s, self.name, self.b, self.par, self.n = steps, name, b, b.par, {}

    def did(self, eng, ins, *names):
        key = (self.name, self.s.names[id(eng)])
        self.n[key] = self.n.get(key, 0) + 1
        ins.then_inc(self.s.sem(*key), 1)
        for step in names:
            self.s.found[(self.name, step)] = (key, self.n[key])

    def moved(self, ins, step):
        key = (self.name, "dma", step)
        self.n[key] = self.n.get(key, 0) + 16
        ins.then_inc(self.s.sem(*key, self.par), 16)
        self.s.found[(self.name, step)] = (key, None)

    def slot(self, ins, step, slot):
        key = (self.name, slot)
        self.n[key] = self.n.get(key, 0) + 16
        ins.then_inc(self.s.sem(*key), 16)
        self.s.found[(self.name, step)] = (key, self.n[key])

    def end(self):
        for key, n in self.n.items():
            self.s.found[key] = n

    def need(self, eng, *steps, lag=0, of=None):
        lane = of or self.name
        for step in steps:
            b = Batch(0, 0) if lane.endswith("setup") else self.b.back(lag)
            if not b.exists():
                continue
            assert b.c >= 0
            key, count = self.s.seen.get((lane, step), ((lane, "pe"), 1))
            per = self.s.seen.get(key, 1)
            if count is None:
                sem, value, const = self.s.sem(*key, b.par), b.half(per, per), (b.c // 2) * per + per
            else:
                sem, value, const = self.s.sem(*key), b.times(per, count), b.c * per + count
            known = (id(eng), sem.name if hasattr(sem, "name") else id(sem))
            if self.s.waited.get(known, -10 ** 9) >= const:
                continue
            self.s.waited[known] = const
            eng.wait_ge(sem, value)
            if eng in (self.s.nc.sync, self.s.nc.gpsimd):
                self.hold(eng)

    def hold(self, eng):
        eng.sem_inc(self.s.sem("held", self.s.names[id(eng)]), 1)

    def ring(self, eng, step, n, depth, total):
        if n >= depth:
            self.need(eng, f"{step}{n - depth}")
        else:
            self.need(eng, f"{step}{n - depth + total}", lag=1)


def pipeline(nc, steps, lanes, stages):
    K = len(stages)
    peel = K + (B - K) % 2

    def turn(u, c):
        steps.waited = {}
        work = []
        for k, stage in enumerate(stages):
            b = Batch(u, c - k)
            if isinstance(u, int) and not 0 <= c - k < B:
                continue
            lane = Lane(steps, lanes[k], b)
            work.append([stage(lane), lane, 0, max(steps.seen.get((lanes[k], "yields"), 1), 1)])
        while work:
            w = min(work, key=lambda w: w[2] / w[3])
            try:
                next(w[0])
                w[2] += 1
            except StopIteration:
                steps.found[(w[1].name, "yields")] = w[2]
                w[1].end()
                work.remove(w)

    for t in range(peel):
        turn(0, t)
    with nc.Fori(0, (B - peel) // 2) as u:
        turn(u, peel)
        turn(u, peel + 1)
    for t in range(B, B + K - 1):
        turn(0, t)


def program(nc, d, seen):
    PE, DVE, ACTE, POOL, SP = nc.tensor, nc.vector, nc.scalar, nc.gpsimd, nc.sync
    top = ExitStack()
    steps = Steps(nc, top, seen)
    with top:
        def tile(ctx, name, shape, dt=F32):
            return ctx.enter_context(nc.sbuf_tensor(name, shape, dt))

        def pair(ctx, name, shape):
            return [tile(ctx, f"{name}_{part}", shape, F32R) for part in ("hi", "lo")]

        def both(ctx, make, name, *a):
            return [make(ctx, f"{name}{i}", *a) for i in range(2)]

        banks = [top.enter_context(nc.psum_tensor(f"bank{i}", [P, 512], F32)) for i in range(8)]
        ident = tile(top, "ident", [P, P])
        headsum = tile(top, "headsum", [P, GH])
        mhalf = tile(top, "mhalf", [P, RH * NT])

        def setup_done(S, *engines):
            S.end()
            for e in engines:
                for step in [k[1] for k in steps.found if k[0] == S.name and isinstance(steps.found[k], tuple)]:
                    S.need(e, step, of=S.name)

        S = Lane(steps, "const_setup", Batch(0, 0))
        S.did(POOL, POOL.memset(ident[:, :], 0.0), "zero")
        S.need(POOL, "zero", of="const_setup")
        S.did(POOL, POOL.affine_select(out=ident[:, :], in_=ident[:, :], compare_op=ALU.not_equal, fill=1.0,
                                       base=0, pattern=[[-1, P]], channel_multiplier=1), "ident")
        S.did(POOL, POOL.memset(mhalf[:, :], -0.5), "mhalf")
        S.did(POOL, POOL.memset(headsum[:, :], 1.0), "ones")
        S.need(POOL, "ones", of="const_setup")
        S.did(POOL, POOL.affine_select(out=headsum[:, :], in_=headsum[:, :], compare_op=ALU.is_ge, fill=0.0,
                                       base=0, pattern=[[-RS, GH]], channel_multiplier=1), "low")
        S.need(POOL, "low", of="const_setup")
        S.did(POOL, POOL.affine_select(out=headsum[:, :], in_=headsum[:, :], compare_op=ALU.is_ge, fill=0.0,
                                       base=RS - 1, pattern=[[RS, GH]], channel_multiplier=-1), "headsum")
        setup_done(S, PE, DVE, POOL)

        def product(out, pairs, first=True, last=True):
            n = len(pairs)
            for i, (lhs, rhs) in enumerate(pairs):
                for j, (x, y) in enumerate(((0, 0), (0, 1), (1, 0))):
                    ins = PE.matmul(out, lhs[x], rhs[y], start=first and i == 0 and j == 0,
                                    stop=last and i == n - 1 and j == 2)
            return ins

        def parts(pr, *idx):
            return [t[idx] for t in pr]

        def load_weights(ctx, S, names):
            out = []
            tmp = ExitStack()
            stage = [tmp.enter_context(nc.sbuf_tensor(f"{S.name}_stage{i}", [P, KC * D], F32, side="right"))
                     for i in range(2)]
            for i, (name, src) in enumerate(names):
                rows, cols = src.shape
                c = rows // min(rows, P)
                w = pair(ctx, f"w_{name}", [min(rows, P), c, cols])
                st = stage[i % 2][0:min(rows, P), 0:c * cols].rearrange("p (c n) -> p c n", c=c)
                if i >= 2:
                    S.need(SP, f"lo{i - 2}", of=S.name)
                S.slot(SP.dma_start(st, src.rearrange("(c p) n -> p c n", p=min(rows, P))), f"load{i}", f"stage{i % 2}")
                S.need(ACTE, f"load{i}", of=S.name)
                S.did(ACTE, ACTE.activation(w[0][:, :, :], st, ACT.Copy), f"hi{i}")
                S.need(DVE, f"hi{i}", f"load{i}", of=S.name)
                S.did(DVE, DVE.tensor_tensor(w[1][:, :, :], st, w[0][:, :, :].bitcast(F32), ALU.subtract), f"lo{i}")
                out.append(w)
            tmp.close()
            return out

        def columns(ctx, S, name, key=None):
            src = d[name]
            n = src.shape[0] // P
            t = tile(ctx, f"c_{name}", [P, n])
            with nc.allow_non_contiguous_dma(reason="a vector of features, once"):
                S.moved(SP.dma_start(t[:, :], src.rearrange("(c p) -> p c", p=P)), "vectors")
            return t

        def rows(ctx, S, name):
            n = d[name].shape[0]
            t = tile(ctx, f"r_{name}", [P, n])
            S.moved(SP.dma_start(t[:, :], d[name].rearrange("(a n) -> a n", a=1).broadcast_to([P, n])), "vectors")
            return t

        def norm(L, x, xn, st, src):
            stats, agg, rstd = st
            L.need(DVE, src)
            L.need(DVE, "pow", "norm1", lag=1)
            for t in range(NT):
                L.did(DVE, DVE.bn_stats(stats[:, t, :], x[:, t, :]), f"bn{t}")
                L.need(DVE, f"bn{t}")
                L.hold(DVE)
                L.did(DVE, DVE.bn_aggr(agg[:, t, :], stats[:, t, :]), f"agg{t}")
            L.need(POOL, "agg1")
            L.need(POOL, "norm1", lag=1)
            L.did(POOL, POOL.tensor_scalar(rstd[:, :], agg[:, :, 1], EPS, None, ALU.add), "vareps")
            L.need(POOL, "vareps")
            L.did(POOL, POOL.tensor_tensor(rstd[:, :], rstd[:, :], mhalf[:, 0:NT], ALU.pow), "pow")
            L.need(DVE, "pow")
            L.need(DVE, "xposed1", lag=1)
            for t in range(NT):
                L.did(DVE, DVE.tensor_scalar(xn[:, t, :], x[:, t, :], agg[:, t, 0:1], rstd[:, t:t + 1],
                                             ALU.subtract, ALU.mult), f"norm{t}")

        def norm_tiles(ctx, name):
            return (tile(ctx, f"{name}_stats", [P, NT, 6]), tile(ctx, f"{name}_agg", [P, NT, 2]),
                    tile(ctx, f"{name}_rstd", [P, NT]))

        def xpose(L, x, bank, c2, name):
            for c in range(2):
                for t in range(NT):
                    ins = PE.transpose(bank[:, c * T + t * P:c * T + (t + 1) * P],
                                       x[:, t, (2 * c2 + c) * P:(2 * c2 + c + 1) * P], ident[:, :])
            L.did(PE, ins, name)

        def split(L, full, pr, name, free=None):
            if free:
                L.need(ACTE, free, lag=1)
            L.did(ACTE, ACTE.activation(pr[0][:], full, ACT.Copy), f"{name}_hi")
            L.need(POOL, f"{name}_hi")
            L.did(POOL, POOL.tensor_tensor(pr[1][:], full, pr[0][:].bitcast(F32), ALU.subtract), f"{name}_lo")

        def chunk2(t, c2):
            return t[:, 2 * c2:2 * c2 + 2, :]

        def as2(bank, n=T):
            return bank[:, 0:2 * n].rearrange("p (c t) -> p c t", c=2)

        def proj_T(bank, w, xT, c2):
            for c in range(2):
                m = 2 * c2 + c
                ins = product(bank[:, c * T:(c + 1) * T],
                              [(parts(w, slice(None), k, slice(m * P, (m + 1) * P)), parts(xT, slice(None), k, slice(None)))
                               for k in range(KC)])
            return ins

        def proj_N(bank, w, xT, t, k0=0, kn=KC, **kw):
            return product(bank[:, :],
                           [(parts(xT, slice(None), k, slice(t * P, (t + 1) * P)), parts(w, slice(None), k, slice(None)))
                            for k in range(k0, k0 + kn)], **kw)

        def attention(ph, x_in, x_out, first):
            ctx = ExitStack()
            with ctx:
                S = Lane(steps, f"{ph}setup", Batch(0, 0))
                F, Bk = f"{ph}f", f"{ph}b"
                if first:
                    gamma, beta = columns(ctx, S, "L0_xattn_ln_gamma"), columns(ctx, S, "L0_xattn_ln_beta")
                    gate = tile(ctx, "gate", [P, 1])
                    S.moved(SP.dma_start(gate[:, :], d["L0_xattn_gate"].rearrange("(a n) -> a n", a=1).broadcast_to([P, 1])), "vectors")
                    ws = ["L0_WqT", "L0_WkT", "L0_WvT", "L0_WoT"]
                else:
                    gamma, beta = columns(ctx, S, "L3_xattn_ln1_w"), columns(ctx, S, "L3_xattn_ln1_b")
                    qb, kb = columns(ctx, S, "L3_xattn_q_b"), columns(ctx, S, "L3_xattn_k_b")
                    vb, cb = rows(ctx, S, "L3_xattn_v_b"), rows(ctx, S, "L3_xattn_cproj_b")
                    ws = ["L3_xattn_q_w", "L3_xattn_k_w", "L3_xattn_v_w", "L3_xattn_cproj_w"]
                wq, wk, wv, wo = load_weights(ctx, S, [(w, d[w]) for w in ws])
                scale = float(HD) ** -0.5
                if first:
                    tg = tile(ctx, "tanh_gate", [P, 1])
                    S.need(ACTE, "vectors", of=S.name)
                    S.did(ACTE, ACTE.activation(tg[:, :], gate[:, :], ACT.Tanh), "tanh_gate")
                else:
                    nqb = tile(ctx, "neg_scaled_qb", [P, KC])
                    S.need(DVE, "vectors", of=S.name)
                    S.did(DVE, DVE.tensor_scalar(nqb[:, :], qb[:, :], -scale, None, ALU.mult), "nqb")
                setup_done(S, PE, DVE, ACTE, POOL, SP)

                x = both(ctx, tile, f"{ph}_x", [P, NT, D])
                raw = tile(ctx, f"{ph}_ctx", [P, NT, D]) if first else None
                other = tile(ctx, f"{ph}_oT", [P, KC, T])
                otherp = pair(ctx, f"{ph}_oTp", [P, KC, T])
                nst = norm_tiles(ctx, ph)
                xn = tile(ctx, f"{ph}_xn", [P, NT, D])
                aT = tile(ctx, f"{ph}_aT", [P, KC, T])
                aTp = pair(ctx, f"{ph}_aTp", [P, KC, T])
                QT = both(ctx, tile, f"{ph}_QT", [P, KC, T])
                KT = both(ctx, tile, f"{ph}_KT", [P, KC, T])
                V = both(ctx, tile, f"{ph}_V", [P, NT, D])
                m8 = both(ctx, tile, f"{ph}_m8", [P, T], U8)
                mb = both(ctx, tile, f"{ph}_mb", [P, T])
                NS = 4
                sm = [tile(ctx, f"{ph}_s{i}", [P, NT, T]) for i in range(NS)]
                smin = tile(ctx, f"{ph}_smin", [P, NT, H])
                ssum = tile(ctx, f"{ph}_ssum", [P, NT, H])
                rsum = tile(ctx, f"{ph}_rsum", [P, NT, H])
                pT = both(ctx, tile, f"{ph}_pT", [P, NT, T])
                on = tile(ctx, f"{ph}_on", [P, NT, D])
                oTp = pair(ctx, f"{ph}_attT", [P, KC, T])
                y = tile(ctx, f"{ph}_y", [P, NT, D])

                fb = banks[0:2]
                NF = 8

                def front(L):
                    b = L.b
                    L.need(SP, "out1", lag=2, of=Bk)
                    tok = lambda n: n.rearrange("(t p) f -> p t f", p=P)
                    L.moved(SP.dma_start(x[L.par][:, :, :], tok(x_in[bass.ds(b.times(T), T), :])), "ld_x")
                    if first:
                        L.need(SP, "norm1", lag=1)
                        L.moved(SP.dma_start(raw[:, :, :], tok(d["ctx"][bass.ds(b.times(T), T), :])), "ld_raw")
                    L.need(SP, "o_lo", lag=1)
                    L.moved(SP.dma_start(other[:, :, :], d["xT" if first else "ctxT"][:, bass.ds(b.times(T), T)]
                                         .rearrange("(c p) t -> p c t", p=P)), "ld_other")
                    L.need(SP, "mask1", lag=2)
                    L.moved(SP.dma_start(m8[L.par][:, :], d["mask"][bass.ds(b.times(1), 1), :].broadcast_to([P, T])), "ld_mask")
                    yield
                    L.need(DVE, "ld_mask")
                    L.need(DVE, f"min{H - 1}_1", lag=2, of=Bk)
                    big = 3e38 if first else FMAX
                    L.did(DVE, DVE.tensor_scalar(mb[L.par][:, :], m8[L.par][:, :], 1.0, -big, ALU.subtract, ALU.mult), "mask0")
                    L.need(DVE, "mask0")
                    L.did(DVE, DVE.tensor_scalar(mb[L.par][:, :], mb[L.par][:, :], 10.0 if first else 1.0, None, ALU.mult), "mask1")
                    L.need(ACTE, "ld_other")
                    L.need(ACTE, "mm5" if not first else "mm3", "mm7", lag=1)
                    split(L, other[:, :, :], otherp, "o")
                    norm(L, raw if first else x[L.par], xn, nst, "ld_raw" if first else "ld_x")
                    yield
                    for c2 in range(2):
                        L.need(PE, "norm1")
                        L.ring(PE, "ev", c2, 2, NF)
                        xpose(L, xn, fb[c2], c2, f"xposed{c2}")
                        L.need(ACTE, f"xposed{c2}")
                        L.need(ACTE, "a_lo", lag=1)
                        for c in range(2):
                            k = 2 * c2 + c
                            L.did(ACTE, ACTE.activation(aT[:, k, :], fb[c2][:, c * T:(c + 1) * T], ACT.Identity,
                                                        scale=gamma[:, k:k + 1], bias=beta[:, k:k + 1]), f"ev{c2}")
                        yield
                    L.need(ACTE, "ev1")
                    L.need(ACTE, "mm7", "mm3", lag=1)
                    split(L, aT[:, :, :], aTp, "a")
                    xTq, kvT = (otherp, aTp) if first else (aTp, otherp)
                    qs, kvs = ("o", "a") if first else ("a", "o")
                    for i in range(2):
                        L.need(PE, f"{qs}_lo")
                        L.ring(PE, "ev", 2 + i, 2, NF)
                        L.did(PE, proj_T(fb[i], wq, xTq, i), f"mm{2 + i}")
                        L.need(ACTE, f"mm{2 + i}")
                        L.need(ACTE, f"qk{H - 1}", lag=2, of=Bk)
                        if first:
                            L.did(ACTE, ACTE.activation(chunk2(QT[L.par], i), as2(fb[i]), ACT.Copy, scale=-scale), f"ev{2 + i}")
                        else:
                            for c in range(2):
                                k = 2 * i + c
                                L.did(ACTE, ACTE.activation(QT[L.par][:, k, :], fb[i][:, c * T:(c + 1) * T], ACT.Identity,
                                                            scale=-scale, bias=nqb[:, k:k + 1]), f"ev{2 + i}")
                        yield
                    for i in range(2):
                        L.need(PE, f"{kvs}_lo")
                        L.ring(PE, "ev", 4 + i, 2, NF)
                        L.did(PE, proj_T(fb[i], wk, kvT, i), f"mm{4 + i}")
                        L.need(ACTE, f"mm{4 + i}")
                        L.need(ACTE, f"qk{H - 1}", lag=2, of=Bk)
                        if first:
                            L.did(ACTE, ACTE.activation(chunk2(KT[L.par], i), as2(fb[i]), ACT.Copy), f"ev{4 + i}")
                        else:
                            for c in range(2):
                                k = 2 * i + c
                                L.did(ACTE, ACTE.activation(KT[L.par][:, k, :], fb[i][:, c * T:(c + 1) * T], ACT.Identity,
                                                            bias=kb[:, k:k + 1]), f"ev{4 + i}")
                        yield
                    for t in range(NT):
                        L.ring(PE, "ev", 6 + t, 2, NF)
                        L.did(PE, proj_N(fb[t], wv, kvT, t), f"mm{6 + t}")
                        L.need(DVE, f"mm{6 + t}")
                        L.need(DVE, f"av{H - 1}", lag=2, of=Bk)
                        if first:
                            L.did(DVE, DVE.tensor_copy(V[L.par][:, t, :], fb[t][:, :]), f"ev{6 + t}")
                        else:
                            L.did(DVE, DVE.tensor_tensor(V[L.par][:, t, :], fb[t][:, :], vb[:, :], ALU.add), f"ev{6 + t}")
                        yield
                    if not first:
                        L.need(POOL, "norm1")
                        L.did(POOL, POOL.tensor_tensor(x[L.par][:, :, :], x[L.par][:, :, :],
                                                       cb[:, None, :].broadcast_to([P, NT, D]), ALU.add), "x_cb")

                sb, tb, ob = banks[2:4], banks[4:6], banks[6:8]

                def back(L):
                    q, k, v = QT[L.par], KT[L.par], V[L.par]
                    L.need(DVE, "ld_x", of=F)

                    def scores(h):
                        r, c = slice(HD * (h % 4), HD * (h % 4) + HD), h // 4
                        L.need(PE, "ev3", "ev5", of=F)
                        if h >= 2:
                            L.need(PE, f"min{h - 2}_1")
                        else:
                            L.need(PE, f"oT_lo{h}", lag=1)
                        for t in range(NT):
                            ins = PE.matmul(sb[h % 2][:, t * T:(t + 1) * T], q[r, c, t * P:(t + 1) * P], k[r, c, :],
                                            start=True, stop=True)
                        L.did(PE, ins, f"qk{h}")
                        L.need(DVE, f"qk{h}")
                        L.need(DVE, "mask1", of=F)
                        L.ring(DVE, "tr", h, NS, H)
                        if h == 0:
                            L.need(DVE, f"exp{H - 1}_1", lag=1)
                        L.hold(DVE)
                        for t in range(NT):
                            L.did(DVE, DVE.tensor_tensor_reduce(
                                out=sm[h % NS][:, t, :], in0=sb[h % 2][:, t * T:(t + 1) * T], in1=mb[L.par][:, :], scale=1.0,
                                scalar=FMAX, op0=ALU.add, op1=ALU.min, accum_out=smin[:, t, h:h + 1]), f"min{h}_{t}")
                        if h == 0:
                            L.need(ACTE, "rsum", lag=1)
                        for t in range(NT):
                            L.need(ACTE, f"min{h}_{t}")
                            L.did(ACTE, ACTE.activation(sm[h % NS][:, t, :], sm[h % NS][:, t, :], ACT.Exp, scale=-1.0,
                                                        bias=smin[:, t, h:h + 1], accum_out=ssum[:, t, h:h + 1]), f"exp{h}_{t}")

                    def transpose_p(h):
                        L.need(PE, f"exp{h}_1")
                        if h >= 2:
                            L.need(PE, f"pT{h - 2}")
                        else:
                            L.need(PE, f"out{h}", lag=1)
                        for kt in range(NT):
                            for t in range(NT):
                                ins = PE.transpose(tb[h % 2][:, kt * T + t * P:kt * T + (t + 1) * P],
                                                   sm[h % NS][:, t, kt * P:(kt + 1) * P], ident[:, :])
                        L.did(PE, ins, f"tr{h}")
                        e = ACTE if h % 2 else DVE
                        L.need(e, f"tr{h}")
                        L.ring(e, "av", h, 2, H)
                        if h % 2:
                            L.did(e, ACTE.activation(pT[h % 2][:, :, :], as2(tb[h % 2]), ACT.Copy), f"pT{h}")
                        else:
                            L.did(e, DVE.tensor_copy(pT[h % 2][:, :, :], as2(tb[h % 2])), f"pT{h}")

                    def values(h):
                        L.need(PE, "ev7", of=F)
                        L.need(PE, f"pT{h}")
                        if h == 0:
                            L.need(PE, "on1", lag=1)
                        for t in range(NT):
                            for kt in range(NT):
                                ins = PE.matmul(ob[t][:, h * HD:(h + 1) * HD], pT[h % 2][:, kt, t * P:(t + 1) * P],
                                                v[:, kt, h * HD:(h + 1) * HD], start=kt == 0, stop=kt == NT - 1)
                        L.did(PE, ins, f"av{h}")

                    for h in range(H + 2):
                        if h < H:
                            scores(h)
                        if 1 <= h < H + 1:
                            transpose_p(h - 1)
                        if h >= 2:
                            values(h - 2)
                        yield
                    L.need(DVE, f"exp{H - 1}_1")
                    L.need(DVE, "on1", lag=1)
                    L.did(DVE, DVE.reciprocal(rsum[:, :, :], ssum[:, :, :]), "rsum")
                    L.need(DVE, "rsum", f"av{H - 1}")
                    L.need(DVE, "ox1", lag=1)
                    for t in range(NT):
                        L.did(DVE, DVE.tensor_tensor(on[:, t, :].rearrange("p (h e) -> p h e", h=H),
                                                     ob[t][:, :].rearrange("p (h e) -> p h e", h=H),
                                                     rsum[:, t, :, None].broadcast_to([P, H, HD]), ALU.mult), f"on{t}")
                    for c2 in range(2):
                        L.need(PE, "on1")
                        L.need(PE, f"min{H - 2 + c2}_1")
                        xpose(L, on, sb[c2], c2, f"ox{c2}")
                        L.need(ACTE, f"ox{c2}")
                        L.need(ACTE, "o1", lag=1)
                        L.did(ACTE, ACTE.activation(chunk2(oTp[0], c2), as2(sb[c2]), ACT.Copy), f"oT_hi{c2}")
                        L.need(DVE, f"oT_hi{c2}")
                        L.did(DVE, DVE.tensor_tensor(chunk2(oTp[1], c2), as2(sb[c2]), chunk2(oTp[0], c2).bitcast(F32),
                                                     ALU.subtract), f"oT_lo{c2}")
                        yield
                    for t in range(NT):
                        L.need(PE, "oT_lo1")
                        L.need(PE, f"pT{H - 2 + t}")
                        L.did(PE, proj_N(tb[t], wo, oTp, t), f"o{t}")
                        L.need(DVE, f"o{t}")
                        L.need(DVE, "st", lag=1)
                        if first:
                            L.did(DVE, DVE.scalar_tensor_tensor(y[:, t, :], tb[t][:, :], tg[:, 0:1], x[L.par][:, t, :],
                                                                ALU.mult, ALU.add), f"out{t}")
                        else:
                            L.need(DVE, "x_cb", of=F)
                            L.did(DVE, DVE.tensor_tensor(y[:, t, :], tb[t][:, :], x[L.par][:, t, :], ALU.add), f"out{t}")
                        yield
                    L.need(POOL, "out1")
                    L.moved(POOL.dma_start(x_out[bass.ds(L.b.times(T), T), :].rearrange("(t p) f -> p t f", p=P), y[:, :, :]), "st")

                pipeline(nc, steps, [F, Bk], [front, back])
                finish(ph, [Bk])

        def finish(ph, lanes):
            for name in lanes:
                for b in (B - 2, B - 1):
                    L = Lane(steps, name, Batch(0, b))
                    steps.waited = {}
                    L.need(SP, "st")
            nc.all_engine_barrier()

        def wide_attention(x_in, x_out):
            ctx = ExitStack()
            with ctx:
                S = Lane(steps, "Bsetup", Batch(0, 0))
                G = pair(ctx, "G", [P, KC, D])
                U = pair(ctx, "U", [P, KC, D])
                alpha = tile(ctx, "alpha", [P, 1])
                S.moved(SP.dma_start(alpha[:, :], d["L1_xattn_alpha"].rearrange("(a n) -> a n", a=1).broadcast_to([P, 1])), "vectors")
                tmp = ExitStack()
                with tmp:
                    wq, wk, wv, woT = load_weights(tmp, S, [(w, d[w]) for w in ("L1_xattn_w_q", "L1_xattn_w_k", "L1_xattn_w_v", "L1_WoT")])
                    for i, (dst, lhs, rhs, last) in enumerate(((G, wq, wk, "lo1"), (U, wv, woT, "lo3"))):
                        for m in range(KC):
                            n = i * KC + m
                            S.need(PE, last, of=S.name)
                            ins = product(banks[n][:, :], [(parts(lhs, slice(None), k, slice(m * P, (m + 1) * P)),
                                                            parts(rhs, slice(None), k, slice(None))) for k in range(KC)])
                            S.did(PE, ins, f"fold{n}")
                            S.need(ACTE, f"fold{n}", of=S.name)
                            S.did(ACTE, ACTE.activation(dst[0][:, m, :], banks[n][:, :], ACT.Copy), f"fold_hi{n}")
                            S.need(DVE, f"fold_hi{n}", of=S.name)
                            S.did(DVE, DVE.tensor_tensor(dst[1][:, m, :], banks[n][:, :], dst[0][:, m, :].bitcast(F32),
                                                         ALU.subtract), f"fold_lo{n}")
                setup_done(S, PE, DVE, ACTE, POOL, SP)
                scale = float(D) ** -0.5

                x = both(ctx, tile, "B_x", [P, NT, D])
                cT = tile(ctx, "B_cT", [P, KC, T])
                cTp = both(ctx, pair, "B_cTp", [P, KC, T])
                xTp = pair(ctx, "B_xTp", [P, KC, T])
                qTp = both(ctx, pair, "B_qTp", [P, KC, T])
                Vp = both(ctx, pair, "B_Vp", [P, NT, D])
                smax = tile(ctx, "B_smax", [P, NT])
                nmax = tile(ctx, "B_nmax", [P, NT])
                pr = tile(ctx, "B_p", [P, NT, T])
                ssum = tile(ctx, "B_ssum", [P, NT])
                rsum = tile(ctx, "B_rsum", [P, NT])
                pTp = pair(ctx, "B_pTp", [P, NT, T])
                y = tile(ctx, "B_y", [P, NT, D])
                fb = banks[0:4]

                def evac(L, bank, pr_c, n, free):
                    L.need(ACTE, f"mm{n}")
                    for f, lag, of in free:
                        L.need(ACTE, f, lag=lag, of=of)
                    L.did(ACTE, ACTE.activation(pr_c[0], bank, ACT.Copy), f"hi{n}")
                    L.need(DVE, f"hi{n}")
                    L.did(DVE, DVE.tensor_tensor(pr_c[1], bank, pr_c[0].bitcast(F32), ALU.subtract), f"ev{n}")

                def front(L):
                    b = L.b
                    L.need(SP, "out1", lag=2, of="Bb")
                    L.moved(SP.dma_start(x[L.par][:, :, :], x_in[bass.ds(b.times(T), T), :].rearrange("(t p) f -> p t f", p=P)), "ld_x")
                    L.need(SP, "c_lo", lag=1)
                    L.moved(SP.dma_start(cT[:, :, :], d["ctxT"][:, bass.ds(b.times(T), T)].rearrange("(c p) t -> p c t", p=P)), "ld_c")
                    yield
                    L.need(ACTE, "ld_c")
                    L.need(ACTE, "mm5", lag=2)
                    L.need(ACTE, "qk", lag=2, of="Bb")
                    split(L, cT[:, :, :], cTp[L.par], "c")
                    for i in range(2):
                        L.need(PE, "ld_x")
                        L.ring(PE, "ev", i, 4, 8)
                        xpose(L, x[L.par], fb[i], i, f"mm{i}")
                        evac(L, as2(fb[i]), [chunk2(xTp[j], i) for j in range(2)], i, [("mm3", 1, None)])
                        yield
                    for i in range(2):
                        n = 2 + i
                        L.need(PE, "ev1")
                        L.ring(PE, "ev", n, 4, 8)
                        L.did(PE, proj_T(fb[n], G, xTp, i), f"mm{n}")
                        evac(L, as2(fb[n]), [chunk2(qTp[L.par][j], i) for j in range(2)], n, [("qk", 2, "Bb")])
                        yield
                    for t in range(NT):
                        n = 4 + t
                        L.need(PE, "c_lo")
                        L.ring(PE, "ev", n, 4, 8)
                        L.did(PE, proj_N(fb[t], U, cTp[L.par], t), f"mm{n}")
                        evac(L, fb[t][:, :], [Vp[L.par][j][:, t, :] for j in range(2)], n, [("pv1", 2, "Bb")])
                        yield
                    S.s.found[(L.name, "ev6")] = S.s.found[(L.name, "ev2")]
                    S.s.found[(L.name, "ev7")] = S.s.found[(L.name, "ev3")]

                sb, tb, ob = banks[4], banks[5], banks[6:8]

                def back(L):
                    L.need(PE, "ev3", of="Bf")
                    L.need(PE, "exp1", lag=1)
                    for t in range(NT):
                        ins = product(sb[:, t * T:(t + 1) * T],
                                      [(parts(qTp[L.par], slice(None), k, slice(t * P, (t + 1) * P)),
                                        parts(cTp[L.par], slice(None), k, slice(None))) for k in range(KC)])
                    L.did(PE, ins, "qk")
                    L.need(DVE, "qk")
                    L.did(DVE, DVE.reduce_max(smax[:, :], as2(sb), AX.X), "max")
                    L.need(DVE, "max")
                    L.need(DVE, "exp1", lag=1)
                    L.did(DVE, DVE.tensor_scalar(nmax[:, :], smax[:, :], -scale, None, ALU.mult), "nmax")
                    L.need(ACTE, "nmax")
                    L.need(ACTE, "pt", "rsum", lag=1)
                    for t in range(NT):
                        L.did(ACTE, ACTE.activation(pr[:, t, :], sb[:, t * T:(t + 1) * T], ACT.Exp, scale=scale,
                                                    bias=nmax[:, t:t + 1], accum_out=ssum[:, t:t + 1]), f"exp{t}")
                    L.need(DVE, "exp1")
                    L.need(DVE, "out1", lag=1)
                    L.did(DVE, DVE.reciprocal(rsum[:, :], ssum[:, :]), "recip")
                    L.need(DVE, "recip")
                    L.did(DVE, DVE.tensor_scalar(rsum[:, :], rsum[:, :], alpha[:, 0:1], None, ALU.mult), "rsum")
                    yield
                    yield
                    L.need(PE, "exp1")
                    L.need(PE, "pT_lo", lag=1)
                    for kt in range(NT):
                        for t in range(NT):
                            ins = PE.transpose(tb[:, kt * T + t * P:kt * T + (t + 1) * P], pr[:, t, kt * P:(kt + 1) * P], ident[:, :])
                    L.did(PE, ins, "pt")
                    L.need(ACTE, "pt")
                    L.need(ACTE, "pv1", lag=1)
                    L.did(ACTE, ACTE.activation(pTp[0][:, :, :], as2(tb), ACT.Copy), "pT_hi")
                    L.need(DVE, "pT_hi")
                    L.did(DVE, DVE.tensor_tensor(pTp[1][:, :, :], as2(tb), pTp[0][:, :, :].bitcast(F32), ALU.subtract), "pT_lo")
                    yield
                    yield
                    for t in range(NT):
                        L.need(PE, "pT_lo")
                        L.need(PE, "ev5", of="Bf")
                        L.need(PE, f"out{t}", lag=1)
                        ins = product(ob[t][:, :], [(parts(pTp, slice(None), kt, slice(t * P, (t + 1) * P)),
                                                     parts(Vp[L.par], slice(None), kt, slice(None))) for kt in range(NT)])
                        L.did(PE, ins, f"pv{t}")
                        L.need(DVE, f"pv{t}", "rsum")
                        L.need(DVE, "st", lag=1)
                        L.did(DVE, DVE.scalar_tensor_tensor(y[:, t, :], ob[t][:, :], rsum[:, t:t + 1], x[L.par][:, t, :],
                                                            ALU.mult, ALU.add), f"out{t}")
                    L.need(POOL, "out1")
                    L.moved(POOL.dma_start(x_out[bass.ds(L.b.times(T), T), :].rearrange("(t p) f -> p t f", p=P), y[:, :, :]), "st")
                    yield

                pipeline(nc, steps, ["Bf", "Bb"], [front, back])
                finish("B", ["Bb"])

        def mix_T(L, out, xT, sx, coef, name):
            for k in range(KC):
                L.did(DVE, DVE.scalar_tensor_tensor(out[:, k, :], sx[:, k, :], coef[:, k:k + 1], xT[:, k, 1:T + 1],
                                                    ALU.mult, ALU.add), name)

        def tokens(ap, b):
            return ap[bass.ds(b.times(T), T), :].rearrange("(t p) f -> p t f", p=P)

        def load_column0(L, xT, row, step):
            with nc.allow_non_contiguous_dma(reason="one token's features, one per partition"):
                L.moved(SP.dma_start(xT[:, :, 0:1], d["ctxT"][:, bass.ds(L.b.times(T, row), 1)]
                                     .rearrange("(c p) t -> p c t", p=P)), step)

        def time_mix(x_in, z_out):
            ctx = ExitStack()
            with ctx:
                S = Lane(steps, "Csetup", Batch(0, 0))
                ln_w, ln_b, maa_x, stack, decay, u, gn_w, gn_b = [
                    columns(ctx, S, "L2_xattn_" + n) for n in
                    ("ln1_w", "ln1_b", "maa_x", "maa_stack", "time_decay", "u", "gn_w", "gn_b")]

                def plain(name, src):
                    rows_, cols = src.shape
                    p = min(rows_, P)
                    t_ = tile(ctx, f"w_{name}", [p, rows_ // p, cols])
                    S.moved(SP.dma_start(t_[:, :, :], src.rearrange("(c p) n -> p c n", p=p)), "weights")
                    return t_

                w1 = plain("maa_w1", d["L2_xattn_maa_w1"])
                w2a = plain("maa_w2a", d["L2_xattn_maa_w2"][0:P, :])
                w2b = plain("maa_w2b", d["L2_xattn_maa_w2"][P:NMIX * DM, :])
                wv, td1, td2 = plain("Wv", d["L2_WvT"]), plain("td_w1", d["L2_xattn_td_w1"]), plain("td_w2", d["L2_xattn_td_w2"])
                wk, wr, wg = plain("Wk", d["L2_WkT"]), plain("Wr", d["L2_WrT"]), plain("Wg", d["L2_WgT"])
                S.need(DVE, "vectors", of=S.name)
                for t_, n in ((gn_w, "half_w"), (gn_b, "half_b")):
                    S.did(DVE, DVE.tensor_scalar(t_[:, :], t_[:, :], 0.5, None, ALU.mult), n)
                setup_done(S, PE, DVE, ACTE, POOL, SP)

                x = both(ctx, tile, "C_x", [P, NT, D])
                nst = norm_tiles(ctx, "C")
                xn = tile(ctx, "C_xn", [P, NT, D])
                xaT = both(ctx, tile, "C_xaT", [P, KC, T + 1])
                sx = tile(ctx, "C_sx", [P, KC, T])
                xi = tile(ctx, "C_xi", [P, KC, T])
                mf = both(ctx, tile, "C_mix", [P, KC, T])
                tx = tile(ctx, "C_tx", [P, 2, T])
                tdt = tile(ctx, "C_tdt", [DD, T])
                th = both(ctx, tile, "C_th", [P, 2, T])
                vT = tile(ctx, "C_vT", [P, KC, T])
                ruk = tile(ctx, "C_ruk", [P, KC, T])
                vtok = both(ctx, tile, "C_vtok", [P, NT, D])
                wT = both(ctx, tile, "C_wT", [P, KC, T])
                kT = both(ctx, tile, "C_kT", [P, KC, T])
                rT = both(ctx, tile, "C_rT", [P, KC, T])
                gT = both(ctx, tile, "C_gT", [P, KC, T])
                ctok = both(ctx, tile, "C_ctok", [P, NT, RH])
                s0 = both(ctx, tile, "C_s0", [P, KC, RS])
                NV, NX = 4, 4
                Vb = [tile(ctx, f"C_V{i}", [P, JH, T]) for i in range(NV)]
                Sx = [tile(ctx, f"C_S{i}", [P, JH, T]) for i in range(NX)]
                og = tile(ctx, "C_og", [P, NT * RH, RS])
                sq = tile(ctx, "C_sq", [P, NT * RH, RS])
                s1 = tile(ctx, "C_s1", [P, NT * RH])
                s2 = tile(ctx, "C_s2", [P, NT * RH])
                zT = tile(ctx, "C_zT", [P, KC, T])
                fb, NF = banks[0:4], 28
                YB, ZB = banks[4:6], banks[6:8]
                QN = RS // JH
                UN = KC * QN
                FRONT, SCAN, TAIL = "C0", "C1", "C2"

                def plain_T(bank, w, xT, c2):
                    for c in range(2):
                        m = 2 * c2 + c
                        for k in range(KC):
                            ins = PE.matmul(bank[:, c * T:(c + 1) * T], w[:, k, m * P:(m + 1) * P], xT[:, k, :],
                                            start=k == 0, stop=k == KC - 1)
                    return ins

                def front(L):
                    b, par = L.b, L.par
                    n = [0]
                    xa = xaT[par]

                    def bank():
                        k = n[0]
                        n[0] += 1
                        L.ring(PE, "ev", k, 4, NF)
                        return k, fb[k % 4]

                    L.need(SP, "norm1", lag=2)
                    L.moved(SP.dma_start(x[par][:, :, :], tokens(x_in, b)), "ld_x")
                    L.need(SP, "add4", lag=2)
                    load_column0(L, xa, 1, "ld_prev")
                    L.need(SP, f"scan{UN - 1}", f"s0_{UN - 1}", lag=2, of=SCAN)
                    for g in range(KC):
                        L.moved(SP.dma_start(s0[par][:, g, :], d["ctx"][bass.ds(b.times(T, 2 + 4 * g), 4), :]
                                             .rearrange("r (q j) -> (r q) j", j=RS)), "ld_s0")
                    yield
                    norm(L, x[par], xn, nst, "ld_x")
                    yield
                    kx = []
                    for c2 in range(2):
                        k, bk = bank()
                        kx.append((k, bk))
                        L.need(PE, "norm1")
                        xpose(L, xn, bk, c2, f"xposed{c2}")
                    yield
                    for c2, (k, bk) in enumerate(kx):
                        L.need(ACTE, f"xposed{c2}")
                        L.need(ACTE, "add4", lag=2)
                        for c in range(2):
                            m = 2 * c2 + c
                            L.did(ACTE, ACTE.activation(xa[:, m, 1:T + 1], bk[:, c * T:(c + 1) * T], ACT.Identity,
                                                        scale=ln_w[:, m:m + 1], bias=ln_b[:, m:m + 1]), f"ev{k}", "xa")
                    yield
                    L.need(DVE, "xa", "ld_prev")
                    L.need(DVE, "mixed4", lag=1)
                    L.did(DVE, DVE.tensor_tensor(sx[:, :, :], xa[:, :, 0:T], xa[:, :, 1:T + 1], ALU.subtract), "sx")
                    L.need(DVE, "sx")
                    L.need(DVE, "w1mm", lag=1)
                    mix_T(L, xi, xa, sx, maa_x, "xi")
                    yield
                    k, bk = bank()
                    L.need(PE, "xi")
                    for c, rows_ in ((0, P), (1, DM)):
                        for q in range(KC):
                            ins = PE.matmul(bk[0:rows_, c * T:(c + 1) * T], w1[:, q, c * P:c * P + rows_], xi[:, q, :],
                                            start=q == 0, stop=q == KC - 1)
                    L.did(PE, ins, "w1mm")
                    yield
                    L.need(ACTE, "w1mm")
                    L.need(ACTE, "w2mm4", lag=1)
                    L.did(ACTE, ACTE.activation(tx[:, 0, :], bk[:, 0:T], ACT.Tanh), "tx0")
                    L.did(ACTE, ACTE.activation(tx[0:DM, 1, :], bk[0:DM, T:2 * T], ACT.Tanh), f"ev{k}", "tx")
                    yield

                    order = (2, 1, 0, 3, 4)
                    held = {}

                    def weights(i):
                        f = order[i]
                        w2, r = (w2a if f < 4 else w2b), slice(DM * (f % 4), DM * (f % 4) + DM)
                        held[i] = []
                        for c2 in range(2):
                            k, bk = bank()
                            held[i].append((k, bk))
                            L.need(PE, "tx")
                            for c in range(2):
                                m = 2 * c2 + c
                                ins = PE.matmul(bk[:, c * T:(c + 1) * T], w2[r, 0, m * P:(m + 1) * P], tx[r, f // 4, :],
                                                start=True, stop=True)
                            L.did(PE, ins, f"w2mm{f}_{c2}", f"w2mm{f}")

                    def mixed(i):
                        f = order[i]
                        for c2, (k, bk) in enumerate(held[i]):
                            L.need(DVE, f"w2mm{f}_{c2}")
                            L.need(DVE, f"proj{order[i - 2]}", lag=0 if i >= 2 else 1)
                            for c in range(2):
                                m = 2 * c2 + c
                                L.did(DVE, DVE.scalar_tensor_tensor(mf[i % 2][:, m, :], bk[:, c * T:(c + 1) * T],
                                                                    stack[:, KC * f + m:KC * f + m + 1], sx[:, m, :],
                                                                    ALU.add, ALU.mult), f"ev{k}", f"mixed{f}")

                    def add(i):
                        f = order[i]
                        L.need(POOL, f"mixed{f}")
                        L.did(POOL, POOL.tensor_tensor(mf[i % 2][:, :, :], mf[i % 2][:, :, :], xa[:, :, 1:T + 1], ALU.add), f"add{f}")

                    def project(i, w):
                        f = order[i]
                        held[f"p{f}"] = []
                        for c2 in range(2):
                            k, bk = bank()
                            held[f"p{f}"].append((k, bk))
                            L.need(PE, f"add{f}")
                            L.did(PE, plain_T(bk, w, mf[i % 2], c2), f"proj{f}_{c2}", f"proj{f}")

                    def copy_out(f, dst, name):
                        for c2, (k, bk) in enumerate(held[f"p{f}"]):
                            L.need(ACTE, f"proj{f}_{c2}")
                            L.did(ACTE, ACTE.activation(chunk2(dst, c2), as2(bk), ACT.Copy), f"ev{k}", name)

                    def v_out():
                        L.need(ACTE, "st_v", "vx", lag=1)
                        copy_out(2, vT, "v")
                        L.need(SP, "v")
                        L.moved(SP.dma_start(d["vT"][bass.ds(b.times(D), D), :].rearrange("(c p) t -> p c t", p=P),
                                             vT[:, :, :]), "st_v")

                    def v_tokens():
                        held["vt"] = []
                        for t in range(NT):
                            k, bk = bank()
                            held["vt"].append((k, bk))
                            L.need(PE, "v")
                            for c in range(KC):
                                ins = PE.transpose(bk[:, c * P:(c + 1) * P], vT[:, c, t * P:(t + 1) * P], ident[:, :])
                            L.did(PE, ins, f"vx{t}", "vx")

                    def v_tokens_out():
                        for t, (k, bk) in enumerate(held["vt"]):
                            L.need(ACTE, f"vx{t}")
                            L.need(ACTE, "cv", lag=2, of=SCAN)
                            L.did(ACTE, ACTE.activation(vtok[par][:, t, :], bk[:, :], ACT.Copy), f"ev{k}", "vtok")

                    def decay_down():
                        k, bk = bank()
                        held["td1"] = (k, bk)
                        L.need(PE, "add1")
                        for q in range(KC):
                            ins = PE.matmul(bk[0:DD, 0:T], td1[:, q, :], mf[1][:, q, :], start=q == 0, stop=q == KC - 1)
                        L.did(PE, ins, "proj1")

                    def decay_tanh():
                        k, bk = held["td1"]
                        L.need(ACTE, "proj1")
                        L.need(ACTE, "td2mm", lag=1)
                        L.did(ACTE, ACTE.activation(tdt[:, :], bk[0:DD, 0:T], ACT.Tanh), f"ev{k}", "tdt")

                    def decay_up():
                        held["td2"] = []
                        for c2 in range(2):
                            k, bk = bank()
                            held["td2"].append((k, bk))
                            L.need(PE, "tdt")
                            for c in range(2):
                                m = 2 * c2 + c
                                ins = PE.matmul(bk[:, c * T:(c + 1) * T], td2[:, 0, m * P:(m + 1) * P], tdt[:, :], start=True, stop=True)
                            L.did(PE, ins, f"td2mm{c2}", "td2mm")

                    def decay_out():
                        for c2, (k, bk) in enumerate(held["td2"]):
                            L.need(ACTE, f"td2mm{c2}")
                            L.need(ACTE, f"scan{UN - 1}", lag=2, of=SCAN)
                            for c in range(2):
                                m = 2 * c2 + c
                                L.did(ACTE, ACTE.activation(wT[par][:, m, :], bk[:, c * T:(c + 1) * T], ACT.Exp,
                                                            bias=decay[:, m:m + 1]), f"ev{k}", "w_log")
                        L.need(ACTE, "w_log")
                        L.did(ACTE, ACTE.activation(wT[par][:, :, :], wT[par][:, :, :], ACT.Exp, scale=-1.0), "w")

                    def k_out():
                        L.need(ACTE, f"a{UN - 1}", lag=2, of=SCAN)
                        copy_out(0, kT[par], "k")

                    def r_out():
                        L.need(ACTE, f"m{UN - 1}", f"m{UN - 2}", lag=2, of=SCAN)
                        copy_out(3, rT[par], "r")

                    def coefficient():
                        L.need(DVE, "k", "r")
                        L.need(DVE, "cmm", lag=1)
                        for m in range(KC):
                            L.did(DVE, DVE.scalar_tensor_tensor(ruk[:, m, :], rT[par][:, m, :], u[:, m:m + 1], kT[par][:, m, :],
                                                                ALU.mult, ALU.mult), "ruk")

                    def coefficient_sum():
                        k, bk = bank()
                        held["c"] = (k, bk)
                        L.need(PE, "ruk")
                        for t in range(NT):
                            for g in range(KC):
                                ins = PE.matmul(bk[:, t * RH + g * GH:t * RH + (g + 1) * GH], ruk[:, g, t * P:(t + 1) * P],
                                                headsum[:, :], start=True, stop=True)
                        L.did(PE, ins, "cmm")

                    def coefficient_out():
                        k, bk = held["c"]
                        L.need(ACTE, "cmm")
                        L.need(ACTE, "cv", lag=2, of=SCAN)
                        L.did(ACTE, ACTE.activation(ctok[par][:, :, :].rearrange("p t h -> p (t h)"), bk[:, 0:NT * RH], ACT.Copy),
                              f"ev{k}", "c")

                    def gate_tanh():
                        for c2, (k, bk) in enumerate(held["p4"]):
                            L.need(ACTE, f"proj4_{c2}")
                            L.need(ACTE, f"g{c2}", lag=1)
                            L.did(ACTE, ACTE.activation(th[c2][:, :, :], as2(bk), ACT.Tanh, scale=0.5), f"th{c2}")

                    def gate():
                        for c2, (k, bk) in enumerate(held["p4"]):
                            L.need(DVE, f"th{c2}")
                            L.need(DVE, "z", lag=2, of=TAIL)
                            L.did(DVE, DVE.scalar_tensor_tensor(chunk2(gT[par], c2), th[c2][:, :, :], 1.0, as2(bk), ALU.add, ALU.mult),
                                  f"ev{k}", f"g{c2}", "g")

                    plan = [
                        [lambda: weights(0)],
                        [lambda: mixed(0)],
                        [lambda: add(0), lambda: weights(1)],
                        [lambda: mixed(1)],
                        [lambda: add(1), lambda: project(0, wv)],
                        [v_out, decay_down],
                        [decay_tanh, lambda: weights(2), v_tokens],
                        [lambda: mixed(2), v_tokens_out, decay_up],
                        [lambda: add(2), decay_out, lambda: weights(3)],
                        [lambda: mixed(3)],
                        [lambda: add(3), lambda: project(2, wk)],
                        [k_out],
                        [lambda: weights(4)],
                        [lambda: mixed(4), lambda: project(3, wr)],
                        [r_out, lambda: add(4)],
                        [coefficient, lambda: project(4, wg)],
                        [gate_tanh, coefficient_sum],
                        [gate, coefficient_out],
                    ]
                    for slot in plan:
                        for act in slot:
                            act()
                        yield
                    assert n[0] == NF - 1
                    L.s.found[(L.name, f"ev{NF - 1}")] = L.s.found[(L.name, f"ev{NF - 5}")]

                def scan(L):
                    b, par = L.b, L.par
                    w, k, r, s = wT[par], kT[par], rT[par], s0[par]

                    def load(n):
                        g, q = n // QN, n % QN
                        L.need(SP, "st_v", of=FRONT)
                        L.ring(SP, "red", n, NV, UN)
                        src = d["vT"][bass.ds(b.times(D, g * P), P), :].rearrange("(h j) t -> h j t", j=RS)[:, q * JH:(q + 1) * JH, :]
                        L.slot(SP.dma_start(Vb[n % NV][:, :, :].rearrange("p j t -> p (j t)"),
                                            src.rearrange("h j t -> h (j t)")[:, None, :].broadcast_to([GH, RS, JH * T])),
                               f"ld_v{n}", f"v_slot{n % NV}")

                    def reduce(n):
                        g, q = n // QN, n % QN
                        L.need(PE, f"m{n}")
                        if n == 0:
                            L.need(PE, "og1", lag=1)
                        for t in range(NT):
                            for j in range(JH):
                                out = YB[t][:, g * P:(g + 1) * P].rearrange("p (h j) -> p h j", j=RS)[:, :, q * JH + j]
                                ins = PE.matmul(out, Vb[n % NV][:, j, t * P:(t + 1) * P], headsum[:, :], start=True, stop=True)
                        L.did(PE, ins, f"red{n}")

                    def product_kv(n):
                        g, q = n // QN, n % QN
                        v, sc = Vb[n % NV], Sx[n % NX]
                        L.need(DVE, f"ld_v{n}")
                        L.need(DVE, "w", "k", of=FRONT)
                        L.did(DVE, DVE.tensor_tensor(v[:, :, :], v[:, :, :], k[:, g:g + 1, :].broadcast_to([P, JH, T]), ALU.mult), f"a{n}")
                        L.need(ACTE, "ld_s0", of=FRONT)
                        L.ring(ACTE, "m", n, NX, UN)
                        L.did(ACTE, ACTE.activation(sc[:, :, 0:1], s[:, g, q * JH:(q + 1) * JH, None], ACT.Copy), f"s0_{n}")

                    load(0)
                    load(1)
                    product_kv(0)
                    for n in range(UN):
                        if n + 2 < UN:
                            load(n + 2)
                        g, q = n // QN, n % QN
                        v, sc = Vb[n % NV], Sx[n % NX]
                        if n + 1 < UN:
                            product_kv(n + 1)
                        L.need(DVE, "ld_s0", of=FRONT)
                        L.need(DVE, f"a{n}")
                        L.ring(DVE, "m", n, NX, UN)
                        for j in range(JH):
                            L.did(DVE, DVE.tensor_tensor_scan(sc[:, j, 1:T], w[:, g, 0:T - 1], v[:, j, 0:T - 1],
                                                              s[:, g, q * JH + j:q * JH + j + 1], ALU.mult, ALU.add), f"scan{n}")
                        e = POOL if q in POOL_UNITS else DVE
                        L.need(e, f"scan{n}", f"s0_{n}")
                        L.need(e, "r", of=FRONT)
                        L.did(e, e.tensor_tensor(v[:, :, :], sc[:, :, :], r[:, g:g + 1, :].broadcast_to([P, JH, T]), ALU.mult), f"m{n}")
                        if n >= 1:
                            reduce(n - 1)
                        yield
                    L.need(POOL, "c", "vtok", of=FRONT)
                    L.need(POOL, "zx1", lag=1, of=TAIL)
                    L.did(POOL, POOL.tensor_tensor(og[:, :, :], vtok[par][:, :, :].rearrange("p t (h j) -> p (t h) j", j=RS),
                                                   ctok[par][:, :, :].rearrange("p t h -> p (t h)")[:, :, None]
                                                   .broadcast_to([P, NT * RH, RS]), ALU.mult), "cv")
                    reduce(UN - 1)
                    yield
                    L.need(DVE, "cv", f"red{UN - 1}")
                    for t in range(NT):
                        o = og[:, t * RH:(t + 1) * RH, :]
                        L.did(DVE, DVE.tensor_tensor(o, YB[t][:, :].rearrange("p (h j) -> p h j", j=RS), o, ALU.add), f"og{t}")

                def tail(L):
                    b, par = L.b, L.par
                    L.need(DVE, "og1", of=SCAN)
                    L.need(DVE, "centred", lag=1)
                    L.did(DVE, DVE.reduce_sum(s1[:, :], og[:, :, :], AX.X), "sum")
                    L.need(DVE, "sum")
                    L.did(DVE, DVE.tensor_scalar(s1[:, :], s1[:, :], 1.0 / RS, None, ALU.mult), "mean")
                    yield
                    L.need(POOL, "mean")
                    L.did(POOL, POOL.tensor_tensor(og[:, :, :], og[:, :, :], s1[:, :, None].broadcast_to([P, NT * RH, RS]),
                                                   ALU.subtract), "centred")
                    yield
                    L.need(ACTE, "centred")
                    L.need(ACTE, "sumsq", lag=1)
                    L.did(ACTE, ACTE.activation(sq[:, :, :], og[:, :, :], ACT.Square), "sq")
                    yield
                    L.need(DVE, "sq")
                    L.need(DVE, "normed", lag=1)
                    L.did(DVE, DVE.reduce_sum(s2[:, :], sq[:, :, :], AX.X), "sumsq")
                    L.need(DVE, "sumsq")
                    L.did(DVE, DVE.tensor_scalar(s2[:, :], s2[:, :], 1.0 / RS, EPS, ALU.mult, ALU.add), "var")
                    yield
                    L.need(ACTE, "var")
                    L.did(ACTE, ACTE.activation(s2[:, :], s2[:, :], ACT.Sqrt), "std")
                    yield
                    L.need(DVE, "std")
                    L.did(DVE, DVE.reciprocal(s2[:, :], s2[:, :]), "rstd")
                    yield
                    L.need(POOL, "rstd")
                    L.did(POOL, POOL.tensor_tensor(og[:, :, :], og[:, :, :], s2[:, :, None].broadcast_to([P, NT * RH, RS]),
                                                   ALU.mult), "normed")
                    yield
                    flat = og[:, :, :].rearrange("p (t h) j -> p t (h j)", t=NT)
                    for c2 in range(2):
                        L.need(PE, "normed")
                        L.need(PE, f"zev{c2}", lag=1)
                        xpose(L, flat, ZB[c2], c2, f"zx{c2}")
                    yield
                    for c2 in range(2):
                        L.need(ACTE, f"zx{c2}")
                        L.need(ACTE, "st", lag=1)
                        for c in range(2):
                            m = 2 * c2 + c
                            L.did(ACTE, ACTE.activation(zT[:, m, :], ZB[c2][:, c * T:(c + 1) * T], ACT.Identity,
                                                        scale=gn_w[:, m:m + 1], bias=gn_b[:, m:m + 1]), f"zev{c2}")
                    yield
                    L.need(POOL, "zev1")
                    L.need(POOL, "g", of=FRONT)
                    L.did(POOL, POOL.tensor_tensor(zT[:, :, :], zT[:, :, :], gT[par][:, :, :], ALU.mult), "z")
                    yield
                    L.need(SP, "z")
                    L.moved(SP.dma_start(z_out[bass.ds(b.times(D), D), :].rearrange("(c p) t -> p c t", p=P), zT[:, :, :]), "st")
                    for _ in range(4):
                        yield

                pipeline(nc, steps, [FRONT, SCAN, TAIL], [front, scan, tail])
                finish("C", [TAIL])


        def channel_mix(x_in, z_in, x_out):
            ctx = ExitStack()
            with ctx:
                S = Lane(steps, "Dsetup", Batch(0, 0))
                ln_w, ln_b, fk, fr = [columns(ctx, S, "L2_xattn_" + n) for n in ("ln2_w", "ln2_b", "ffn_maa_k", "ffn_maa_r")]
                wo, wfk, wfr, wfv = load_weights(ctx, S, [(n, d[f"L2_{n}T"]) for n in ("Wo", "Wfk", "Wfr", "Wfv")])
                setup_done(S, PE, DVE, ACTE, POOL, SP)
                zT = tile(ctx, "D_zT", [P, KC, T])
                zTp = pair(ctx, "D_zTp", [P, KC, T])
                x = tile(ctx, "D_x", [P, NT, D])
                x1 = both(ctx, tile, "D_x1", [P, NT, D])
                xr = both(ctx, tile, "D_xr", [P, NT, D])
                nst = norm_tiles(ctx, "D")
                xn = tile(ctx, "D_xn", [P, NT, D])
                xcT = both(ctx, tile, "D_xcT", [P, KC, T + 1])
                sx = tile(ctx, "D_sx", [P, KC, T])
                mk, mr = both(ctx, tile, "D_mix", [P, KC, T])
                mkp, mrp = both(ctx, pair, "D_mixp", [P, KC, T])
                kr = tile(ctx, "D_kr", [P, KC, T])
                kkp = both(ctx, pair, "D_kkp", [P, KC, T])
                rt = both(ctx, tile, "D_rt", [P, NT, D])
                y = tile(ctx, "D_y", [P, NT, D])

                def first(L):
                    b, par = L.b, L.par
                    L.need(SP, "z_lo", lag=1)
                    L.moved(SP.dma_start(zT[:, :, :], z_in[bass.ds(b.times(D), D), :].rearrange("(c p) t -> p c t", p=P)), "ld_z")
                    L.need(SP, "x1_1", lag=1)
                    L.moved(SP.dma_start(x[:, :, :], tokens(x_in, b)), "ld_x")
                    L.need(SP, "mr", lag=2, of="D1")
                    load_column0(L, xcT[par], 0, "ld_prev")
                    L.need(ACTE, "ld_z")
                    L.need(ACTE, "o1", lag=1)
                    split(L, zT[:, :, :], zTp, "z")
                    yield
                    for t in range(NT):
                        L.need(PE, "z_lo")
                        L.need(PE, f"x1_{t}", lag=1)
                        L.did(PE, proj_N(banks[t], wo, zTp, t), f"o{t}")
                        L.need(DVE, f"o{t}", "ld_x")
                        L.need(DVE, "xr", lag=2, of="D1")
                        L.did(DVE, DVE.tensor_tensor(x1[par][:, t, :], banks[t][:, :], x[:, t, :], ALU.add), f"x1_{t}")
                        yield
                    norm(L, x1[par], xn, nst, "x1_1")
                    yield
                    for c2 in range(2):
                        L.need(PE, "norm1")
                        L.need(PE, f"xc{c2}", lag=1)
                        xpose(L, xn, banks[2 + c2], c2, f"xposed{c2}")
                        L.need(ACTE, f"xposed{c2}")
                        L.need(ACTE, "mr", lag=2, of="D1")
                        for c in range(2):
                            m = 2 * c2 + c
                            L.did(ACTE, ACTE.activation(xcT[par][:, m, 1:T + 1], banks[2 + c2][:, c * T:(c + 1) * T],
                                                        ACT.Identity, scale=ln_w[:, m:m + 1], bias=ln_b[:, m:m + 1]), f"xc{c2}")
                        yield

                def second(L):
                    par = L.par
                    xc = xcT[par]
                    L.need(POOL, "x1_1", of="D0")
                    L.need(POOL, "out1", lag=2, of="D2")
                    L.did(POOL, POOL.tensor_copy(xr[par][:, :, :], x1[par][:, :, :]), "xr")
                    L.need(DVE, "xc1", "ld_prev", of="D0")
                    L.did(DVE, DVE.tensor_tensor(sx[:, :, :], xc[:, :, 0:T], xc[:, :, 1:T + 1], ALU.subtract), "sx")
                    L.need(DVE, "sx")
                    L.need(DVE, "mk_lo", lag=1)
                    mix_T(L, mk, xc, sx, fk, "mk")
                    L.need(DVE, "mr_lo", lag=1)
                    mix_T(L, mr, xc, sx, fr, "mr")
                    L.need(ACTE, "mk")
                    L.need(ACTE, "k1", lag=1)
                    split(L, mk[:, :, :], mkp, "mk")
                    L.need(ACTE, "mr")
                    L.need(ACTE, "r1", lag=1)
                    split(L, mr[:, :, :], mrp, "mr")
                    yield
                    for c2 in range(2):
                        L.need(PE, "mk_lo")
                        L.need(PE, f"rt{c2}", lag=1)
                        L.did(PE, proj_T(banks[4 + c2], wfk, mkp, c2), f"k{c2}")
                        L.need(ACTE, f"k{c2}")
                        L.need(ACTE, "kk_lo", lag=1)
                        L.did(ACTE, ACTE.activation(chunk2(kr, c2), as2(banks[4 + c2]), ACT.Relu), f"kr{c2}")
                        yield
                    L.need(POOL, "kr1")
                    L.did(POOL, POOL.tensor_tensor(kr[:, :, :], kr[:, :, :], kr[:, :, :], ALU.mult), "kk")
                    L.need(ACTE, "kk")
                    L.need(ACTE, "v1", lag=2, of="D2")
                    split(L, kr[:, :, :], kkp[par], "kk")
                    for t in range(NT):
                        L.need(PE, "mr_lo", f"kr{t}")
                        L.did(PE, proj_N(banks[4 + t], wfr, mrp, t), f"r{t}")
                        L.need(ACTE, f"r{t}")
                        L.need(ACTE, "gated1", lag=2, of="D2")
                        L.did(ACTE, ACTE.activation(rt[par][:, t, :], banks[4 + t][:, :], ACT.Tanh, scale=0.5), f"rt{t}")
                        yield

                def third(L):
                    par = L.par
                    for t in range(NT):
                        L.need(PE, "kk_lo", of="D1")
                        L.need(PE, f"gated{t}", lag=1)
                        L.did(PE, proj_N(banks[6 + t], wfv, kkp[par], t), f"v{t}")
                        L.need(DVE, f"v{t}")
                        L.need(DVE, f"rt{t}", "xr", of="D1")
                        L.need(DVE, "st", lag=1)
                        L.did(DVE, DVE.scalar_tensor_tensor(y[:, t, :], rt[par][:, t, :], 1.0, banks[6 + t][:, :],
                                                            ALU.add, ALU.mult), f"gated{t}")
                        L.need(DVE, f"gated{t}")
                        L.did(DVE, DVE.scalar_tensor_tensor(y[:, t, :], y[:, t, :], 0.5, xr[par][:, t, :],
                                                            ALU.mult, ALU.add), f"out{t}")
                        yield
                    L.need(POOL, "out1")
                    L.moved(POOL.dma_start(tokens(x_out, L.b), y[:, :, :]), "st")

                pipeline(nc, steps, ["D0", "D1", "D2"], [first, second, third])
                finish("D", ["D2"])

        def mlp(x_in, x_out):
            ctx = ExitStack()
            with ctx:
                S = Lane(steps, "Fsetup", Batch(0, 0))
                ln_w, ln_b, fcb = [columns(ctx, S, "L3_xattn_" + n) for n in ("ln2_w", "ln2_b", "fc_b")]
                pb = rows(ctx, S, "L3_xattn_proj_b")
                fc, pj = d["L3_xattn_fc_w"], d["L3_xattn_proj_w"]
                ws = load_weights(ctx, S, [(f"fc{i}", fc[:, i * D:(i + 1) * D]) for i in range(4)]
                                  + [(f"pj{i}", pj[i * D:(i + 1) * D, :]) for i in range(4)])
                setup_done(S, PE, DVE, ACTE, POOL, SP)
                x = both(ctx, tile, "F_x", [P, NT, D])
                nst = norm_tiles(ctx, "F")
                xn = tile(ctx, "F_xn", [P, NT, D])
                aT = tile(ctx, "F_aT", [P, KC, T])
                aTp = both(ctx, pair, "F_aTp", [P, KC, T])
                NH = 4
                hf = both(ctx, tile, "F_h", [P, 2, T])
                hp = [pair(ctx, f"F_hp{i}", [P, 2, T]) for i in range(NH)]
                y = tile(ctx, "F_y", [P, NT, D])
                NU = NI // 2

                def front(L):
                    b, par = L.b, L.par
                    L.need(SP, "out1", lag=2, of="F1")
                    L.moved(SP.dma_start(x[par][:, :, :], tokens(x_in, b)), "ld_x")
                    norm(L, x[par], xn, nst, "ld_x")
                    L.need(POOL, "norm1")
                    L.did(POOL, POOL.tensor_tensor(x[par][:, :, :], x[par][:, :, :], pb[:, None, :].broadcast_to([P, NT, D]), ALU.add), "x_pb")
                    yield
                    for c2 in range(2):
                        L.need(PE, "norm1")
                        L.need(PE, f"ev{c2}", lag=1)
                        xpose(L, xn, banks[c2], c2, f"xposed{c2}")
                        L.need(ACTE, f"xposed{c2}")
                        L.need(ACTE, "a_lo", lag=1)
                        for c in range(2):
                            m = 2 * c2 + c
                            L.did(ACTE, ACTE.activation(aT[:, m, :], banks[c2][:, c * T:(c + 1) * T], ACT.Identity,
                                                        scale=ln_w[:, m:m + 1], bias=ln_b[:, m:m + 1]), f"ev{c2}")
                        yield
                    L.need(ACTE, "ev1")
                    L.need(ACTE, f"fc{NU - 1}", lag=2, of="F1")
                    split(L, aT[:, :, :], aTp[par], "a")
                    yield

                def back(L):
                    par = L.par

                    def up(n):
                        bk = banks[2 + n % 4]
                        L.need(PE, "a_lo", of="F0")
                        L.ring(PE, "g", n, 4, NU)
                        for c in range(2):
                            m = 2 * n + c
                            w, q = ws[m // 4], m % 4
                            ins = product(bk[:, c * T:(c + 1) * T], [(parts(w, slice(None), k, slice(q * P, (q + 1) * P)),
                                                                      parts(aTp[par], slice(None), k, slice(None))) for k in range(KC)])
                        L.did(PE, ins, f"fc{n}")
                        L.need(ACTE, f"fc{n}")
                        L.ring(ACTE, "lo", n, 2, NU)
                        for c in range(2):
                            m = 2 * n + c
                            L.did(ACTE, ACTE.activation(hf[n % 2][:, c, :], bk[:, c * T:(c + 1) * T], ACT.Gelu_apprx_tanh,
                                                        bias=fcb[:, m:m + 1]), f"g{n}")
                        L.need(ACTE, f"g{n}")
                        L.ring(ACTE, "pj", n, NH, NU)
                        L.did(ACTE, ACTE.activation(hp[n % NH][0][:, :, :], hf[n % 2][:, :, :], ACT.Copy), f"hi{n}")
                        L.need(DVE, f"hi{n}")
                        L.did(DVE, DVE.tensor_tensor(hp[n % NH][1][:, :, :], hf[n % 2][:, :, :],
                                                     hp[n % NH][0][:, :, :].bitcast(F32), ALU.subtract), f"lo{n}")

                    def down(n):
                        L.need(PE, f"lo{n}")
                        if n == 0:
                            L.need(PE, "out1", lag=1)
                        for t in range(NT):
                            w = ws[4 + n // 2]
                            ins = product(banks[6 + t][:, :],
                                          [(parts(hp[n % NH], slice(None), c, slice(t * P, (t + 1) * P)),
                                            parts(w, slice(None), (2 * n + c) % 4, slice(None))) for c in range(2)],
                                          first=n == 0, last=n == NU - 1)
                        L.did(PE, ins, f"pj{n}")

                    for n in range(NU + 2):
                        if n < NU:
                            up(n)
                        if n >= 2:
                            down(n - 2)
                        yield
                    for t in range(NT):
                        L.need(DVE, f"pj{NU - 1}")
                        L.need(DVE, "x_pb", of="F0")
                        L.need(DVE, "st", lag=1)
                        L.did(DVE, DVE.tensor_tensor(y[:, t, :], banks[6 + t][:, :], x[par][:, t, :], ALU.add), f"out{t}")
                    L.need(POOL, "out1")
                    L.moved(POOL.dma_start(tokens(x_out, L.b), y[:, :, :]), "st")
                    yield

                pipeline(nc, steps, ["F0", "F1"], [front, back])
                finish("F", ["F1"])

        at = [d["x"], d["x1"], d["x2"], d["x3"], d["x4"]]
        flow = {"A": lambda i, o: attention("A", i, o, True), "B": wide_attention,
                "CD": lambda i, o: (time_mix(i, d["zT"]), channel_mix(i, d["zT"], o)),
                "E": lambda i, o: attention("E", i, o, False), "F": mlp}
        todo = [k for k in flow if k in PHASES]
        for n, k in enumerate(todo):
            flow[k](at[n], d["out"] if n == len(todo) - 1 else at[n + 1])
    return steps.found


PHASES = ["A", "B", "CD", "E", "F"]
POOL_UNITS = (1, 3)


_NAMES = ["L0_xattn_ln_gamma", "L0_xattn_ln_beta", "L0_xattn_gate", "L1_xattn_w_q", "L1_xattn_w_k", "L1_xattn_w_v",
          "L1_xattn_alpha", "L3_xattn_ln1_w", "L3_xattn_ln1_b", "L3_xattn_q_w", "L3_xattn_q_b", "L3_xattn_k_w",
          "L3_xattn_k_b", "L3_xattn_v_w", "L3_xattn_v_b", "L3_xattn_cproj_w", "L3_xattn_cproj_b",
          "L3_xattn_ln2_w", "L3_xattn_ln2_b", "L3_xattn_fc_w", "L3_xattn_fc_b", "L3_xattn_proj_w", "L3_xattn_proj_b"] \
    + ["L2_xattn_" + n for n in ("ln1_w", "ln1_b", "ln2_w", "ln2_b", "maa_x", "maa_w1", "maa_w2", "maa_stack",
                                 "time_decay", "td_w1", "td_w2", "u", "gn_w", "gn_b", "ffn_maa_k", "ffn_maa_r")]


def layout(i):
    a = {n: np.asarray(i[n]) for n in _NAMES}
    x, c = np.asarray(i["x"]).reshape(B * T, D), np.asarray(i["ctx_2048"]).reshape(B * T, D)
    a.update(x=x, xT=x.T, ctx=c, ctxT=c.T, mask=np.asarray(i["mask_BxS2_bf1"]).view(np.uint8),
             L1_WoT=np.asarray(i["L1_xattn_w_o"]).T)
    for w in ("Wq", "Wk", "Wv", "Wo"):
        a[f"L0_{w}T"] = np.asarray(i[f"L0_xattn_{w}"]).T
    for w in ("Wr", "Wk", "Wv", "Wg", "Wo", "Wfk", "Wfr", "Wfv"):
        a[f"L2_{w}T"] = np.asarray(i[f"L2_xattn_{w}"]).T
    a["L1_xattn_alpha"] = a["L1_xattn_alpha"].reshape(1)
    a["L2_xattn_maa_w2"] = a["L2_xattn_maa_w2"].reshape(NMIX * DM, D)
    a["L2_xattn_maa_stack"] = a["L2_xattn_maa_stack"].reshape(NMIX * D)
    a["L2_xattn_u"] = a["L2_xattn_u"].reshape(D)
    return {n: np.ascontiguousarray(v) for n, v in a.items()}


def build(nc, arrays, seen):
    d = {n: nc.dram_tensor(f"in_{n}", v.shape, mybir.dt.from_np(v.dtype), kind="ExternalInput").ap()
         for n, v in arrays.items()}
    d["out"] = nc.dram_tensor("out_0", (B * T, D), F32, kind="ExternalOutput").ap()
    for n in ("x1", "x2", "x3", "x4"):
        d[n] = nc.dram_tensor(f"act_{n}", (B * T, D), F32, kind="Internal").ap()
    d["zT"] = nc.dram_tensor("act_zT", (B * D, T), F32, kind="Internal").ap()
    d["vT"] = nc.dram_tensor("act_vT", (B * D, T), F32, kind="Internal").ap()
    return program(nc, d, seen)


def kernel(**inputs):
    import concourse.bacc as _bacc
    from concourse.bass_utils import run_bass_kernel_spmd as _run

    arrays = layout(inputs)
    seen = build(_bacc.Bacc("TRN2", target_bir_lowering=False, num_devices=1), arrays, {})
    nc = _bacc.Bacc("TRN2", target_bir_lowering=False, num_devices=1)
    build(nc, arrays, seen)
    r = _run(nc, [{f"in_{n}": v for n, v in arrays.items()}], core_ids=[0])
    return r.results[0]["out_0"].reshape(B, T, D)
```

```python
from contextlib import ExitStack

import numpy as np
import concourse.bass as bass
from concourse import mybir

F32 = mybir.dt.float32
F32R = mybir.dt.float32r
U8 = mybir.dt.uint8
ALU = mybir.AluOpType
ACT = mybir.ActivationFunctionType
AX = mybir.AxisListType

P = 128
B = 16
T = 256
NT = T // P
D = 512
KC = D // P
H = 16
HD = D // H
RH = 32
RS = D // RH
GH = P // RS
DM = 32
NMIX = 5
DD = 64
INNER = 4 * D
NI = INNER // P
EPS = 1e-5
FMAX = 3.4028235e38
JH = 4
POOL_UNITS = (1, 3)

SKEW = 2
AVS = 1
NPT = 3
PT_ACT = 2
STACK = 3
PREP = 7
FRONT_PAD = 2
HEAD_PAD = 8
HEAD_TAIL = 4
OUT_PAD = 24


class Batch:

    def __init__(self, u, c):
        self.u, self.c = u, c
        self.par = c % 2

    def times(self, n, plus=0):
        return self.u * (2 * n) + (self.c * n + plus)

    def half(self, n, plus=0):
        return self.u * n + ((self.c // 2) * n + plus)

    def back(self, lag):
        return Batch(self.u, self.c - lag)

    def exists(self):
        return not isinstance(self.u, int) or 0 <= 2 * self.u + self.c


class Steps:

    def __init__(self, nc, ctx, seen):
        self.nc, self.ctx, self.seen, self.found, self.sems, self.waited = nc, ctx, seen, {}, {}, {}
        self.base, self.free = {}, []
        self.names = {id(nc.tensor): "pe", id(nc.vector): "dve", id(nc.scalar): "act",
                      id(nc.gpsimd): "pool", id(nc.sync): "sp"}

    def sem(self, *key):
        if key not in self.sems:
            reuse = self.free and key[0] != "held" and not self.software(key)
            self.sems[key], self.base[key] = (self.free.pop(0) if reuse else
                                              (self.ctx.enter_context(self.nc.semaphore("_".join(map(str, key)))), 0))
        return self.sems[key]

    def software(self, key):
        return key[1] == "dma" and key[2] in ("st", "stackQ", "stackK")

    def release(self):
        for key in [k for k in self.sems if k[0] != "held"]:
            dma = key[1] == "dma"
            per = self.seen.get(key[0:3] if dma else key, 1)
            times = 1 if key[0].endswith("setup") else B // 2 if dma else B
            sem, base = self.sems.pop(key), self.base.pop(key)
            if not self.software(key):
                self.free.append((sem, base + per * times))


class Lane:
    def __init__(self, steps, name, b):
        self.s, self.name, self.b, self.par, self.n = steps, name, b, b.par, {}

    def did(self, eng, ins, *names):
        key = (self.name, self.s.names[id(eng)])
        self.n[key] = self.n.get(key, 0) + 1
        ins.then_inc(self.s.sem(*key), 1)
        for step in names:
            self.s.found[(self.name, step)] = (key, self.n[key])

    def moved(self, ins, step):
        key = (self.name, "dma", step)
        self.n[key] = self.n.get(key, 0) + 16
        ins.then_inc(self.s.sem(*key, self.par), 16)
        self.s.found[(self.name, step)] = (key, None)

    def slot(self, ins, step, slot):
        key = (self.name, slot)
        self.n[key] = self.n.get(key, 0) + 16
        ins.then_inc(self.s.sem(*key), 16)
        self.s.found[(self.name, step)] = (key, self.n[key])

    def end(self):
        for key, n in self.n.items():
            self.s.found[key] = n

    def need(self, eng, *steps, lag=0, of=None):
        lane = of or self.name
        for step in steps:
            b = Batch(0, 0) if lane.endswith("setup") else self.b.back(lag)
            if not b.exists():
                continue
            assert b.c >= 0
            key, count = self.s.seen.get((lane, step), ((lane, "pe"), 1))
            per = self.s.seen.get(key, 1)
            full = key if count is not None else (*key, b.par)
            sem = self.s.sem(*full)
            base = self.s.base[full]
            if count is None:
                value, const = b.half(per, base + per), base + (b.c // 2) * per + per
            else:
                value, const = b.times(per, base + count), base + b.c * per + count
            known = (id(eng), sem.name if hasattr(sem, "name") else id(sem))
            if self.s.waited.get(known, -10 ** 9) >= const:
                continue
            self.s.waited[known] = const
            eng.wait_ge(sem, value)
            if eng in (self.s.nc.sync, self.s.nc.gpsimd):
                self.hold(eng)

    def hold(self, eng):
        eng.sem_inc(self.s.sem("held", self.s.names[id(eng)]), 1)

    def ring(self, eng, step, n, depth, total):
        if n >= depth:
            self.need(eng, f"{step}{n - depth}")
        else:
            self.need(eng, f"{step}{n - depth + total}", lag=1)


def pipeline(nc, steps, lanes, stages):
    K = len(stages)
    peel = K + (B - K) % 2

    def turn(u, c):
        steps.waited = {}
        work = []
        for k, stage in enumerate(stages):
            b = Batch(u, c - k)
            if isinstance(u, int) and not 0 <= c - k < B:
                continue
            lane = Lane(steps, lanes[k], b)
            work.append([stage(lane), lane, 0, max(steps.seen.get((lanes[k], "yields"), 1), 1)])
        while work:
            w = min(work, key=lambda w: w[2] / w[3])
            try:
                next(w[0])
                w[2] += 1
            except StopIteration:
                steps.found[(w[1].name, "yields")] = w[2]
                w[1].end()
                work.remove(w)

    for t in range(peel):
        turn(0, t)
    with nc.Fori(0, (B - peel) // 2) as u:
        turn(u, peel)
        turn(u, peel + 1)
    for t in range(B, B + K - 1):
        turn(0, t)


def program(nc, d, seen):
    PE, DVE, ACTE, POOL, SP = nc.tensor, nc.vector, nc.scalar, nc.gpsimd, nc.sync
    top = ExitStack()
    steps = Steps(nc, top, seen)
    with top:
        def tile(ctx, name, shape, dt=F32):
            return ctx.enter_context(nc.sbuf_tensor(name, shape, dt))

        def pair(ctx, name, shape):
            return [tile(ctx, f"{name}_{part}", shape, F32R) for part in ("hi", "lo")]

        def both(ctx, make, name, *a):
            return [make(ctx, f"{name}{i}", *a) for i in range(2)]

        banks = [top.enter_context(nc.psum_tensor(f"bank{i}", [P, 512], F32)) for i in range(8)]
        ident = tile(top, "ident", [P, P])
        headsum = tile(top, "headsum", [P, GH])
        mhalf = tile(top, "mhalf", [P, NT])

        def setup_done(S, *engines):
            S.end()
            for e in engines:
                for step in [k[1] for k in steps.found if k[0] == S.name and isinstance(steps.found[k], tuple)]:
                    S.need(e, step, of=S.name)

        S = Lane(steps, "const_setup", Batch(0, 0))
        S.did(POOL, POOL.memset(ident[:, :], 0.0), "zero")
        S.need(POOL, "zero", of="const_setup")
        S.did(POOL, POOL.affine_select(out=ident[:, :], in_=ident[:, :], compare_op=ALU.not_equal, fill=1.0,
                                       base=0, pattern=[[-1, P]], channel_multiplier=1), "ident")
        S.did(POOL, POOL.memset(mhalf[:, :], -0.5), "mhalf")
        S.did(POOL, POOL.memset(headsum[:, :], 1.0), "ones")
        S.need(POOL, "ones", of="const_setup")
        S.did(POOL, POOL.affine_select(out=headsum[:, :], in_=headsum[:, :], compare_op=ALU.is_ge, fill=0.0,
                                       base=0, pattern=[[-RS, GH]], channel_multiplier=1), "low")
        S.need(POOL, "low", of="const_setup")
        S.did(POOL, POOL.affine_select(out=headsum[:, :], in_=headsum[:, :], compare_op=ALU.is_ge, fill=0.0,
                                       base=RS - 1, pattern=[[RS, GH]], channel_multiplier=-1), "headsum")
        setup_done(S, PE, DVE, POOL)

        def product(out, pairs, first=True, last=True):
            n = len(pairs)
            for i, (lhs, rhs) in enumerate(pairs):
                for j, (x, y) in enumerate(((0, 0), (0, 1), (1, 0))):
                    ins = PE.matmul(out, lhs[x], rhs[y], start=first and i == 0 and j == 0,
                                    stop=last and i == n - 1 and j == 2)
            return ins

        def parts(pr, *idx):
            return [t[idx] for t in pr]

        def load_weights(ctx, S, names, scales={}):
            out = []
            tmp = ExitStack()
            stage = [tmp.enter_context(nc.sbuf_tensor(f"{S.name}_stage{i}", [P, KC * D], F32, side="right"))
                     for i in range(2)]
            for i, (name, src) in enumerate(names):
                rows, cols = src.shape
                c = rows // min(rows, P)
                w = pair(ctx, f"w_{name}", [min(rows, P), c, cols])
                st = stage[i % 2][0:min(rows, P), 0:c * cols].rearrange("p (c n) -> p c n", c=c)
                if i >= 2:
                    S.need(SP, f"lo{i - 2}", of=S.name)
                S.slot(SP.dma_start(st, src.rearrange("(c p) n -> p c n", p=min(rows, P))), f"load{i}", f"stage{i % 2}")
                S.need(ACTE, f"load{i}", of=S.name)
                f = scales.get(name, 1.0)
                S.did(ACTE, ACTE.activation(w[0][:, :, :], st, ACT.Copy, scale=f), f"hi{i}")
                S.need(DVE, f"hi{i}", f"load{i}", of=S.name)
                S.did(DVE, DVE.scalar_tensor_tensor(w[1][:, :, :], st, f, w[0][:, :, :].bitcast(F32), ALU.mult, ALU.subtract), f"lo{i}")
                out.append(w)
            tmp.close()
            return out

        def columns(ctx, S, name):
            src = d[name]
            n = src.shape[0] // P
            t = tile(ctx, f"c_{name}", [P, n])
            with nc.allow_non_contiguous_dma(reason="a vector of features, once"):
                S.moved(SP.dma_start(t[:, :], src.rearrange("(c p) -> p c", p=P)), "vectors")
            return t

        def rows(ctx, S, name):
            n = d[name].shape[0]
            t = tile(ctx, f"r_{name}", [P, n])
            S.moved(SP.dma_start(t[:, :], d[name].rearrange("(a n) -> a n", a=1).broadcast_to([P, n])), "vectors")
            return t

        def norm_steps(L, x, xn, st, src):
            stats, agg, rstd = st
            L.need(DVE, src)
            L.need(DVE, "pow", "norm1", lag=1)
            for t in range(NT):
                L.did(DVE, DVE.bn_stats(stats[:, t, :], x[:, t, :]), f"bn{t}")
                L.need(DVE, f"bn{t}")
                L.hold(DVE)
                L.did(DVE, DVE.bn_aggr(agg[:, t, :], stats[:, t, :]), f"agg{t}")
            L.need(POOL, "agg1")
            L.need(POOL, "norm1", lag=1)
            L.did(POOL, POOL.tensor_scalar(rstd[:, :], agg[:, :, 1], EPS, None, ALU.add), "vareps")
            L.need(POOL, "vareps")
            L.did(POOL, POOL.tensor_tensor(rstd[:, :], rstd[:, :], mhalf[:, 0:NT], ALU.pow), "pow")
            yield
            yield
            L.need(DVE, "pow")
            if xn is not x:
                L.need(DVE, "xposed1", lag=1)
            for t in range(NT):
                L.did(DVE, DVE.tensor_scalar(xn[:, t, :], x[:, t, :], agg[:, t, 0:1], rstd[:, t:t + 1],
                                             ALU.subtract, ALU.mult), f"norm{t}")

        def norm_tiles(ctx, name):
            return (tile(ctx, f"{name}_stats", [P, NT, 6]), tile(ctx, f"{name}_agg", [P, NT, 2]),
                    tile(ctx, f"{name}_rstd", [P, NT]))

        def xpose(L, x, bank, c2, name):
            for c in range(2):
                for t in range(NT):
                    ins = PE.transpose(bank[:, c * T + t * P:c * T + (t + 1) * P],
                                       x[:, t, (2 * c2 + c) * P:(2 * c2 + c + 1) * P], ident[:, :])
            L.did(PE, ins, name)

        def split(L, full, pr, name, free=None):
            if free:
                L.need(ACTE, free, lag=1)
            L.did(ACTE, ACTE.activation(pr[0][:], full, ACT.Copy), f"{name}_hi")
            L.need(POOL, f"{name}_hi")
            L.did(POOL, POOL.tensor_tensor(pr[1][:], full, pr[0][:].bitcast(F32), ALU.subtract), f"{name}_lo")

        def split_half(L, whole, pr, c2, name):
            L.did(ACTE, ACTE.activation(chunk2(pr[0], c2), chunk2(whole, c2), ACT.Copy), f"{name}_hi{c2}")
            L.need(DVE, f"{name}_hi{c2}")
            L.did(DVE, DVE.tensor_tensor(chunk2(pr[1], c2), chunk2(whole, c2), chunk2(pr[0], c2).bitcast(F32), ALU.subtract),
                  f"{name}_lo{c2}", f"{name}_lo")

        def chunk2(t, c2):
            return t[:, 2 * c2:2 * c2 + 2, :]

        def as2(bank, n=T):
            return bank[:, 0:2 * n].rearrange("p (c t) -> p c t", c=2)

        def proj_T(bank, w, xT, c2):
            for c in range(2):
                m = 2 * c2 + c
                ins = product(bank[:, c * T:(c + 1) * T],
                              [(parts(w, slice(None), k, slice(m * P, (m + 1) * P)), parts(xT, slice(None), k, slice(None)))
                               for k in range(KC)])
            return ins

        def proj_N(bank, w, xT, t, k0=0, kn=KC, **kw):
            return product(bank[:, :],
                           [(parts(xT, slice(None), k, slice(t * P, (t + 1) * P)), parts(w, slice(None), k, slice(None)))
                            for k in range(k0, k0 + kn)], **kw)

        def tokens(ap, b):
            return ap[bass.ds(b.times(T), T), :].rearrange("(t p) f -> p t f", p=P)

        def attention(ph, x_in, x_out, first):
            ctx = ExitStack()
            with ctx:
                S = Lane(steps, f"{ph}setup", Batch(0, 0))
                PREPARE, FRONT, HEADS, OUT = [f"{ph}{i}" for i in range(4)]
                scale = float(HD) ** -0.5
                if first:
                    gamma, beta = columns(ctx, S, "L0_xattn_ln_gamma"), columns(ctx, S, "L0_xattn_ln_beta")
                    gate = tile(ctx, "gate", [P, 1])
                    S.moved(SP.dma_start(gate[:, :], d["L0_xattn_gate"].rearrange("(a n) -> a n", a=1).broadcast_to([P, 1])), "vectors")
                    ws = ["L0_WqT", "L0_WkT", "L0_WvT", "L0_WoT"]
                else:
                    gamma, beta = columns(ctx, S, "L3_xattn_ln1_w"), columns(ctx, S, "L3_xattn_ln1_b")
                    qb, kb = columns(ctx, S, "L3_xattn_q_b"), columns(ctx, S, "L3_xattn_k_b")
                    vb, cb = rows(ctx, S, "L3_xattn_v_b"), rows(ctx, S, "L3_xattn_cproj_b")
                    ws = ["L3_xattn_q_w", "L3_xattn_k_w", "L3_xattn_v_w", "L3_xattn_cproj_w"]
                wq, wk, wv, wo = load_weights(ctx, S, [(w, d[w]) for w in ws], {ws[0]: -scale})
                if first:
                    tg = tile(ctx, "tanh_gate", [P, 1])
                    S.need(ACTE, "vectors", of=S.name)
                    S.did(ACTE, ACTE.activation(tg[:, :], gate[:, :], ACT.Tanh), "tanh_gate")
                else:
                    S.need(DVE, "vectors", of=S.name)
                    S.did(DVE, DVE.tensor_scalar(qb[:, :], qb[:, :], -scale, None, ALU.mult), "qb")
                setup_done(S, PE, DVE, ACTE, POOL, SP)

                raw = tile(ctx, f"{ph}_raw", [P, NT, D])
                otherp = pair(ctx, f"{ph}_otherp", [P, KC, T])
                nst = norm_tiles(ctx, ph)
                aTp = pair(ctx, f"{ph}_aTp", [P, KC, T])
                whole = tile(ctx, f"{ph}_whole", [P, KC, T])
                QKp = pair(ctx, f"{ph}_QKp", [P, KC, T])
                Qs = [tile(ctx, f"{ph}_Qs{i}", [3 * HD, H, T], F32R) for i in range(2)]
                Ks = [tile(ctx, f"{ph}_Ks{i}", [3 * HD, H, T], F32R) for i in range(2)]
                V = both(ctx, tile, f"{ph}_V", [P, NT, D])
                m8 = both(ctx, tile, f"{ph}_m8", [P, T], U8)
                mb = both(ctx, tile, f"{ph}_mb", [P, T])
                NS = 4
                sm = [tile(ctx, f"{ph}_s{i}", [P, NT, T]) for i in range(NS)]
                smin = tile(ctx, f"{ph}_smin", [P, NT, H])
                ssum = tile(ctx, f"{ph}_ssum", [P, NT, H])
                rsum = tile(ctx, f"{ph}_rsum", [P, NT, H])
                pT = [tile(ctx, f"{ph}_pT{i}", [P, NT, T]) for i in range(NPT)]
                on = tile(ctx, f"{ph}_on", [P, NT, D])
                oTp = pair(ctx, f"{ph}_attT", [P, KC, T])
                xo = tile(ctx, f"{ph}_xo", [P, NT, D])
                fb, sb, tb, ob, xb = banks[0:2], banks[2:4], banks[4], banks[5:7], banks[7]
                NF = 8

                def prepare(L):
                    b = L.b
                    for _ in range(PREP):
                        yield
                    L.need(SP, "xposed1", lag=1, of=FRONT)
                    L.moved(SP.dma_start(raw[:, :, :], tokens(d["ctx"] if first else x_in, b)), "ld_raw")
                    L.need(SP, "a_lo", lag=1, of=FRONT)
                    L.moved(SP.dma_start(whole[:, :, :], d["xT" if first else "ctxT"][:, bass.ds(b.times(T), T)]
                                         .rearrange("(c p) t -> p c t", p=P)), "ld_other")
                    yield
                    yield
                    yield
                    yield from norm_steps(L, raw, raw, nst, "ld_raw")
                    yield
                    yield

                def front(L):
                    b, par = L.b, L.par
                    L.need(ACTE, "ld_other", of=PREPARE)
                    L.need(ACTE, "mmQ1" if first else "mmV1", lag=1)
                    for c2 in range(2):
                        split_half(L, whole, otherp, c2, "o")
                    L.need(SP, "mask1", lag=2)
                    L.moved(SP.dma_start(m8[par][:, :], d["mask"][bass.ds(b.times(1), 1), :].broadcast_to([P, T])), "ld_mask")
                    for _ in range(FRONT_PAD):
                        yield
                    L.need(DVE, "ld_mask")
                    L.need(DVE, f"min{H - 1}_1", lag=2, of=HEADS)
                    big = 3e38 if first else FMAX
                    L.did(DVE, DVE.tensor_scalar(mb[par][:, :], m8[par][:, :], 1.0, -big, ALU.subtract, ALU.mult), "mask0")
                    L.need(DVE, "mask0")
                    L.did(DVE, DVE.tensor_scalar(mb[par][:, :], mb[par][:, :], 10.0 if first else 1.0, None, ALU.mult), "mask1")
                    use, later = [0], []

                    def bank():
                        n = use[0]
                        use[0] += 1
                        L.ring(PE, "ev", n, 2, NF)
                        return n, fb[n % 2]

                    def transposed():
                        for c2 in range(2):
                            n, bk = bank()
                            L.need(PE, "norm1", of=PREPARE)
                            xpose(L, raw, bk, c2, f"xposed{c2}")
                            yield
                            L.need(ACTE, f"xposed{c2}")
                            L.need(ACTE, "o_lo")
                            for c in range(2):
                                k = 2 * c2 + c
                                L.did(ACTE, ACTE.activation(whole[:, k, :], bk[:, c * T:(c + 1) * T], ACT.Identity,
                                                            scale=gamma[:, k:k + 1], bias=beta[:, k:k + 1]), f"ev{n}")
                            L.need(ACTE, f"ev{n}")
                            L.need(ACTE, "mmV1" if first else "mmQ1", lag=1)
                            split_half(L, whole, aTp, c2, "a")
                            yield

                    def features(name, w, src, xT, dst, stacked, bias):
                        for c2 in range(2):
                            n, bk = bank()
                            L.need(PE, f"{src}_lo")
                            for c in range(2):
                                m = 2 * c2 + c
                                ins = product(bk[:, c * T:(c + 1) * T],
                                              [(parts(w, slice(None), k, slice(m * P, (m + 1) * P)), parts(xT, slice(None), k, slice(None)))
                                               for k in range(KC)])
                                if c == 0:
                                    yield
                            L.did(PE, ins, f"mm{name}{c2}")
                            L.need(ACTE, f"mm{name}{c2}")
                            if name == ("Q" if first else "K"):
                                L.need(ACTE, "stackK" if first else "stackQ", lag=1)
                            else:
                                L.need(ACTE, "stackQ" if first else "stackK")
                            if bias is None:
                                L.did(ACTE, ACTE.activation(chunk2(dst[0], c2), as2(bk), ACT.Copy), f"hi{name}{c2}")
                                L.need(DVE, f"hi{name}{c2}")
                                L.did(DVE, DVE.tensor_tensor(chunk2(dst[1], c2), as2(bk), chunk2(dst[0], c2).bitcast(F32), ALU.subtract),
                                      f"ev{n}", f"lo{name}")
                            else:
                                for c in range(2):
                                    m = 2 * c2 + c
                                    L.did(ACTE, ACTE.activation(dst[0][:, m, :], bk[:, c * T:(c + 1) * T], ACT.Identity,
                                                                bias=bias[:, m:m + 1]), f"hi{name}{c2}")
                                L.need(DVE, f"hi{name}{c2}")
                                for c in range(2):
                                    m = 2 * c2 + c
                                    L.did(DVE, DVE.scalar_tensor_tensor(dst[1][:, m, :], bk[:, c * T:(c + 1) * T], bias[:, m:m + 1],
                                                                        dst[0][:, m, :].bitcast(F32), ALU.add, ALU.subtract),
                                          f"ev{n}", f"lo{name}")
                            yield
                        for i, part in enumerate(stacked):
                            for r in range(P // HD):
                                later.append((name, i, part, r))

                    def stack(name, i, part, r):
                        L.need(POOL, f"lo{name}")
                        L.need(POOL, f"qk{H - 1}", lag=2, of=HEADS)
                        to = (Qs if name == "Q" else Ks)[par]
                        L.moved(POOL.dma_start(to[HD * i:HD * (i + 1), :, :].rearrange("p (c r) t -> p c r t", c=KC)[:, :, r, :],
                                               QKp[part][HD * r:HD * (r + 1), :, :]), f"stack{name}")

                    def values(src, xT):
                        for t in range(NT):
                            n, bk = bank()
                            L.need(PE, f"{src}_lo")
                            for half in range(2):
                                ins = proj_N(bk, wv, xT, t, 2 * half, 2, first=half == 0, last=half == 1)
                                if half == 0:
                                    yield
                            L.did(PE, ins, f"mmV{t}")
                            L.need(DVE, f"mmV{t}")
                            L.need(DVE, f"av{H - 1}", lag=2, of=HEADS)
                            if first:
                                L.did(DVE, DVE.tensor_copy(V[par][:, t, :], bk[:, :]), f"ev{n}", "V")
                            else:
                                L.did(DVE, DVE.tensor_tensor(V[par][:, t, :], bk[:, :], vb[:, :], ALU.add), f"ev{n}", "V")
                            yield

                    Q = lambda *a: features("Q", wq, *a, QKp, (0, 0, 1), None if first else qb)
                    K = lambda *a: features("K", wk, *a, QKp, (0, 1, 0), None if first else kb)
                    def products():
                        yield from Q("o", otherp) if first else K("o", otherp)
                        yield from transposed()
                        yield
                        yield from K("a", aTp) if first else Q("a", aTp)
                        yield from values(*(("a", aTp) if first else ("o", otherp)))

                    work = products()
                    while True:
                        more = next(work, "end") != "end"
                        for _ in range(STACK):
                            if later:
                                stack(*later.pop(0))
                        if not more and not later:
                            break
                        yield

                def heads(L):
                    q, k, v = Qs[L.par], Ks[L.par], V[L.par]

                    def scores(h):
                        L.need(PE, "stackQ", "stackK", of=FRONT)
                        L.ring(PE, "smin", h, 2, H)
                        for t in range(NT):
                            ins = PE.matmul(sb[h % 2][:, t * T:(t + 1) * T], q[:, h, t * P:(t + 1) * P], k[:, h, :],
                                            start=True, stop=True)
                        L.did(PE, ins, f"qk{h}")

                    def softmax(h):
                        L.need(DVE, f"qk{h}")
                        L.need(DVE, "mask1", of=FRONT)
                        L.ring(DVE, "tr", h, NS, H)
                        if h == 0:
                            L.need(DVE, f"exp{H - 1}_1", lag=1)
                        L.hold(DVE)
                        for t in range(NT):
                            L.did(DVE, DVE.tensor_tensor_reduce(
                                out=sm[h % NS][:, t, :], in0=sb[h % 2][:, t * T:(t + 1) * T], in1=mb[L.par][:, :], scale=1.0,
                                scalar=FMAX, op0=ALU.add, op1=ALU.min, accum_out=smin[:, t, h:h + 1]), f"min{h}_{t}", f"smin{h}")
                        if h == 0:
                            L.need(ACTE, "rsum", lag=1)
                        for t in range(NT):
                            L.need(ACTE, f"min{h}_{t}")
                            L.did(ACTE, ACTE.activation(sm[h % NS][:, t, :], sm[h % NS][:, t, :], ACT.Exp, scale=-1.0,
                                                        bias=smin[:, t, h:h + 1], accum_out=ssum[:, t, h:h + 1]), f"exp{h}_{t}")

                    def transpose_p(h):
                        L.need(PE, f"exp{h}_1")
                        L.ring(PE, "pT", h, 1, H)
                        for kt in range(NT):
                            for t in range(NT):
                                ins = PE.transpose(tb[:, kt * T + t * P:kt * T + (t + 1) * P],
                                                   sm[h % NS][:, t, kt * P:(kt + 1) * P], ident[:, :])
                        L.did(PE, ins, f"tr{h}")
                        e = ACTE if h % PT_ACT == 1 else DVE
                        L.need(e, f"tr{h}")
                        L.ring(e, "av", h, NPT, H)
                        if e is ACTE:
                            L.did(e, ACTE.activation(pT[h % NPT][:, :, :], as2(tb), ACT.Copy), f"pT{h}")
                        else:
                            L.did(e, DVE.tensor_copy(pT[h % NPT][:, :, :], as2(tb)), f"pT{h}")

                    def values(h):
                        L.need(PE, "V", of=FRONT)
                        L.need(PE, f"pT{h}")
                        if h == 0:
                            L.need(PE, "on1", lag=1)
                        for t in range(NT):
                            for kt in range(NT):
                                ins = PE.matmul(ob[t][:, h * HD:(h + 1) * HD], pT[h % NPT][:, kt, t * P:(t + 1) * P],
                                                v[:, kt, h * HD:(h + 1) * HD], start=kt == 0, stop=kt == NT - 1)
                        L.did(PE, ins, f"av{h}")

                    for _ in range(HEAD_PAD):
                        yield
                    for h in range(H + SKEW + AVS):
                        if 0 <= h - SKEW < H:
                            transpose_p(h - SKEW)
                        if h < H:
                            scores(h)
                            softmax(h)
                        yield
                        if 0 <= h - SKEW - AVS < H:
                            values(h - SKEW - AVS)
                        yield
                    L.need(DVE, f"exp{H - 1}_1")
                    L.need(DVE, "on1", lag=1)
                    L.did(DVE, DVE.reciprocal(rsum[:, :, :], ssum[:, :, :]), "rsum")
                    L.need(DVE, "rsum", f"av{H - 1}")
                    L.need(DVE, "ox1", lag=1, of=OUT)
                    for t in range(NT):
                        L.did(DVE, DVE.tensor_tensor(on[:, t, :].rearrange("p (h e) -> p h e", h=H),
                                                     ob[t][:, :].rearrange("p (h e) -> p h e", h=H),
                                                     rsum[:, t, :, None].broadcast_to([P, H, HD]), ALU.mult), f"on{t}")
                    for _ in range(HEAD_TAIL):
                        yield

                def out(L):
                    L.need(SP, "st", lag=1)
                    L.moved(SP.dma_start(xo[:, :, :], tokens(x_in, L.b)), "ld_xo")
                    yield
                    yield
                    if not first:
                        L.need(POOL, "ld_xo")
                        L.did(POOL, POOL.tensor_tensor(xo[:, :, :], xo[:, :, :], cb[:, None, :].broadcast_to([P, NT, D]), ALU.add), "x_cb")
                    for c2 in range(2):
                        L.need(PE, "on1", of=HEADS)
                        L.need(PE, "oT_lo0") if c2 else L.need(PE, "out1", lag=1)
                        xpose(L, on, xb, c2, f"ox{c2}")
                        yield
                        L.need(ACTE, f"ox{c2}")
                        L.need(ACTE, "o1", lag=1)
                        L.did(ACTE, ACTE.activation(chunk2(oTp[0], c2), as2(xb), ACT.Copy), f"oT_hi{c2}")
                        L.need(DVE, f"oT_hi{c2}")
                        L.did(DVE, DVE.tensor_tensor(chunk2(oTp[1], c2), as2(xb), chunk2(oTp[0], c2).bitcast(F32),
                                                     ALU.subtract), f"oT_lo{c2}")
                        yield
                        yield
                    for t in range(NT):
                        L.need(PE, "out0" if t else "oT_lo1")
                        for half in range(2):
                            ins = proj_N(xb, wo, oTp, t, 2 * half, 2, first=half == 0, last=half == 1)
                            if half == 0:
                                yield
                        L.did(PE, ins, f"o{t}")
                        L.need(DVE, f"o{t}")
                        if first:
                            L.need(DVE, "ld_xo")
                            L.did(DVE, DVE.scalar_tensor_tensor(xo[:, t, :], xb[:, :], tg[:, 0:1], xo[:, t, :],
                                                                ALU.mult, ALU.add), f"out{t}")
                        else:
                            L.need(DVE, "x_cb")
                            L.did(DVE, DVE.tensor_tensor(xo[:, t, :], xb[:, :], xo[:, t, :], ALU.add), f"out{t}")
                        yield
                        yield
                    L.need(POOL, "out1")
                    L.moved(POOL.dma_start(tokens(x_out, L.b), xo[:, :, :]), "st")
                    for _ in range(OUT_PAD):
                        yield

                pipeline(nc, steps, [PREPARE, FRONT, HEADS, OUT], [prepare, front, heads, out])
                finish(ph, [OUT])

        def finish(ph, lanes):
            for name in lanes:
                for b in (B - 2, B - 1):
                    L = Lane(steps, name, Batch(0, b))
                    steps.waited = {}
                    L.need(SP, "st")
            nc.all_engine_barrier()
            steps.release()

        def wide_attention(x_in, x_out):
            ctx = ExitStack()
            with ctx:
                S = Lane(steps, "Bsetup", Batch(0, 0))
                G = pair(ctx, "G", [P, KC, D])
                U = pair(ctx, "U", [P, KC, D])
                alpha = tile(ctx, "alpha", [P, 1])
                S.moved(SP.dma_start(alpha[:, :], d["L1_xattn_alpha"].rearrange("(a n) -> a n", a=1).broadcast_to([P, 1])), "vectors")
                tmp = ExitStack()
                with tmp:
                    wq, wk, wv, woT = load_weights(tmp, S, [(w, d[w]) for w in ("L1_xattn_w_q", "L1_xattn_w_k", "L1_xattn_w_v", "L1_WoT")])
                    for i, (dst, lhs, rhs, last) in enumerate(((G, wq, wk, "lo1"), (U, wv, woT, "lo3"))):
                        for m in range(KC):
                            n = i * KC + m
                            S.need(PE, last, of=S.name)
                            ins = product(banks[n][:, :], [(parts(lhs, slice(None), k, slice(m * P, (m + 1) * P)),
                                                            parts(rhs, slice(None), k, slice(None))) for k in range(KC)])
                            S.did(PE, ins, f"fold{n}")
                            S.need(ACTE, f"fold{n}", of=S.name)
                            S.did(ACTE, ACTE.activation(dst[0][:, m, :], banks[n][:, :], ACT.Copy), f"fold_hi{n}")
                            S.need(DVE, f"fold_hi{n}", of=S.name)
                            S.did(DVE, DVE.tensor_tensor(dst[1][:, m, :], banks[n][:, :], dst[0][:, m, :].bitcast(F32),
                                                         ALU.subtract), f"fold_lo{n}")
                setup_done(S, PE, DVE, ACTE, POOL, SP)
                scale = float(D) ** -0.5

                x = both(ctx, tile, "B_x", [P, NT, D])
                cT = tile(ctx, "B_cT", [P, KC, T])
                cTp = both(ctx, pair, "B_cTp", [P, KC, T])
                xTp = pair(ctx, "B_xTp", [P, KC, T])
                qTp = both(ctx, pair, "B_qTp", [P, KC, T])
                Vp = both(ctx, pair, "B_Vp", [P, NT, D])
                smax = tile(ctx, "B_smax", [P, NT])
                nmax = tile(ctx, "B_nmax", [P, NT])
                pr = tile(ctx, "B_p", [P, NT, T])
                ssum = tile(ctx, "B_ssum", [P, NT])
                rsum = tile(ctx, "B_rsum", [P, NT])
                pTp = pair(ctx, "B_pTp", [P, NT, T])
                y = tile(ctx, "B_y", [P, NT, D])
                fb = banks[0:4]

                def evac(L, bank, pr_c, n, free):
                    L.need(ACTE, f"mm{n}")
                    for f, lag, of in free:
                        L.need(ACTE, f, lag=lag, of=of)
                    L.did(ACTE, ACTE.activation(pr_c[0], bank, ACT.Copy), f"hi{n}")
                    L.need(DVE, f"hi{n}")
                    L.did(DVE, DVE.tensor_tensor(pr_c[1], bank, pr_c[0].bitcast(F32), ALU.subtract), f"ev{n}")

                def front(L):
                    b = L.b
                    L.need(SP, "out1", lag=2, of="Bb")
                    L.moved(SP.dma_start(x[L.par][:, :, :], x_in[bass.ds(b.times(T), T), :].rearrange("(t p) f -> p t f", p=P)), "ld_x")
                    L.need(SP, "c_lo", lag=1)
                    L.moved(SP.dma_start(cT[:, :, :], d["ctxT"][:, bass.ds(b.times(T), T)].rearrange("(c p) t -> p c t", p=P)), "ld_c")
                    yield
                    L.need(ACTE, "ld_c")
                    L.need(ACTE, "mm5", lag=2)
                    L.need(ACTE, "qk", lag=2, of="Bb")
                    split(L, cT[:, :, :], cTp[L.par], "c")
                    for i in range(2):
                        L.need(PE, "ld_x")
                        L.ring(PE, "ev", i, 4, 8)
                        xpose(L, x[L.par], fb[i], i, f"mm{i}")
                        evac(L, as2(fb[i]), [chunk2(xTp[j], i) for j in range(2)], i, [("mm3", 1, None)])
                        yield
                    for i in range(2):
                        n = 2 + i
                        L.need(PE, "ev1")
                        L.ring(PE, "ev", n, 4, 8)
                        L.did(PE, proj_T(fb[n], G, xTp, i), f"mm{n}")
                        evac(L, as2(fb[n]), [chunk2(qTp[L.par][j], i) for j in range(2)], n, [("qk", 2, "Bb")])
                        yield
                    for t in range(NT):
                        n = 4 + t
                        L.need(PE, "c_lo")
                        L.ring(PE, "ev", n, 4, 8)
                        L.did(PE, proj_N(fb[t], U, cTp[L.par], t), f"mm{n}")
                        evac(L, fb[t][:, :], [Vp[L.par][j][:, t, :] for j in range(2)], n, [("pv1", 2, "Bb")])
                        yield
                    S.s.found[(L.name, "ev6")] = S.s.found[(L.name, "ev2")]
                    S.s.found[(L.name, "ev7")] = S.s.found[(L.name, "ev3")]

                sb, tb, ob = banks[4], banks[5], banks[6:8]

                def back(L):
                    L.need(PE, "ev3", of="Bf")
                    L.need(PE, "exp1", lag=1)
                    for t in range(NT):
                        ins = product(sb[:, t * T:(t + 1) * T],
                                      [(parts(qTp[L.par], slice(None), k, slice(t * P, (t + 1) * P)),
                                        parts(cTp[L.par], slice(None), k, slice(None))) for k in range(KC)])
                    L.did(PE, ins, "qk")
                    L.need(DVE, "qk")
                    L.did(DVE, DVE.reduce_max(smax[:, :], as2(sb), AX.X), "max")
                    L.need(DVE, "max")
                    L.need(DVE, "exp1", lag=1)
                    L.did(DVE, DVE.tensor_scalar(nmax[:, :], smax[:, :], -scale, None, ALU.mult), "nmax")
                    L.need(ACTE, "nmax")
                    L.need(ACTE, "pt", "rsum", lag=1)
                    for t in range(NT):
                        L.did(ACTE, ACTE.activation(pr[:, t, :], sb[:, t * T:(t + 1) * T], ACT.Exp, scale=scale,
                                                    bias=nmax[:, t:t + 1], accum_out=ssum[:, t:t + 1]), f"exp{t}")
                    L.need(DVE, "exp1")
                    L.need(DVE, "out1", lag=1)
                    L.did(DVE, DVE.reciprocal(rsum[:, :], ssum[:, :]), "recip")
                    L.need(DVE, "recip")
                    L.did(DVE, DVE.tensor_scalar(rsum[:, :], rsum[:, :], alpha[:, 0:1], None, ALU.mult), "rsum")
                    yield
                    yield
                    L.need(PE, "exp1")
                    L.need(PE, "pT_lo", lag=1)
                    for kt in range(NT):
                        for t in range(NT):
                            ins = PE.transpose(tb[:, kt * T + t * P:kt * T + (t + 1) * P], pr[:, t, kt * P:(kt + 1) * P], ident[:, :])
                    L.did(PE, ins, "pt")
                    L.need(ACTE, "pt")
                    L.need(ACTE, "pv1", lag=1)
                    L.did(ACTE, ACTE.activation(pTp[0][:, :, :], as2(tb), ACT.Copy), "pT_hi")
                    L.need(DVE, "pT_hi")
                    L.did(DVE, DVE.tensor_tensor(pTp[1][:, :, :], as2(tb), pTp[0][:, :, :].bitcast(F32), ALU.subtract), "pT_lo")
                    yield
                    yield
                    for t in range(NT):
                        L.need(PE, "pT_lo")
                        L.need(PE, "ev5", of="Bf")
                        L.need(PE, f"out{t}", lag=1)
                        ins = product(ob[t][:, :], [(parts(pTp, slice(None), kt, slice(t * P, (t + 1) * P)),
                                                     parts(Vp[L.par], slice(None), kt, slice(None))) for kt in range(NT)])
                        L.did(PE, ins, f"pv{t}")
                        L.need(DVE, f"pv{t}", "rsum")
                        L.need(DVE, "st", lag=1)
                        L.did(DVE, DVE.scalar_tensor_tensor(y[:, t, :], ob[t][:, :], rsum[:, t:t + 1], x[L.par][:, t, :],
                                                            ALU.mult, ALU.add), f"out{t}")
                    L.need(POOL, "out1")
                    L.moved(POOL.dma_start(x_out[bass.ds(L.b.times(T), T), :].rearrange("(t p) f -> p t f", p=P), y[:, :, :]), "st")
                    yield

                pipeline(nc, steps, ["Bf", "Bb"], [front, back])
                finish("B", ["Bb"])

        def mix_T(L, out, xT, sx, coef, name):
            for k in range(KC):
                L.did(DVE, DVE.scalar_tensor_tensor(out[:, k, :], sx[:, k, :], coef[:, k:k + 1], xT[:, k, 1:T + 1],
                                                    ALU.mult, ALU.add), name)

        def load_column0(L, xT, row, step):
            with nc.allow_non_contiguous_dma(reason="one token's features, one per partition"):
                L.moved(SP.dma_start(xT[:, :, 0:1], d["ctxT"][:, bass.ds(L.b.times(T, row), 1)]
                                     .rearrange("(c p) t -> p c t", p=P)), step)

        def time_mix(x_in, z_out):
            ctx = ExitStack()
            with ctx:
                S = Lane(steps, "Csetup", Batch(0, 0))
                ln_w, ln_b, maa_x, stack, decay, u, gn_w, gn_b = [
                    columns(ctx, S, "L2_xattn_" + n) for n in
                    ("ln1_w", "ln1_b", "maa_x", "maa_stack", "time_decay", "u", "gn_w", "gn_b")]

                def plain(name, src):
                    rows_, cols = src.shape
                    p = min(rows_, P)
                    t_ = tile(ctx, f"w_{name}", [p, rows_ // p, cols])
                    S.moved(SP.dma_start(t_[:, :, :], src.rearrange("(c p) n -> p c n", p=p)), "weights")
                    return t_

                w1 = plain("maa_w1", d["L2_xattn_maa_w1"])
                w2a = plain("maa_w2a", d["L2_xattn_maa_w2"][0:P, :])
                w2b = plain("maa_w2b", d["L2_xattn_maa_w2"][P:NMIX * DM, :])
                wv, td1, td2 = plain("Wv", d["L2_WvT"]), plain("td_w1", d["L2_xattn_td_w1"]), plain("td_w2", d["L2_xattn_td_w2"])
                wk, wr, wg = plain("Wk", d["L2_WkT"]), plain("Wr", d["L2_WrT"]), plain("Wg", d["L2_WgT"])
                S.need(DVE, "vectors", of=S.name)
                for t_, n in ((gn_w, "half_w"), (gn_b, "half_b")):
                    S.did(DVE, DVE.tensor_scalar(t_[:, :], t_[:, :], 0.5, None, ALU.mult), n)
                setup_done(S, PE, DVE, ACTE, POOL, SP)

                x = both(ctx, tile, "C_x", [P, NT, D])
                nst = norm_tiles(ctx, "C")
                xn = tile(ctx, "C_xn", [P, NT, D])
                xaT = both(ctx, tile, "C_xaT", [P, KC, T + 1])
                sx = tile(ctx, "C_sx", [P, KC, T])
                xi = tile(ctx, "C_xi", [P, KC, T])
                mf = [tile(ctx, f"C_mix{i}", [P, KC, T]) for i in range(3)]
                tx = tile(ctx, "C_tx", [P, 2, T])
                tdt = tile(ctx, "C_tdt", [DD, T])
                th = both(ctx, tile, "C_th", [P, 2, T])
                vT = tile(ctx, "C_vT", [P, KC, T])
                ruk = tile(ctx, "C_ruk", [P, KC, T])
                vtok = both(ctx, tile, "C_vtok", [P, NT, D])
                wT = both(ctx, tile, "C_wT", [P, KC, T])
                kT = both(ctx, tile, "C_kT", [P, KC, T])
                rT = both(ctx, tile, "C_rT", [P, KC, T])
                gT = both(ctx, tile, "C_gT", [P, KC, T])
                ctok = both(ctx, tile, "C_ctok", [P, NT, RH])
                s0 = both(ctx, tile, "C_s0", [P, KC, RS])
                NV, NX = 4, 4
                Vb = [tile(ctx, f"C_V{i}", [P, JH, T]) for i in range(NV)]
                Sx = [tile(ctx, f"C_S{i}", [P, JH, T]) for i in range(NX)]
                og = tile(ctx, "C_og", [P, NT * RH, RS])
                sq = tile(ctx, "C_sq", [P, NT * RH, RS])
                s1 = tile(ctx, "C_s1", [P, NT * RH])
                s2 = tile(ctx, "C_s2", [P, NT * RH])
                zT = tile(ctx, "C_zT", [P, KC, T])
                fb, NF = banks[0:4], 28
                YB, ZB = banks[4:6], banks[6:8]
                QN = RS // JH
                UN = KC * QN
                AHEAD = 2
                FRONT, SCAN, TAIL = "C0", "C1", "C2"

                def plain_T(bank, w, xT, c2):
                    for c in range(2):
                        m = 2 * c2 + c
                        for k in range(KC):
                            ins = PE.matmul(bank[:, c * T:(c + 1) * T], w[:, k, m * P:(m + 1) * P], xT[:, k, :],
                                            start=k == 0, stop=k == KC - 1)
                    return ins

                def front(L):
                    b, par = L.b, L.par
                    n = [0]
                    xa = xaT[par]

                    def bank():
                        k = n[0]
                        n[0] += 1
                        L.ring(PE, "ev", k, 4, NF)
                        return k, fb[k % 4]

                    L.need(SP, "norm1", lag=2)
                    L.moved(SP.dma_start(x[par][:, :, :], tokens(x_in, b)), "ld_x")
                    L.need(SP, "add4", lag=2)
                    load_column0(L, xa, 1, "ld_prev")
                    L.need(SP, f"scan{UN - 1}", f"s0_{UN - 1}", lag=2, of=SCAN)
                    for g in range(KC):
                        L.moved(SP.dma_start(s0[par][:, g, :], d["ctx"][bass.ds(b.times(T, 2 + 4 * g), 4), :]
                                             .rearrange("r (q j) -> (r q) j", j=RS)), "ld_s0")
                    yield
                    yield from norm_steps(L, x[par], xn, nst, "ld_x")
                    yield
                    kx = []
                    for c2 in range(2):
                        k, bk = bank()
                        kx.append((k, bk))
                        L.need(PE, "norm1")
                        xpose(L, xn, bk, c2, f"xposed{c2}")
                    yield
                    for c2, (k, bk) in enumerate(kx):
                        L.need(ACTE, f"xposed{c2}")
                        L.need(ACTE, "add4", lag=2)
                        for c in range(2):
                            m = 2 * c2 + c
                            L.did(ACTE, ACTE.activation(xa[:, m, 1:T + 1], bk[:, c * T:(c + 1) * T], ACT.Identity,
                                                        scale=ln_w[:, m:m + 1], bias=ln_b[:, m:m + 1]), f"ev{k}", "xa")
                    yield
                    L.need(DVE, "xa", "ld_prev")
                    L.need(DVE, "mixed4", lag=1)
                    L.did(DVE, DVE.tensor_tensor(sx[:, :, :], xa[:, :, 0:T], xa[:, :, 1:T + 1], ALU.subtract), "sx")
                    L.need(DVE, "sx")
                    L.need(DVE, "w1mm", lag=1)
                    mix_T(L, xi, xa, sx, maa_x, "xi")
                    yield
                    k, bk = bank()
                    L.need(PE, "xi")
                    for c, rows_ in ((0, P), (1, DM)):
                        for q in range(KC):
                            ins = PE.matmul(bk[0:rows_, c * T:(c + 1) * T], w1[:, q, c * P:c * P + rows_], xi[:, q, :],
                                            start=q == 0, stop=q == KC - 1)
                    L.did(PE, ins, "w1mm")
                    yield
                    L.need(ACTE, "w1mm")
                    L.need(ACTE, "w2mm4", lag=1)
                    L.did(ACTE, ACTE.activation(tx[:, 0, :], bk[:, 0:T], ACT.Tanh), "tx0")
                    L.did(ACTE, ACTE.activation(tx[0:DM, 1, :], bk[0:DM, T:2 * T], ACT.Tanh), f"ev{k}", "tx")
                    yield

                    order = (2, 1, 0, 3, 4)
                    held = {}

                    def weights(i):
                        f = order[i]
                        w2, r = (w2a if f < 4 else w2b), slice(DM * (f % 4), DM * (f % 4) + DM)
                        held[i] = []
                        for c2 in range(2):
                            k, bk = bank()
                            held[i].append((k, bk))
                            L.need(PE, "tx")
                            for c in range(2):
                                m = 2 * c2 + c
                                ins = PE.matmul(bk[:, c * T:(c + 1) * T], w2[r, 0, m * P:(m + 1) * P], tx[r, f // 4, :],
                                                start=True, stop=True)
                            L.did(PE, ins, f"w2mm{f}_{c2}", f"w2mm{f}")

                    def mixed(i):
                        f = order[i]
                        for c2, (k, bk) in enumerate(held[i]):
                            L.need(DVE, f"w2mm{f}_{c2}")
                            L.need(DVE, f"proj{order[i - 3 if i >= 3 else (3, 4, 2)[i]]}", lag=0 if i >= 3 else 1)
                            for c in range(2):
                                m = 2 * c2 + c
                                L.did(DVE, DVE.scalar_tensor_tensor(mf[i % 3][:, m, :], bk[:, c * T:(c + 1) * T],
                                                                    stack[:, KC * f + m:KC * f + m + 1], sx[:, m, :],
                                                                    ALU.add, ALU.mult), f"ev{k}", f"mixed{f}")

                    def add(i):
                        f = order[i]
                        L.need(POOL, f"mixed{f}")
                        L.did(POOL, POOL.tensor_tensor(mf[i % 3][:, :, :], mf[i % 3][:, :, :], xa[:, :, 1:T + 1], ALU.add), f"add{f}")

                    def project(i, w, c2):
                        f = order[i]
                        k, bk = bank()
                        held.setdefault(f"p{f}", []).append((k, bk))
                        L.need(PE, f"add{f}")
                        L.did(PE, plain_T(bk, w, mf[i % 3], c2), f"proj{f}_{c2}", f"proj{f}")

                    def copy_out(f, dst, name):
                        for c2, (k, bk) in enumerate(held[f"p{f}"]):
                            L.need(ACTE, f"proj{f}_{c2}")
                            L.did(ACTE, ACTE.activation(chunk2(dst, c2), as2(bk), ACT.Copy), f"ev{k}", name)

                    def v_out():
                        L.need(ACTE, "st_v", "vx", lag=1)
                        copy_out(2, vT, "v")
                        L.need(ACTE, "v")
                        L.hold(ACTE)
                        L.moved(ACTE.dma_start(d["vT"][bass.ds(b.times(D), D), :].rearrange("(c p) t -> p c t", p=P),
                                               vT[:, :, :]), "st_v")

                    def v_tokens():
                        held["vt"] = []
                        for t in range(NT):
                            k, bk = bank()
                            held["vt"].append((k, bk))
                            L.need(PE, "v")
                            for c in range(KC):
                                ins = PE.transpose(bk[:, c * P:(c + 1) * P], vT[:, c, t * P:(t + 1) * P], ident[:, :])
                            L.did(PE, ins, f"vx{t}", "vx")

                    def v_tokens_out():
                        for t, (k, bk) in enumerate(held["vt"]):
                            L.need(ACTE, f"vx{t}")
                            L.need(ACTE, "cv", lag=2, of=SCAN)
                            L.did(ACTE, ACTE.activation(vtok[par][:, t, :], bk[:, :], ACT.Copy), f"ev{k}", "vtok")

                    def decay_down():
                        k, bk = bank()
                        held["td1"] = (k, bk)
                        L.need(PE, "add1")
                        for q in range(KC):
                            ins = PE.matmul(bk[0:DD, 0:T], td1[:, q, :], mf[1][:, q, :], start=q == 0, stop=q == KC - 1)
                        L.did(PE, ins, "proj1")

                    def decay_tanh():
                        k, bk = held["td1"]
                        L.need(ACTE, "proj1")
                        L.need(ACTE, "td2mm", lag=1)
                        L.did(ACTE, ACTE.activation(tdt[:, :], bk[0:DD, 0:T], ACT.Tanh), f"ev{k}", "tdt")

                    def decay_up():
                        held["td2"] = []
                        for c2 in range(2):
                            k, bk = bank()
                            held["td2"].append((k, bk))
                            L.need(PE, "tdt")
                            for c in range(2):
                                m = 2 * c2 + c
                                ins = PE.matmul(bk[:, c * T:(c + 1) * T], td2[:, 0, m * P:(m + 1) * P], tdt[:, :], start=True, stop=True)
                            L.did(PE, ins, f"td2mm{c2}", "td2mm")

                    def decay_out():
                        for c2, (k, bk) in enumerate(held["td2"]):
                            L.need(ACTE, f"td2mm{c2}")
                            L.need(ACTE, f"scan{UN - 1}", lag=2, of=SCAN)
                            for c in range(2):
                                m = 2 * c2 + c
                                L.did(ACTE, ACTE.activation(wT[par][:, m, :], bk[:, c * T:(c + 1) * T], ACT.Exp,
                                                            bias=decay[:, m:m + 1]), f"ev{k}", "w_log")
                        L.need(ACTE, "w_log")
                        L.did(ACTE, ACTE.activation(wT[par][:, :, :], wT[par][:, :, :], ACT.Exp, scale=-1.0), "w")

                    def k_out():
                        L.need(ACTE, f"a{UN - 1}", lag=2, of=SCAN)
                        copy_out(0, kT[par], "k")

                    def r_out():
                        L.need(ACTE, f"m{UN - 1}", f"m{UN - 2}", lag=2, of=SCAN)
                        copy_out(3, rT[par], "r")

                    def coefficient():
                        L.need(DVE, "k", "r")
                        L.need(DVE, "cmm", lag=1)
                        for m in range(KC):
                            L.did(DVE, DVE.scalar_tensor_tensor(ruk[:, m, :], rT[par][:, m, :], u[:, m:m + 1], kT[par][:, m, :],
                                                                ALU.mult, ALU.mult), "ruk")

                    def coefficient_sum():
                        k, bk = bank()
                        held["c"] = (k, bk)
                        L.need(PE, "ruk")
                        for t in range(NT):
                            for g in range(KC):
                                ins = PE.matmul(bk[:, t * RH + g * GH:t * RH + (g + 1) * GH], ruk[:, g, t * P:(t + 1) * P],
                                                headsum[:, :], start=True, stop=True)
                        L.did(PE, ins, "cmm")

                    def coefficient_out():
                        k, bk = held["c"]
                        L.need(ACTE, "cmm")
                        L.need(ACTE, "cv", lag=2, of=SCAN)
                        L.did(ACTE, ACTE.activation(ctok[par][:, :, :].rearrange("p t h -> p (t h)"), bk[:, 0:NT * RH], ACT.Copy),
                              f"ev{k}", "c")

                    def gate_tanh():
                        for c2, (k, bk) in enumerate(held["p4"]):
                            L.need(ACTE, f"proj4_{c2}")
                            L.need(ACTE, f"g{c2}", lag=1)
                            L.did(ACTE, ACTE.activation(th[c2][:, :, :], as2(bk), ACT.Tanh, scale=0.5), f"th{c2}")

                    def gate():
                        for c2, (k, bk) in enumerate(held["p4"]):
                            L.need(DVE, f"th{c2}")
                            L.need(DVE, "z", lag=2, of=TAIL)
                            L.did(DVE, DVE.scalar_tensor_tensor(chunk2(gT[par], c2), th[c2][:, :, :], 1.0, as2(bk), ALU.add, ALU.mult),
                                  f"ev{k}", f"g{c2}", "g")

                    plan = [
                        [lambda: weights(0)],
                        [lambda: mixed(0), lambda: weights(1)],
                        [lambda: add(0), lambda: mixed(1)],
                        [lambda: add(1), lambda: project(0, wv, 0)],
                        [lambda: project(0, wv, 1)],
                        [v_out, lambda: weights(2)],
                        [decay_down],
                        [lambda: mixed(2), decay_tanh, v_tokens],
                        [lambda: add(2), v_tokens_out, decay_up],
                        [lambda: weights(3), decay_out],
                        [lambda: mixed(3)],
                        [lambda: add(3), lambda: weights(4), lambda: project(2, wk, 0)],
                        [lambda: mixed(4), lambda: project(2, wk, 1)],
                        [k_out, lambda: add(4), lambda: project(3, wr, 0)],
                        [lambda: project(3, wr, 1)],
                        [r_out, lambda: project(4, wg, 0)],
                        [lambda: project(4, wg, 1)],
                        [coefficient, gate_tanh, coefficient_sum],
                        [gate, coefficient_out],
                    ]
                    for slot in plan:
                        for act in slot:
                            act()
                        yield
                    assert n[0] == NF - 1
                    L.s.found[(L.name, f"ev{NF - 1}")] = L.s.found[(L.name, f"ev{NF - 5}")]

                def scan(L):
                    b, par = L.b, L.par
                    w, k, r, s = wT[par], kT[par], rT[par], s0[par]

                    def load(n):
                        g, q = n // QN, n % QN
                        L.need(SP, "st_v", of=FRONT)
                        L.ring(SP, "red", n, NV, UN)
                        src = d["vT"][bass.ds(b.times(D, g * P), P), :].rearrange("(h j) t -> h j t", j=RS)[:, q * JH:(q + 1) * JH, :]
                        L.slot(SP.dma_start(Vb[n % NV][:, :, :].rearrange("p j t -> p (j t)"),
                                            src.rearrange("h j t -> h (j t)")[:, None, :].broadcast_to([GH, RS, JH * T])),
                               f"ld_v{n}", f"v_slot{n % NV}")

                    def reduce(n):
                        g, q = n // QN, n % QN
                        L.need(PE, f"m{n}")
                        if n == 0:
                            L.need(PE, "og1", lag=1, of=TAIL)
                        for t in range(NT):
                            for j in range(JH):
                                out = YB[t][:, g * P:(g + 1) * P].rearrange("p (h j) -> p h j", j=RS)[:, :, q * JH + j]
                                ins = PE.matmul(out, Vb[n % NV][:, j, t * P:(t + 1) * P], headsum[:, :], start=True, stop=True)
                        L.did(PE, ins, f"red{n}")

                    def product_kv(n):
                        g, q = n // QN, n % QN
                        v, sc = Vb[n % NV], Sx[n % NX]
                        L.need(DVE, f"ld_v{n}")
                        L.need(DVE, "w", "k", of=FRONT)
                        L.did(DVE, DVE.tensor_tensor(v[:, :, :], v[:, :, :], k[:, g:g + 1, :].broadcast_to([P, JH, T]), ALU.mult), f"a{n}")
                        L.need(ACTE, "ld_s0", of=FRONT)
                        L.ring(ACTE, "m", n, NX, UN)
                        L.did(ACTE, ACTE.activation(sc[:, :, 0:1], s[:, g, q * JH:(q + 1) * JH, None], ACT.Copy), f"s0_{n}")

                    for n in range(AHEAD):
                        load(n)
                    product_kv(0)
                    for n in range(UN):
                        if n + AHEAD < UN:
                            load(n + AHEAD)
                        g, q = n // QN, n % QN
                        v, sc = Vb[n % NV], Sx[n % NX]
                        if n + 1 < UN:
                            product_kv(n + 1)
                        L.need(DVE, "ld_s0", of=FRONT)
                        L.need(DVE, f"a{n}")
                        L.ring(DVE, "m", n, NX, UN)
                        for j in range(JH):
                            L.did(DVE, DVE.tensor_tensor_scan(sc[:, j, 1:T], w[:, g, 0:T - 1], v[:, j, 0:T - 1],
                                                              s[:, g, q * JH + j:q * JH + j + 1], ALU.mult, ALU.add), f"scan{n}")
                        e = POOL if q in POOL_UNITS else DVE
                        L.need(e, f"scan{n}", f"s0_{n}")
                        L.need(e, "r", of=FRONT)
                        L.did(e, e.tensor_tensor(v[:, :, :], sc[:, :, :], r[:, g:g + 1, :].broadcast_to([P, JH, T]), ALU.mult), f"m{n}")
                        if n >= 1:
                            reduce(n - 1)
                        yield
                    L.need(POOL, "c", "vtok", of=FRONT)
                    L.need(POOL, "zx1", lag=1, of=TAIL)
                    L.did(POOL, POOL.tensor_tensor(og[:, :, :], vtok[par][:, :, :].rearrange("p t (h j) -> p (t h) j", j=RS),
                                                   ctok[par][:, :, :].rearrange("p t h -> p (t h)")[:, :, None]
                                                   .broadcast_to([P, NT * RH, RS]), ALU.mult), "cv")
                    reduce(UN - 1)

                def tail(L):
                    b, par = L.b, L.par
                    L.need(DVE, "cv", f"red{UN - 1}", of=SCAN)
                    for t in range(NT):
                        o = og[:, t * RH:(t + 1) * RH, :]
                        L.did(DVE, DVE.tensor_tensor(o, YB[t][:, :].rearrange("p (h j) -> p h j", j=RS), o, ALU.add), f"og{t}")
                    L.need(DVE, "og1")
                    L.need(DVE, "centred", lag=1)
                    L.did(DVE, DVE.reduce_sum(s1[:, :], og[:, :, :], AX.X), "sum")
                    L.need(DVE, "sum")
                    L.did(DVE, DVE.tensor_scalar(s1[:, :], s1[:, :], 1.0 / RS, None, ALU.mult), "mean")
                    yield
                    L.need(POOL, "mean")
                    L.did(POOL, POOL.tensor_tensor(og[:, :, :], og[:, :, :], s1[:, :, None].broadcast_to([P, NT * RH, RS]),
                                                   ALU.subtract), "centred")
                    yield
                    L.need(ACTE, "centred")
                    L.need(ACTE, "sumsq", lag=1)
                    L.did(ACTE, ACTE.activation(sq[:, :, :], og[:, :, :], ACT.Square), "sq")
                    yield
                    L.need(DVE, "sq")
                    L.need(DVE, "normed", lag=1)
                    L.did(DVE, DVE.reduce_sum(s2[:, :], sq[:, :, :], AX.X), "sumsq")
                    L.need(DVE, "sumsq")
                    L.did(DVE, DVE.tensor_scalar(s2[:, :], s2[:, :], 1.0 / RS, EPS, ALU.mult, ALU.add), "var")
                    yield
                    L.need(ACTE, "var")
                    L.did(ACTE, ACTE.activation(s2[:, :], s2[:, :], ACT.Sqrt), "std")
                    yield
                    L.need(DVE, "std")
                    L.did(DVE, DVE.reciprocal(s2[:, :], s2[:, :]), "rstd")
                    yield
                    L.need(POOL, "rstd")
                    L.did(POOL, POOL.tensor_tensor(og[:, :, :], og[:, :, :], s2[:, :, None].broadcast_to([P, NT * RH, RS]),
                                                   ALU.mult), "normed")
                    yield
                    flat = og[:, :, :].rearrange("p (t h) j -> p t (h j)", t=NT)
                    for c2 in range(2):
                        L.need(PE, "normed")
                        L.need(PE, f"zev{c2}", lag=1)
                        xpose(L, flat, ZB[c2], c2, f"zx{c2}")
                    yield
                    for c2 in range(2):
                        L.need(ACTE, f"zx{c2}")
                        L.need(ACTE, "st", lag=1)
                        for c in range(2):
                            m = 2 * c2 + c
                            L.did(ACTE, ACTE.activation(zT[:, m, :], ZB[c2][:, c * T:(c + 1) * T], ACT.Identity,
                                                        scale=gn_w[:, m:m + 1], bias=gn_b[:, m:m + 1]), f"zev{c2}")
                    yield
                    L.need(POOL, "zev1")
                    L.need(POOL, "g", of=FRONT)
                    L.did(POOL, POOL.tensor_tensor(zT[:, :, :], zT[:, :, :], gT[par][:, :, :], ALU.mult), "z")
                    yield
                    L.need(POOL, "z")
                    L.moved(POOL.dma_start(z_out[bass.ds(b.times(D), D), :].rearrange("(c p) t -> p c t", p=P), zT[:, :, :]), "st")
                    for _ in range(4):
                        yield

                pipeline(nc, steps, [FRONT, SCAN, TAIL], [front, scan, tail])
                finish("C", [TAIL])


        def channel_mix(x_in, z_in, x_out):
            ctx = ExitStack()
            with ctx:
                S = Lane(steps, "Dsetup", Batch(0, 0))
                ln_w, ln_b, fk, fr = [columns(ctx, S, "L2_xattn_" + n) for n in ("ln2_w", "ln2_b", "ffn_maa_k", "ffn_maa_r")]
                wo, wfk, wfr, wfv = load_weights(ctx, S, [(n, d[f"L2_{n}T"]) for n in ("Wo", "Wfk", "Wfr", "Wfv")])
                setup_done(S, PE, DVE, ACTE, POOL, SP)
                zT = tile(ctx, "D_zT", [P, KC, T])
                zTp = pair(ctx, "D_zTp", [P, KC, T])
                x = tile(ctx, "D_x", [P, NT, D])
                x1 = both(ctx, tile, "D_x1", [P, NT, D])
                xr = both(ctx, tile, "D_xr", [P, NT, D])
                nst = norm_tiles(ctx, "D")
                xn = tile(ctx, "D_xn", [P, NT, D])
                xcT = both(ctx, tile, "D_xcT", [P, KC, T + 1])
                sx = tile(ctx, "D_sx", [P, KC, T])
                mk, mr = both(ctx, tile, "D_mix", [P, KC, T])
                mkp, mrp = both(ctx, pair, "D_mixp", [P, KC, T])
                kr = tile(ctx, "D_kr", [P, KC, T])
                kkp = both(ctx, pair, "D_kkp", [P, KC, T])
                rt = both(ctx, tile, "D_rt", [P, NT, D])
                y = tile(ctx, "D_y", [P, NT, D])

                def first(L):
                    b, par = L.b, L.par
                    L.need(SP, "z_lo", lag=1)
                    L.moved(SP.dma_start(zT[:, :, :], z_in[bass.ds(b.times(D), D), :].rearrange("(c p) t -> p c t", p=P)), "ld_z")
                    L.need(SP, "x1_1", lag=1)
                    L.moved(SP.dma_start(x[:, :, :], tokens(x_in, b)), "ld_x")
                    L.need(SP, "mr", lag=2, of="D1")
                    load_column0(L, xcT[par], 0, "ld_prev")
                    L.need(ACTE, "ld_z")
                    L.need(ACTE, "o1", lag=1)
                    split(L, zT[:, :, :], zTp, "z")
                    yield
                    for t in range(NT):
                        L.need(PE, "z_lo")
                        L.need(PE, f"x1_{t}", lag=1)
                        L.did(PE, proj_N(banks[t], wo, zTp, t), f"o{t}")
                        L.need(DVE, f"o{t}", "ld_x")
                        L.need(DVE, "xr", lag=2, of="D1")
                        L.did(DVE, DVE.tensor_tensor(x1[par][:, t, :], banks[t][:, :], x[:, t, :], ALU.add), f"x1_{t}")
                        yield
                    yield from norm_steps(L, x1[par], xn, nst, "x1_1")
                    yield
                    for c2 in range(2):
                        L.need(PE, "norm1")
                        L.need(PE, f"xc{c2}", lag=1)
                        xpose(L, xn, banks[2 + c2], c2, f"xposed{c2}")
                        L.need(ACTE, f"xposed{c2}")
                        L.need(ACTE, "mr", lag=2, of="D1")
                        for c in range(2):
                            m = 2 * c2 + c
                            L.did(ACTE, ACTE.activation(xcT[par][:, m, 1:T + 1], banks[2 + c2][:, c * T:(c + 1) * T],
                                                        ACT.Identity, scale=ln_w[:, m:m + 1], bias=ln_b[:, m:m + 1]), f"xc{c2}")
                        yield

                def second(L):
                    par = L.par
                    xc = xcT[par]
                    L.need(POOL, "x1_1", of="D0")
                    L.need(POOL, "out1", lag=2, of="D2")
                    L.did(POOL, POOL.tensor_copy(xr[par][:, :, :], x1[par][:, :, :]), "xr")
                    L.need(DVE, "xc1", "ld_prev", of="D0")
                    L.did(DVE, DVE.tensor_tensor(sx[:, :, :], xc[:, :, 0:T], xc[:, :, 1:T + 1], ALU.subtract), "sx")
                    L.need(DVE, "sx")
                    L.need(DVE, "mk_lo", lag=1)
                    mix_T(L, mk, xc, sx, fk, "mk")
                    L.need(DVE, "mr_lo", lag=1)
                    mix_T(L, mr, xc, sx, fr, "mr")
                    L.need(ACTE, "mk")
                    L.need(ACTE, "k1", lag=1)
                    split(L, mk[:, :, :], mkp, "mk")
                    L.need(ACTE, "mr")
                    L.need(ACTE, "r1", lag=1)
                    split(L, mr[:, :, :], mrp, "mr")
                    yield
                    for c2 in range(2):
                        L.need(PE, "mk_lo")
                        L.need(PE, f"rt{c2}", lag=1)
                        L.did(PE, proj_T(banks[4 + c2], wfk, mkp, c2), f"k{c2}")
                        L.need(ACTE, f"k{c2}")
                        L.need(ACTE, "kk_lo", lag=1)
                        L.did(ACTE, ACTE.activation(chunk2(kr, c2), as2(banks[4 + c2]), ACT.Relu), f"kr{c2}")
                        yield
                    L.need(POOL, "kr1")
                    L.did(POOL, POOL.tensor_tensor(kr[:, :, :], kr[:, :, :], kr[:, :, :], ALU.mult), "kk")
                    L.need(ACTE, "kk")
                    L.need(ACTE, "v1", lag=2, of="D2")
                    split(L, kr[:, :, :], kkp[par], "kk")
                    for t in range(NT):
                        L.need(PE, "mr_lo", f"kr{t}")
                        L.did(PE, proj_N(banks[4 + t], wfr, mrp, t), f"r{t}")
                        L.need(ACTE, f"r{t}")
                        L.need(ACTE, "gated1", lag=2, of="D2")
                        L.did(ACTE, ACTE.activation(rt[par][:, t, :], banks[4 + t][:, :], ACT.Tanh, scale=0.5), f"rt{t}")
                        yield

                def third(L):
                    par = L.par
                    for t in range(NT):
                        L.need(PE, "kk_lo", of="D1")
                        L.need(PE, f"gated{t}", lag=1)
                        L.did(PE, proj_N(banks[6 + t], wfv, kkp[par], t), f"v{t}")
                        L.need(DVE, f"v{t}")
                        L.need(DVE, f"rt{t}", "xr", of="D1")
                        L.need(DVE, "st", lag=1)
                        L.did(DVE, DVE.scalar_tensor_tensor(y[:, t, :], rt[par][:, t, :], 1.0, banks[6 + t][:, :],
                                                            ALU.add, ALU.mult), f"gated{t}")
                        L.need(DVE, f"gated{t}")
                        L.did(DVE, DVE.scalar_tensor_tensor(y[:, t, :], y[:, t, :], 0.5, xr[par][:, t, :],
                                                            ALU.mult, ALU.add), f"out{t}")
                        yield
                    L.need(POOL, "out1")
                    L.moved(POOL.dma_start(tokens(x_out, L.b), y[:, :, :]), "st")

                pipeline(nc, steps, ["D0", "D1", "D2"], [first, second, third])
                finish("D", ["D2"])

        def mlp(x_in, x_out):
            ctx = ExitStack()
            with ctx:
                S = Lane(steps, "Fsetup", Batch(0, 0))
                ln_w, ln_b, fcb = [columns(ctx, S, "L3_xattn_" + n) for n in ("ln2_w", "ln2_b", "fc_b")]
                pb = rows(ctx, S, "L3_xattn_proj_b")
                fc, pj = d["L3_xattn_fc_w"], d["L3_xattn_proj_w"]
                ws = load_weights(ctx, S, [(f"fc{i}", fc[:, i * D:(i + 1) * D]) for i in range(4)]
                                  + [(f"pj{i}", pj[i * D:(i + 1) * D, :]) for i in range(4)])
                setup_done(S, PE, DVE, ACTE, POOL, SP)
                x = both(ctx, tile, "F_x", [P, NT, D])
                nst = norm_tiles(ctx, "F")
                xn = tile(ctx, "F_xn", [P, NT, D])
                aT = tile(ctx, "F_aT", [P, KC, T])
                aTp = both(ctx, pair, "F_aTp", [P, KC, T])
                NH = 4
                hf = both(ctx, tile, "F_h", [P, 2, T])
                hp = [pair(ctx, f"F_hp{i}", [P, 2, T]) for i in range(NH)]
                y = tile(ctx, "F_y", [P, NT, D])
                NU = NI // 2

                def front(L):
                    b, par = L.b, L.par
                    L.need(SP, "out1", lag=2, of="F1")
                    L.moved(SP.dma_start(x[par][:, :, :], tokens(x_in, b)), "ld_x")
                    yield from norm_steps(L, x[par], xn, nst, "ld_x")
                    L.need(POOL, "norm1")
                    L.did(POOL, POOL.tensor_tensor(x[par][:, :, :], x[par][:, :, :], pb[:, None, :].broadcast_to([P, NT, D]), ALU.add), "x_pb")
                    yield
                    for c2 in range(2):
                        L.need(PE, "norm1")
                        L.need(PE, f"ev{c2}", lag=1)
                        xpose(L, xn, banks[c2], c2, f"xposed{c2}")
                        L.need(ACTE, f"xposed{c2}")
                        L.need(ACTE, "a_lo", lag=1)
                        for c in range(2):
                            m = 2 * c2 + c
                            L.did(ACTE, ACTE.activation(aT[:, m, :], banks[c2][:, c * T:(c + 1) * T], ACT.Identity,
                                                        scale=ln_w[:, m:m + 1], bias=ln_b[:, m:m + 1]), f"ev{c2}")
                        yield
                    L.need(ACTE, "ev1")
                    L.need(ACTE, f"fc{NU - 1}", lag=2, of="F1")
                    split(L, aT[:, :, :], aTp[par], "a")
                    yield

                def back(L):
                    par = L.par

                    def up(n):
                        bk = banks[2 + n % 4]
                        L.need(PE, "a_lo", of="F0")
                        L.ring(PE, "g", n, 4, NU)
                        for c in range(2):
                            m = 2 * n + c
                            w, q = ws[m // 4], m % 4
                            ins = product(bk[:, c * T:(c + 1) * T], [(parts(w, slice(None), k, slice(q * P, (q + 1) * P)),
                                                                      parts(aTp[par], slice(None), k, slice(None))) for k in range(KC)])
                        L.did(PE, ins, f"fc{n}")
                        L.need(ACTE, f"fc{n}")
                        L.ring(ACTE, "lo", n, 2, NU)
                        for c in range(2):
                            m = 2 * n + c
                            L.did(ACTE, ACTE.activation(hf[n % 2][:, c, :], bk[:, c * T:(c + 1) * T], ACT.Gelu_apprx_tanh,
                                                        bias=fcb[:, m:m + 1]), f"g{n}")
                        L.need(ACTE, f"g{n}")
                        L.ring(ACTE, "pj", n, NH, NU)
                        L.did(ACTE, ACTE.activation(hp[n % NH][0][:, :, :], hf[n % 2][:, :, :], ACT.Copy), f"hi{n}")
                        L.need(DVE, f"hi{n}")
                        L.did(DVE, DVE.tensor_tensor(hp[n % NH][1][:, :, :], hf[n % 2][:, :, :],
                                                     hp[n % NH][0][:, :, :].bitcast(F32), ALU.subtract), f"lo{n}")

                    def down(n):
                        L.need(PE, f"lo{n}")
                        if n == 0:
                            L.need(PE, "out1", lag=1)
                        for t in range(NT):
                            w = ws[4 + n // 2]
                            ins = product(banks[6 + t][:, :],
                                          [(parts(hp[n % NH], slice(None), c, slice(t * P, (t + 1) * P)),
                                            parts(w, slice(None), (2 * n + c) % 4, slice(None))) for c in range(2)],
                                          first=n == 0, last=n == NU - 1)
                        L.did(PE, ins, f"pj{n}")

                    for n in range(NU + 2):
                        if n < NU:
                            up(n)
                        if n >= 2:
                            down(n - 2)
                        yield
                    for t in range(NT):
                        L.need(DVE, f"pj{NU - 1}")
                        L.need(DVE, "x_pb", of="F0")
                        L.need(DVE, "st", lag=1)
                        L.did(DVE, DVE.tensor_tensor(y[:, t, :], banks[6 + t][:, :], x[par][:, t, :], ALU.add), f"out{t}")
                    L.need(POOL, "out1")
                    L.moved(POOL.dma_start(tokens(x_out, L.b), y[:, :, :]), "st")
                    yield

                pipeline(nc, steps, ["F0", "F1"], [front, back])
                finish("F", ["F1"])

        at = [d["x"], d["x1"], d["x2"], d["x3"], d["x4"]]
        flow = {"A": lambda i, o: attention("A", i, o, True), "B": wide_attention,
                "CD": lambda i, o: (time_mix(i, d["zT"]), channel_mix(i, d["zT"], o)),
                "E": lambda i, o: attention("E", i, o, False), "F": mlp}
        for n, k in enumerate(flow):
            flow[k](at[n], d["out"] if n == len(flow) - 1 else at[n + 1])
    return steps.found


_NAMES = ["L0_xattn_ln_gamma", "L0_xattn_ln_beta", "L0_xattn_gate", "L1_xattn_w_q", "L1_xattn_w_k", "L1_xattn_w_v",
          "L1_xattn_alpha", "L3_xattn_ln1_w", "L3_xattn_ln1_b", "L3_xattn_q_w", "L3_xattn_q_b", "L3_xattn_k_w",
          "L3_xattn_k_b", "L3_xattn_v_w", "L3_xattn_v_b", "L3_xattn_cproj_w", "L3_xattn_cproj_b",
          "L3_xattn_ln2_w", "L3_xattn_ln2_b", "L3_xattn_fc_w", "L3_xattn_fc_b", "L3_xattn_proj_w", "L3_xattn_proj_b"] \
    + ["L2_xattn_" + n for n in ("ln1_w", "ln1_b", "ln2_w", "ln2_b", "maa_x", "maa_w1", "maa_w2", "maa_stack",
                                 "time_decay", "td_w1", "td_w2", "u", "gn_w", "gn_b", "ffn_maa_k", "ffn_maa_r")]


def layout(i):
    a = {n: np.asarray(i[n]) for n in _NAMES}
    x, c = np.asarray(i["x"]).reshape(B * T, D), np.asarray(i["ctx_2048"]).reshape(B * T, D)
    a.update(x=x, xT=x.T, ctx=c, ctxT=c.T, mask=np.asarray(i["mask_BxS2_bf1"]).view(np.uint8),
             L1_WoT=np.asarray(i["L1_xattn_w_o"]).T)
    for w in ("Wq", "Wk", "Wv", "Wo"):
        a[f"L0_{w}T"] = np.asarray(i[f"L0_xattn_{w}"]).T
    for w in ("Wr", "Wk", "Wv", "Wg", "Wo", "Wfk", "Wfr", "Wfv"):
        a[f"L2_{w}T"] = np.asarray(i[f"L2_xattn_{w}"]).T
    a["L1_xattn_alpha"] = a["L1_xattn_alpha"].reshape(1)
    a["L2_xattn_maa_w2"] = a["L2_xattn_maa_w2"].reshape(NMIX * DM, D)
    a["L2_xattn_maa_stack"] = a["L2_xattn_maa_stack"].reshape(NMIX * D)
    a["L2_xattn_u"] = a["L2_xattn_u"].reshape(D)
    return {n: np.ascontiguousarray(v) for n, v in a.items()}


def build(nc, arrays, seen):
    d = {n: nc.dram_tensor(f"in_{n}", v.shape, mybir.dt.from_np(v.dtype), kind="ExternalInput").ap()
         for n, v in arrays.items()}
    d["out"] = nc.dram_tensor("out_0", (B * T, D), F32, kind="ExternalOutput").ap()
    for n in ("x1", "x2", "x3", "x4"):
        d[n] = nc.dram_tensor(f"act_{n}", (B * T, D), F32, kind="Internal").ap()
    d["zT"] = nc.dram_tensor("act_zT", (B * D, T), F32, kind="Internal").ap()
    d["vT"] = nc.dram_tensor("act_vT", (B * D, T), F32, kind="Internal").ap()
    return program(nc, d, seen)


def kernel(**inputs):
    import concourse.bacc as _bacc
    from concourse.bass_utils import run_bass_kernel_spmd as _run

    arrays = layout(inputs)
    seen = build(_bacc.Bacc("TRN2", target_bir_lowering=False, num_devices=1), arrays, {})
    nc = _bacc.Bacc("TRN2", target_bir_lowering=False, num_devices=1)
    build(nc, arrays, seen)
    r = _run(nc, [{f"in_{n}": v for n, v in arrays.items()}], core_ids=[0])
    return r.results[0]["out_0"].reshape(B, T, D)
```
